# Optimizing a Trainium2 kernel written in Bass

```python
import numpy as np
import jax
import jax.numpy as jnp

def _softmax(x, axis=-1):
    return jax.nn.softmax(x, axis=axis)
def _gelu(x):
    return jax.nn.gelu(x, approximate=True)
def _silu(x):
    return jax.nn.silu(x)
def _sigmoid(x):
    return jax.nn.sigmoid(x)
def _layernorm(x, axis=-1, eps=1e-5):
    m = jnp.mean(x, axis=axis, keepdims=True)
    v = jnp.var(x, axis=axis, keepdims=True)
    return (x - m) / jnp.sqrt(v + eps)
def _scatter_add(tgt, idx, src, axis=0):
    return tgt.at[idx].add(src)
def _segment_sum(src, seg, n):
    return jax.ops.segment_sum(src, seg, n)

kernel_name = 'mk_conv_preact_d2_conv_nchw96_61ad1a'

def setup_inputs(seed: int = 0):
    np.random.seed(seed)
    _w = jnp.asarray
    def _rec_inputs():
        import jax
        import jax.numpy as jnp
        _gk = jax.random.key(seed)
        x = -0.0008768 + 1.001 * jax.random.normal(jax.random.fold_in(_gk, 1), (2, 96, 96, 96), jnp.float32)
        return x
    x = _rec_inputs()
    def _L0_conv_setup():
        import jax, jax.numpy as jnp
        import numpy as np
        C_IN = 96
        D2 = 2 * C_IN
        D4 = 4 * D2
        N = 16
        DR = 6
        B, H, W = (2, 96, 96)

        def _selective_scan(u, delta, A, Bm, Cm, Dv):
            b, L, d4 = u.shape
            n = A.shape[1]

            def step(h, inps):
                u_t, dt, B_t, C_t = inps
                dA = jnp.exp(dt[:, :, None] * A)
                h = dA * h + (dt * u_t)[:, :, None] * B_t[:, None, :]
                y = jnp.einsum('bdn,bn->bd', h, C_t) + Dv * u_t
                return (h, y)
            h0 = jnp.zeros((b, d4, n), u.dtype)
            xs = (jnp.swapaxes(u, 0, 1), jnp.swapaxes(delta, 0, 1), jnp.swapaxes(Bm, 0, 1), jnp.swapaxes(Cm, 0, 1))
            _, ys = jax.lax.scan(step, h0, xs)
            return jnp.swapaxes(ys, 0, 1)
        key = jax.random.key(seed)
        ks = jax.random.split(key, 8)
        g = lambda k, shape, s: jax.random.normal(k, shape, jnp.float32) * s
        return {'x': jax.random.normal(ks[0], (B, C_IN, H, W), jnp.float32), 'W_in': g(ks[1], (C_IN, 2 * D2), 0.05), 'b_in': jnp.zeros((2 * D2,), jnp.float32), 'w_dw': g(ks[2], (D2, 1, 3, 3), 0.1), 'b_dw': jnp.zeros((D2,), jnp.float32), 'A_log': jnp.log(jnp.tile(jnp.arange(1.0, N + 1.0, dtype=jnp.float32), (D4, 1))), 'Dp': jnp.ones((D4,), jnp.float32), 'W_x': g(ks[3], (D4, DR + 2 * N), 0.05), 'W_delta': g(ks[4], (DR, D4), 0.1), 'b_delta': g(ks[5], (D4,), 0.1), 'ln_g': jnp.ones((D2,), jnp.float32), 'ln_b': jnp.zeros((D2,), jnp.float32), 'W_out': g(ks[6], (D2, C_IN), 0.05)}
    _L0_conv_all = _L0_conv_setup()
    _L0_conv_in = {k: v for k, v in _L0_conv_all.items() if k in ('W_in', 'b_in', 'w_dw', 'b_dw', 'A_log', 'Dp', 'W_x', 'W_delta', 'b_delta', 'ln_g', 'ln_b', 'W_out', )}
    del _L0_conv_all

    def _L1_conv_setup():
        import jax, jax.numpy as jnp
        import numpy as np
        IN_CH = 96
        OUT_CH = 96
        LATENT = 256
        BATCH, H, W = (2, 128, 128)

        def _linear(x, w, b):
            return x @ w.T + b

        def _s6(x, xw, xb, bcw, bcb, dw, db, yw, yb):
            u = _linear(x, xw, xb)
            bc = _linear(x, bcw, bcb)
            delta = _linear(x, dw, db)
            Bm, Cm = jnp.split(bc, 2, axis=-1)
            A_bar = jnp.exp(-jax.nn.softplus(delta))
            B_bar = (1.0 - A_bar) * Bm
            elems = (A_bar, B_bar * u)

            def combine(c1, c2):
                a1, b1 = c1
                a2, b2 = c2
                return (a1 * a2, a2 * b1 + b2)
            _, h = jax.lax.associative_scan(combine, elems, axis=1)
            y = Cm * h
            return _linear(y, yw, yb)
        key = jax.random.key(seed)
        ks = jax.random.split(key, 16)
        s = 0.02
        inp = {'x': jax.random.normal(ks[0], (BATCH, IN_CH, H, W), jnp.float32), 'xw': jax.random.normal(ks[1], (LATENT, IN_CH), jnp.float32) * s, 'xb': jnp.zeros((LATENT,), jnp.float32), 'bcw': jax.random.normal(ks[2], (2 * LATENT, IN_CH), jnp.float32) * s, 'bcb': jnp.zeros((2 * LATENT,), jnp.float32), 'dw': jax.random.normal(ks[3], (LATENT, IN_CH), jnp.float32) * s, 'db': jnp.zeros((LATENT,), jnp.float32), 'yw': jax.random.normal(ks[4], (LATENT, LATENT), jnp.float32) * s, 'yb': jnp.zeros((LATENT,), jnp.float32), 'mw': jax.random.normal(ks[5], (LATENT, 4 * LATENT), jnp.float32) * s, 'mb': jnp.zeros((LATENT,), jnp.float32), 'gw': jax.random.normal(ks[6], (LATENT, 4 * LATENT), jnp.float32) * s, 'gb': jnp.zeros((LATENT,), jnp.float32), 'ow': jax.random.normal(ks[7], (OUT_CH, LATENT), jnp.float32) * s, 'ob': jnp.zeros((OUT_CH,), jnp.float32)}
        return inp
    _L1_conv_all = _L1_conv_setup()
    _L1_conv_in = {k: v for k, v in _L1_conv_all.items() if k in ('xw', 'xb', 'bcw', 'bcb', 'dw', 'db', 'yw', 'yb', 'mw', 'mb', 'gw', 'gb', 'ow', 'ob', )}
    del _L1_conv_all

    return {
        "x": x,
        "L0_conv_W_in": _L0_conv_in["W_in"],
        "L0_conv_b_in": _L0_conv_in["b_in"],
        "L0_conv_w_dw": _L0_conv_in["w_dw"],
        "L0_conv_b_dw": _L0_conv_in["b_dw"],
        "L0_conv_A_log": _L0_conv_in["A_log"],
        "L0_conv_Dp": _L0_conv_in["Dp"],
        "L0_conv_W_x": _L0_conv_in["W_x"],
        "L0_conv_W_delta": _L0_conv_in["W_delta"],
        "L0_conv_b_delta": _L0_conv_in["b_delta"],
        "L0_conv_ln_g": _L0_conv_in["ln_g"],
        "L0_conv_ln_b": _L0_conv_in["ln_b"],
        "L0_conv_W_out": _L0_conv_in["W_out"],
        "L1_conv_xw": _L1_conv_in["xw"],
        "L1_conv_xb": _L1_conv_in["xb"],
        "L1_conv_bcw": _L1_conv_in["bcw"],
        "L1_conv_bcb": _L1_conv_in["bcb"],
        "L1_conv_dw": _L1_conv_in["dw"],
        "L1_conv_db": _L1_conv_in["db"],
        "L1_conv_yw": _L1_conv_in["yw"],
        "L1_conv_yb": _L1_conv_in["yb"],
        "L1_conv_mw": _L1_conv_in["mw"],
        "L1_conv_mb": _L1_conv_in["mb"],
        "L1_conv_gw": _L1_conv_in["gw"],
        "L1_conv_gb": _L1_conv_in["gb"],
        "L1_conv_ow": _L1_conv_in["ow"],
        "L1_conv_ob": _L1_conv_in["ob"],
    }

def reference(x, L0_conv_W_in, L0_conv_b_in, L0_conv_w_dw, L0_conv_b_dw, L0_conv_A_log, L0_conv_Dp, L0_conv_W_x, L0_conv_W_delta, L0_conv_b_delta, L0_conv_ln_g, L0_conv_ln_b, L0_conv_W_out, L1_conv_xw, L1_conv_xb, L1_conv_bcw, L1_conv_bcb, L1_conv_dw, L1_conv_db, L1_conv_yw, L1_conv_yb, L1_conv_mw, L1_conv_mb, L1_conv_gw, L1_conv_gb, L1_conv_ow, L1_conv_ob):
    import jax
    import jax.numpy as jnp
    def _L0_conv_ref(x, W_in, b_in, w_dw, b_dw, A_log, Dp, W_x, W_delta, b_delta, ln_g, ln_b, W_out):
        import jax, jax.numpy as jnp
        import numpy as np
        C_IN = 96
        D2 = 2 * C_IN
        D4 = 4 * D2
        N = 16
        DR = 6
        B, H, W = (2, 96, 96)

        def _selective_scan(u, delta, A, Bm, Cm, Dv):
            b, L, d4 = u.shape
            n = A.shape[1]

            def step(h, inps):
                u_t, dt, B_t, C_t = inps
                dA = jnp.exp(dt[:, :, None] * A)
                h = dA * h + (dt * u_t)[:, :, None] * B_t[:, None, :]
                y = jnp.einsum('bdn,bn->bd', h, C_t) + Dv * u_t
                return (h, y)
            h0 = jnp.zeros((b, d4, n), u.dtype)
            xs = (jnp.swapaxes(u, 0, 1), jnp.swapaxes(delta, 0, 1), jnp.swapaxes(Bm, 0, 1), jnp.swapaxes(Cm, 0, 1))
            _, ys = jax.lax.scan(step, h0, xs)
            return jnp.swapaxes(ys, 0, 1)
        b, c, Hh, Ww = x.shape
        d = W_in.shape[1] // 2
        xz = jnp.einsum('bchw,ce->bhwe', x, W_in) + b_in
        xx, z = jnp.split(xz, 2, axis=-1)
        xc = jnp.transpose(xx, (0, 3, 1, 2))
        xc = jax.lax.conv_general_dilated(xc, w_dw, (1, 1), 'SAME', feature_group_count=d, dimension_numbers=('NCHW', 'OIHW', 'NCHW')) + b_dw[None, :, None, None]
        xc = jax.nn.silu(xc)
        L = Hh * Ww
        flat = xc.reshape(b, d, L)
        flipped = xc[:, :, ::-1, ::-1].reshape(b, d, L)
        xl = jnp.swapaxes(jnp.concatenate([flat, flat, flipped, flipped], axis=1), 1, 2)
        A = -jnp.exp(A_log)
        x_dbl = xl @ W_x
        dr, n = (W_delta.shape[0], A.shape[1])
        dt_r = x_dbl[..., :dr]
        Bm = x_dbl[..., dr:dr + n]
        Cm = x_dbl[..., dr + n:]
        delta = jax.nn.softplus(dt_r @ W_delta + b_delta)
        y = _selective_scan(xl, delta, A, Bm, Cm, Dp)
        y = jnp.transpose(y.reshape(b, L, 4, d), (0, 2, 3, 1))
        y1 = y[:, 0].reshape(b, d, Hh, Ww)
        y2 = y[:, 1].reshape(b, d, Hh, Ww)
        y3 = y[:, 2].reshape(b, d, Hh, Ww)[:, :, ::-1, ::-1]
        y4 = y[:, 3].reshape(b, d, Hh, Ww)[:, :, ::-1, ::-1]
        yh = jnp.transpose(y1 + y2 + y3 + y4, (0, 2, 3, 1))
        mu = yh.mean(-1, keepdims=True)
        var = ((yh - mu) ** 2).mean(-1, keepdims=True)
        yn = (yh - mu) * jax.lax.rsqrt(var + 1e-05) * ln_g + ln_b
        out = yn * jax.nn.silu(z) @ W_out
        return jnp.transpose(out, (0, 3, 1, 2))

    def _L1_conv_ref(x, xw, xb, bcw, bcb, dw, db, yw, yb, mw, mb, gw, gb, ow, ob):
        import jax, jax.numpy as jnp
        import numpy as np
        IN_CH = 96
        OUT_CH = 96
        LATENT = 256
        BATCH, H, W = (2, 128, 128)

        def _linear(x, w, b):
            return x @ w.T + b

        def _s6(x, xw, xb, bcw, bcb, dw, db, yw, yb):
            u = _linear(x, xw, xb)
            bc = _linear(x, bcw, bcb)
            delta = _linear(x, dw, db)
            Bm, Cm = jnp.split(bc, 2, axis=-1)
            A_bar = jnp.exp(-jax.nn.softplus(delta))
            B_bar = (1.0 - A_bar) * Bm
            elems = (A_bar, B_bar * u)

            def combine(c1, c2):
                a1, b1 = c1
                a2, b2 = c2
                return (a1 * a2, a2 * b1 + b2)
            _, h = jax.lax.associative_scan(combine, elems, axis=1)
            y = Cm * h
            return _linear(y, yw, yb)
        B, C, Hh, Ww = x.shape
        s1 = x.transpose(0, 2, 3, 1).reshape(B, Hh * Ww, C)
        s2 = x.transpose(0, 3, 2, 1).reshape(B, Ww * Hh, C)
        s3 = s1[:, ::-1, :]
        s4 = s2[:, ::-1, :]
        p = (xw, xb, bcw, bcb, dw, db, yw, yb)
        y1 = _s6(s1, *p)
        y2 = _s6(s2, *p)
        y3 = _s6(s3, *p)
        y4 = _s6(s4, *p)
        y_cat = jnp.concatenate([y1, y2, y3, y4], axis=-1)
        y_merged = _linear(y_cat, mw, mb)
        gate = jax.nn.sigmoid(_linear(y_cat, gw, gb))
        out = _linear(y_merged * gate, ow, ob)
        return out.reshape(B, Hh, Ww, -1).transpose(0, 3, 1, 2)

    def _gn(v, G=32, eps=1e-5):
        B_, C_, H_, W_ = v.shape
        g = v.reshape(B_, G, C_ // G, H_, W_)
        m = jnp.mean(g, axis=(2, 3, 4), keepdims=True)
        s = jnp.var(g, axis=(2, 3, 4), keepdims=True)
        return ((g - m) / jnp.sqrt(s + eps)).reshape(v.shape)

    def _ln_c(v, eps=1e-6):
        m = jnp.mean(v, axis=1, keepdims=True)
        s = jnp.var(v, axis=1, keepdims=True)
        return (v - m) / jnp.sqrt(s + eps)

    def _ln_t(v, eps=1e-5):
        m = jnp.mean(v, axis=-1, keepdims=True)
        s = jnp.var(v, axis=-1, keepdims=True)
        return (v - m) / jnp.sqrt(s + eps)

    def _to_tokens(v):
        B_, C_, H_, W_ = v.shape
        return v.reshape(B_, C_, H_ * W_).transpose(0, 2, 1)
    def _from_tokens(t, like):
        B_, C_, H_, W_ = like.shape
        return t.transpose(0, 2, 1).reshape(B_, C_, H_, W_)

    x = x + _L0_conv_ref(_gn(x), L0_conv_W_in, L0_conv_b_in, L0_conv_w_dw, L0_conv_b_dw, L0_conv_A_log, L0_conv_Dp, L0_conv_W_x, L0_conv_W_delta, L0_conv_b_delta, L0_conv_ln_g, L0_conv_ln_b, L0_conv_W_out)
    x = x + _L1_conv_ref(_gn(x), L1_conv_xw, L1_conv_xb, L1_conv_bcw, L1_conv_bcb, L1_conv_dw, L1_conv_db, L1_conv_yw, L1_conv_yb, L1_conv_mw, L1_conv_mb, L1_conv_gw, L1_conv_gb, L1_conv_ow, L1_conv_ob)
    return x


_drawn_inputs = setup_inputs


def setup_inputs(seed=0):
    import zlib

    import numpy as np

    out = dict(_drawn_inputs(seed))
    spreads = {'L0_conv_b_in': (0.0, 0.1),
     'L0_conv_b_dw': (0.0, 0.1),
     'L0_conv_Dp': (1.0, 0.6),
     'L0_conv_ln_g': (1.0, 0.2),
     'L0_conv_ln_b': (0.0, 0.448),
     'L1_conv_xb': (0.0, 0.8),
     'L1_conv_bcb': (0.0, 0.8),
     'L1_conv_db': (0.0, 0.8),
     'L1_conv_yb': (0.0, 0.8),
     'L1_conv_mb': (0.0, 2.0),
     'L1_conv_gb': (0.0, 0.8),
     'L1_conv_ob': (0.0, 0.8)}
    factors = {'L0_conv_A_log': 8.0,
     'L0_conv_W_x': 8.0,
     'L0_conv_W_delta': 8.0,
     'L0_conv_b_delta': 8.0,
     'L1_conv_xw': 8.0,
     'L1_conv_bcw': 8.0,
     'L1_conv_dw': 8.0,
     'L1_conv_yw': 8.0,
     'L1_conv_mw': 5.833,
     'L1_conv_gw': 8.0,
     'L1_conv_ow': 2.69}
    for name, (base, spread) in spreads.items():
        noise = np.random.default_rng([zlib.crc32(name.encode()), seed]).standard_normal(out[name].shape)
        drawn = base * np.exp(spread * noise) if base else spread * noise
        out[name] = jnp.asarray(drawn.astype(out[name].dtype))
    for name, factor in factors.items():
        out[name] = (out[name] * factor).astype(out[name].dtype)
    return out
```

```python
from contextlib import ExitStack

import concourse.bass as bass
from concourse import mybir

F32 = mybir.dt.float32
ALU = mybir.AluOpType
ACT = mybir.ActivationFunctionType

B, C, H, W = 2, 96, 96, 96
L = H * W
D = 192
N = 16
KT = 4 * D // 128
T = 512
NCH = L // T
TB = T // 128
R4 = 4 * W
NR = L // R4
PW = W + 2
XC = 80
DTR, B0, C0 = 6, 32, 64
LAT = 256
RB = 2 * R4
NB = L // RB
PB = NR + NB
NPASS = 4
EPS = 1e-5
K_ID, K_SF, K_SB, K_GM, K_MEAN = 0, 128, 256, 384, 480
K_EPS = 608
K_END = 609


def vmamba_then_s6(nc, x, win, wdw, v192, wxp, alog, dp, wdel, wout, w1, b1, yw, yb, wt, bm, ow, ob, const, edge, out):
    ctx = ExitStack()
    with ctx:
        def sb(name, shape):
            return ctx.enter_context(nc.sbuf_tensor(name, shape, F32))

        def sem(name):
            return ctx.enter_context(nc.semaphore(name))

        u_d = nc.dram_tensor("u_d", [D, L], F32).ap()
        c_d = nc.dram_tensor("c_d", [2, N, T], F32).ap()
        yf_d = nc.dram_tensor("yf_d", [D, L], F32).ap()
        yb_d = nc.dram_tensor("yb_d", [D, L], F32).ap()
        yc_d = nc.dram_tensor("yc_d", [4, LAT, L], F32).ap()
        mf_d = nc.dram_tensor("mf_d", [128, 8 * 2 * LAT], F32).ap()

        cst = sb("cst", [128, K_END])
        ident = cst[:, K_ID:K_ID + 128]
        gmask = cst[0:C, K_GM:K_GM + C]
        eps = cst[:, K_EPS:K_EPS + 1]
        mean192 = cst[:, K_MEAN:K_MEAN + 128]
        seld = sb("seld", [128, KT, 128])
        wx = sb("wx", [128, 2, 4, XC])
        wdl = sb("wdl", [DTR + 1, KT * 128])
        aneg = sb("aneg", [128, N * KT])
        dps = sb("dps", [128, KT])
        vec = sb("vec", [128, 8])
        wz = sb("wz", [C, D])
        wzs = sb("wzs", [C, D])
        bzs = sb("bzs", [128, 2])
        wo = sb("wo", [128, 2, C])
        b1t = sb("b1t", [128, 8])
        b1s = sb("b1s", [128, 8])
        nb1 = sb("nb1", [128, 2])
        bmt = sb("bmt", [128, 4])
        bmf = sb("bmf", [128, 4])
        owt = sb("owt", [128, 2, C])
        obt = sb("obt", [C, 1])
        ybt = sb("ybt", [128, 2])
        onesr = sb("onesr", [1, T])
        e6 = sb("e6", [1, XC])
        bnst = sb("bnst", [C, NCH * 6])
        mv = sb("mv", [C, 2])
        gn = sb("gn", [C, 8])
        carry = sb("carry", [128, N, KT])

        AR = 44000
        arena = sb("arena", [128, AR])

        def lay(at, sizes):
            out_ = []
            for n in sizes:
                out_.append(arena[:, at:at + n])
                at += n
            assert at <= AR, at
            return out_

        (xr,) = lay(0, [L])
        xr = xr[0:C, :]
        s_wt, s_yw, s_mf = lay(0, [8 * 512, 2 * LAT, 8 * 512])
        s_wt = s_wt.rearrange("p (k m) -> p k m", k=8)
        s_yw = s_yw.rearrange("p (k m) -> p k m", k=2)
        s_mf = s_mf.rearrange("p (k m) -> p k m", k=8)
        p_xp, p_wa, p_wi, p_us = lay(L, [PW * PW, 9 * D, D, 4 * R4])
        p_wa = p_wa[0:C + 1, :].rearrange("p (t d) -> p t d", t=9)
        p_xp = p_xp[0:C + 1, :].rearrange("p (h w) -> p h w", w=PW)
        p_wi = p_wi[0:C + 1, :]
        p_us = p_us.rearrange("p (q j t) -> p q j t", q=2, j=2)
        (dt, duT, z, dA, h, hc, cb, uu, xd, ee, ll, qq, du, ys) = lay(0, [
            2 * KT * T, 2 * TB * KT * 128, 2 * TB * KT * 128, KT * T, 2 * KT * T, KT * T, 4 * T, 4 * T, T, 2 * T, 2 * T,
            T, KT * T, 3 * T])
        dt = dt.rearrange("p (q k t) -> p q k t", q=2, k=KT)
        duT = duT.rearrange("p (q b d) -> p q b d", q=2, b=TB)
        z = z.rearrange("p (q b d) -> p q b d", q=2, b=TB)
        dA = dA.rearrange("p (k t) -> p k t", k=KT)
        h = h.rearrange("p (q k t) -> p q k t", q=2, k=KT)
        hc = hc.rearrange("p (k t) -> p k t", k=KT)
        cb = cb.rearrange("p (q j t) -> p q j t", q=2, j=2)
        uu = uu.rearrange("p (j t) -> p j t", j=4)
        ee = ee.rearrange("p (q t) -> p q t", q=2)
        ll = ll.rearrange("p (q t) -> p q t", q=2)
        du = du.rearrange("p (k t) -> p k t", k=KT)
        ys = ys.rearrange("p (k t) -> p k t", k=3)
        bt = sb("bt", [128, 2, TB, N])
        (o_yf, o_yb, o_x, o_g, o_sq, o_rs, o_t, o_n, o_s, o_p) = lay(L, [4 * T, 4 * T, 2 * T, 2 * T, 2 * T, T, 2 * T,
                                                                         2 * T, 2 * T, 2 * T])
        o_yf = o_yf.rearrange("p (q j t) -> p q j t", q=2, j=2)
        o_yb = o_yb.rearrange("p (q j t) -> p q j t", q=2, j=2)
        o_x = o_x[0:C, :].rearrange("p (q t) -> p q t", q=2)
        o_g, o_sq, o_t, o_n, o_s, o_p = (v.rearrange("p (j t) -> p j t", j=2) for v in (o_g, o_sq, o_t, o_n, o_s, o_p))
        l_a, l_v, l_c, l_sg, l_t, l_h, l_y, l_w, l_ws = lay(L, [L, L, L, 2 * R4, 2 * R4, 2 * RB, 2 * RB, 8 * 128, 8 * 128])
        l_sg, l_t, l_h, l_y = (v.rearrange("p (q t) -> p q t", q=2) for v in (l_sg, l_t, l_h, l_y))
        l_w, l_ws = l_w[0:C, :], l_ws[0:C, :]
        m_f, m_y, m_g, m_p, m_o = lay(L, [8 * 512, 2 * 8 * T, 2 * T, 2 * T, T])
        m_f = m_f.rearrange("p (k m) -> p k m", k=8)
        m_y = m_y.rearrange("p (q k t) -> p q k t", q=2, k=8)
        m_g, m_p = (v.rearrange("p (j t) -> p j t", j=2) for v in (m_g, m_p))
        m_o = m_o[0:C, :]

        bank = [ctx.enter_context(nc.psum_tensor(f"bank{i}", [128, T], F32)) for i in range(8)]
        Y, DB, WB = bank[0:3], bank[3:6], bank[6:8]

        s_w = sem("weights_in")
        s_bar = sem("barrier")
        s_alone = sem("wait_carrier")
        s_set = sem("setup_step")
        s_ms = sem("merge_weight_psum"); s_mc = sem("merge_weight_copied")
        s_xin = sem("image_in")
        s_st = sem("stats_mean"); s_gp = sem("group_psum"); s_gq = sem("group_spread"); s_gs = sem("group_std"); s_psd = sem("post_std")
        s_cw = sem("conv_weights_in"); s_wa = sem("conv_weights_ready"); s_xp = sem("padded_ready")
        s_cm = sem("conv_psum"); s_us = sem("silu_done"); s_ust = [sem(f"u_stored_{q}") for q in range(2)]
        s_zero = sem("pads_zeroed"); s_edge = sem("edge_in")
        s_u = sem("u_in"); s_skip = sem("skip_added")
        s_xm = sem("xdbl_psum"); s_xd = sem("xdbl_copied"); s_cst = sem("c_stored")
        s_btp = sem("bT_psum"); s_bt = sem("bT_ready")
        s_dl = sem("delta_psum"); s_abs = sem("abs_done"); s_e = sem("exp_neg_done"); s_ln = sem("ln_done")
        s_q1 = sem("log_rest1"); s_q2 = sem("log_rest"); s_m = sem("softplus_main"); s_dt = sem("dt_ready")
        s_du = sem("du_ready"); s_ct = sem("duT_psum"); s_ev = sem("duT_ready")
        s_z = sem("z_ready"); s_exp = sem("dA_ready"); s_d = sem("dBu_ready")
        s_scan = sem("scanned"); s_hc = sem("hc_ready"); s_ns = sem("n_summed"); s_car = sem("carry_kept")
        s_c0 = sem("carry_zeroed")
        s_cb = [sem(f"c_spread_{q}") for q in range(2)]; s_yev = sem("y_copied"); s_yst = sem("y_stored")
        s_zw = sem("z_weights"); s_bzp = sem("z_bias_psum")
        s_pl = [sem(f"post_in_{q}") for q in range(2)]; s_pg = sem("post_sum"); s_pm = sem("post_mean"); s_pz = sem("post_z")
        s_pc = sem("post_centred"); s_pq = sem("post_square"); s_pv = sem("post_var"); s_pr = sem("post_rstd")
        s_pt = sem("post_norm"); s_pa = sem("post_act"); s_pp = sem("post_gated"); s_po = sem("post_out")
        s_px = sem("x1_ready")
        s_lw = sem("l1_weights_in"); s_lws = sem("l1_weights_scaled"); s_lbp = sem("l1_bias_psum"); s_lb = sem("l1_bias")
        s_lp = sem("l1_psum"); s_ls = sem("l1_gate"); s_lc = sem("l1_c"); s_lt = sem("l1_bgate"); s_lv = sem("l1_v")
        s_lh = sem("l1_scanned"); s_ly = sem("l1_y"); s_lst = [sem(f"l1_stored_{q}") for q in range(2)]; s_l0 = sem("l1_state_zeroed")
        s_mfi = sem("merge_weights_in"); s_ml = [sem(f"merge_in_{q}") for q in range(2)]; s_mp = sem("merge_psum"); s_mg = sem("merge_gate")
        s_mr = sem("merge_prod"); s_mo = sem("merge_out_psum"); s_mx = sem("merge_out"); s_mst = sem("out_stored")

        NW = 24
        NBAR = 5
        OY = 3 * NCH

        def alone(eng):
            eng.sem_inc(s_alone, 1)

        def barrier(eng, index):
            alone(eng)
            eng.drain().then_inc(s_bar, 1)
            eng.wait_ge(s_bar, 5 * (index + 1))
            alone(eng)

        def conv_rhs(r, tap):
            return p_xp[:, bass.ds(r * 4 + tap // 3, 4), tap % 3:tap % 3 + W]

        def backward(v, r):
            return v[:, ::-1][:, r * RB:(r + 1) * RB]

        block = ctx.enter_context(nc.Block())

        @block.sync
        def _(sp):
            loads = [
                (cst[:, :], const), (dps[:, :], dp), (aneg[:, :], alog), (wdl[:, :], wdel), (vec[:, :], v192),
                (wz[:, :], win[0:C, D:2 * D]), (wo[0:128, 0, :], wout[0:128, :]), (wo[0:64, 1, :], wout[128:D, :]),
                (b1t[:, :], b1), (bmt[:, :], bm), (owt[:, :, :], ow.rearrange("(k p) c -> p k c", p=128)),
                (obt[:, :], ob), (ybt[:, :], yb), (onesr[:, :], edge[0:1, 0:T]), (e6[:, :], edge[1:2, 0:XC]),
                (s_wt, wt.rearrange("(k p) m -> p k m", p=128)), (s_yw, yw.rearrange("(k p) m -> p k m", p=128)),
            ]
            for g in range(2):
                for way in range(2):
                    base = (2 * way + g) * D
                    loads.append((wx[0:128, g, 2 * way, :], wxp[base:base + 128, :]))
                    loads.append((wx[0:64, g, 2 * way + 1, :], wxp[base + 128:base + D, :]))
            assert len(loads) == NW + 1
            for ahead in (s_cst, s_yst, *s_ust, *s_lst):
                sp.sem_inc(ahead, 1)
            for to, of in loads:
                sp.dma_start(to, of).then_inc(s_w, 16)
            sp.wait_ge(s_mc, 8)
            sp.dma_start(mf_d, s_mf.rearrange("p k m -> p (k m)")).then_inc(s_set, 16)
            sp.wait_ge(s_set, 16)
            barrier(sp, 0)
            with sp.Fori(0, B) as b:
                sp.dma_start(xr, x[bass.ds(b, 1), :, :].rearrange("o c l -> (o c) l")).then_inc(s_xin, 16)
                sp.dma_start(p_wa, wdw.unsqueeze(0).broadcast_to([C + 1, 9, D])).then_inc(s_cw, 16)
                sp.dma_start(p_wi, win[:, 0:D]).then_inc(s_cw, 16)
                sp.wait_ge(s_zero, b + 1)
                alone(sp)
                sp.dma_start(p_xp[C:C + 1, :, :], edge[2:2 + 1, :].rearrange("o (h w) -> o h w", w=PW)).then_inc(s_edge, 16)
                with sp.Fori(0, NR // 2) as r2:
                    for q in range(2):
                        r = r2 * 2 + q
                        i = b * NR + r
                        sp.wait_ge(s_us, 2 * i + 6)
                        alone(sp)
                        sp.dma_start(u_d[0:128, bass.ds(r * R4, R4)], p_us[:, q, 0, :]).then_inc(s_ust[q], 16)
                        sp.dma_start(u_d[128:D, bass.ds(r * R4, R4)], p_us[0:64, q, 1, :]).then_inc(s_ust[q], 16)
                for q in range(2):
                    sp.wait_ge(s_ust[q], (b + 1) * NR * 16 + 1)
                    alone(sp)
                alone(sp)
                barrier(sp, b * NBAR + 1)

                def load_u(c, m):
                    sp.wait_ge(s_skip, m + 1)
                    alone(sp)
                    sp.wait_ge(s_du, KT * m + 1)
                    alone(sp)
                    fwd, bwd = bass.ds(c * T, T), bass.ds(L - T - c * T, T)
                    sp.dma_start(uu[:, 0, :], u_d[0:128, fwd]).then_inc(s_u, 16)
                    sp.dma_start(uu[0:64, 1, :], u_d[128:D, fwd]).then_inc(s_u, 16)
                    sp.dma_start(uu[64:128, 1, :], u_d[128:D, fwd]).then_inc(s_u, 16)
                    sp.dma_start(uu[:, 2, :], u_d[0:128, bwd]).then_inc(s_u, 16)
                    sp.dma_start(uu[0:64, 3, :], u_d[128:D, bwd]).then_inc(s_u, 16)
                    sp.dma_start(uu[64:128, 3, :], u_d[128:D, bwd]).then_inc(s_u, 16)

                def store_c(m, q):
                    sp.wait_ge(s_xd, m + 1)
                    alone(sp)
                    sp.dma_start(c_d[q], xd[C0:C0 + N, :]).then_inc(s_cst, 16)

                def store_y(c, m):
                    fwd, bwd = bass.ds(c * T, T), bass.ds(L - T - c * T, T)
                    sp.wait_ge(s_yev, 4 * (m + 1) + 1)
                    alone(sp)
                    sp.dma_start(yf_d[0:128, fwd], ys[:, 0, :]).then_inc(s_yst, 16)
                    sp.dma_start(yb_d[0:128, bwd], ys[:, 1, :]).then_inc(s_yst, 16)
                    sp.dma_start(yf_d[128:D, fwd], ys[0:64, 2, :]).then_inc(s_yst, 16)
                    sp.dma_start(yb_d[128:D, bwd], ys[64:128, 2, :]).then_inc(s_yst, 16)

                def spread_c(m, q, first, last):
                    alone(sp)
                    with sp.Fori(first, last) as p2:
                        for par in range(2):
                            p = p2 * 2 + par
                            pair = m * (N // 2) + p
                            sp.wait_ge(s_hc, 4 * pair + 1)
                            alone(sp)
                            sp.dma_start(cb[:, par, :, :], c_d[q, bass.ds(p * 2, 2), :].unsqueeze(0)
                                         .broadcast_to([128, 2, T])).then_inc(s_cb[par], 16)

                def chunk(c, q, first, last):
                    m = b * NCH + c
                    sp.wait_ge(s_cst, 16 * (m + 1) + 1)
                    alone(sp)
                    spread_c(m, q, 0, 1)
                    if not first:
                        store_y(c - 1, m - 1)
                    if not last:
                        load_u(c + 1, m + 1)
                    spread_c(m, q, 1, 2)
                    if not last:
                        store_c(m + 1, 1 - q)
                    spread_c(m, q, 2, 4)

                load_u(0, b * NCH)
                store_c(b * NCH, 0)
                chunk(0, 0, True, False)
                with sp.Fori(0, (NCH - 2) // 2) as cp:
                    chunk(cp * 2 + 1, 1, False, False)
                    chunk(cp * 2 + 2, 0, False, False)
                chunk(NCH - 1, 1, False, True)
                store_y(NCH - 1, b * NCH + NCH - 1)
                sp.wait_ge(s_yst, (b + 1) * NCH * 64 + 1)
                alone(sp)
                barrier(sp, b * NBAR + 2)

                with sp.Fori(0, NCH // 2) as c2:
                    for q in range(2):
                        c = c2 * 2 + q
                        m = b * NCH + c
                        at = bass.ds(c * T, T)
                        sp.wait_ge(s_px, m + 1)
                        alone(sp)
                        sp.dma_start(o_yf[:, q, 0, :], yf_d[0:128, at]).then_inc(s_pl[q], 16)
                        sp.dma_start(o_yf[0:64, q, 1, :], yf_d[128:D, at]).then_inc(s_pl[q], 16)
                        sp.dma_start(o_yb[:, q, 0, :], yb_d[0:128, at]).then_inc(s_pl[q], 16)
                        sp.dma_start(o_yb[0:64, q, 1, :], yb_d[128:D, at]).then_inc(s_pl[q], 16)
                        sp.dma_start(o_x[:, q, :], x[bass.ds(b, 1), :, at].rearrange("o c l -> (o c) l")).then_inc(s_pl[q], 16)
                barrier(sp, b * NBAR + 3)

                sp.dma_start(l_w, w1).then_inc(s_lw, 16)
                for o in range(NPASS):
                    order, ct = o // 2, o % 2
                    for back, n_, len_ in ((0, NR, R4), (1, NB, RB)):
                        with sp.Fori(0, n_ // 2) as r2:
                            for q in range(2):
                                r = r2 * 2 + q
                                i = (b * NPASS + o) * PB + back * NR + r
                                sp.wait_ge(s_ly, i + 3)
                                alone(sp)
                                sp.dma_start(yc_d[order + 2 * back, ct * 128:ct * 128 + 128, bass.ds(r * len_, len_)],
                                             l_y[:, q, 0:len_]).then_inc(s_lst[q], 16)
                for q in range(2):
                    sp.wait_ge(s_lst[q], (b + 1) * NPASS * PB * 8 + 1)
                    alone(sp)
                alone(sp)
                barrier(sp, b * NBAR + 4)

                sp.dma_start(m_f.rearrange("p k m -> p (k m)"), mf_d).then_inc(s_mfi, 16)
                with sp.Fori(0, NCH // 2) as c2:
                    for q in range(2):
                        c = c2 * 2 + q
                        m = b * NCH + c
                        sp.wait_ge(s_mp, 4 * (m + 1))
                        alone(sp)
                        sp.dma_start(m_y[:, q, :, :], yc_d.rearrange("d (k p) l -> p (d k) l", p=128)[:, :, bass.ds(c * T, T)]) \
                            .then_inc(s_ml[q], 16)
                barrier(sp, b * NBAR + 5)
            sp.wait_ge(s_mst, B * NCH * 16 + 1)
            alone(sp)

        @block.gpsimd
        def _(pool):
            pool.sem_inc(s_pp, 1)
            pool.sem_inc(s_hc, 5)
            pool.sem_inc(s_ly, 2)
            barrier(pool, 0)
            with pool.Fori(0, B) as b:
                pool.memset(p_xp, 0.0).then_inc(s_zero, 1)
                barrier(pool, b * NBAR + 1)

                def half_states(g, par, slot, j):
                    for s in range(2):
                        ks = slice(3 * s, 3 * s + 3)
                        pool.wait_ge(s_scan, g * KT + 3 * s + 3 + KT)
                        pool.wait_ge(s_ns, 2 * g + s + 1)
                        pool.tensor_tensor(hc[:, ks, :], h[:, par, ks, :],
                                           cb[:, slot, j, :].unsqueeze(1).broadcast_to([128, 3, T]),
                                           ALU.mult).then_inc(s_hc, 1)

                with pool.Fori(0, NCH) as c:
                    with pool.Fori(0, N // 4) as p2:
                        for slot in range(2):
                            for j in range(2):
                                g = (b * NCH + c) * N + p2 * 4 + slot * 2 + j
                                if j == 0:
                                    pool.wait_ge(s_cb[slot], ((b * NCH + c) * (N // 4) + p2 + 1) * 16)
                                half_states(g, j, slot, j)
                barrier(pool, b * NBAR + 2)
                with pool.Fori(0, NCH) as c:
                    m = b * NCH + c
                    pool.wait_ge(s_pa, 4 * (m + 1) + 1)
                    pool.wait_ge(s_po, m + 1)
                    pool.tensor_tensor(o_p[:, 0, :], o_n[:, 0, :], o_s[:, 0, :], ALU.mult).then_inc(s_pp, 1)
                    pool.tensor_tensor(o_p[0:64, 1, :], o_n[0:64, 1, :], o_s[0:64, 1, :], ALU.mult).then_inc(s_pp, 1)
                barrier(pool, b * NBAR + 3)
                for o in range(NPASS):
                    def output(i, turns, q, n_, c_):
                        pool.wait_ge(s_lst[q], 16 * turns + 1)
                        pool.wait_ge(s_lh, i + 1 + 1)
                        pool.tensor_tensor(l_y[:, q, 0:n_], l_h[:, q, 0:n_], c_, ALU.mult).then_inc(s_ly, 1)

                    with pool.Fori(0, NR // 2) as r2:
                        for q in range(2):
                            r = r2 * 2 + q
                            pool.wait_ge(s_lc, (b * NPASS + o) * NR + r + 3)
                            output((b * NPASS + o) * PB + r, (b * NPASS + o) * (PB // 2) + r2, q, R4, l_c[:, bass.ds(r * R4, R4)])
                    for r in range(NB):
                        output((b * NPASS + o) * PB + NR + r, (b * NPASS + o) * (PB // 2) + (NR + r) // 2, r % 2, RB, backward(l_c, r))
                barrier(pool, b * NBAR + 4)
                barrier(pool, b * NBAR + 5)

        @block.scalar
        def _(act):
            for ahead in (s_pq, s_pa, s_mst, s_ev):
                act.sem_inc(ahead, 1)
            act.sem_inc(s_us, 4)
            act.sem_inc(s_lc, 2)
            act.sem_inc(s_mg, 2)
            act.wait_ge(s_w, 16 * (NW + 1))
            act.activation(aneg[:, :], aneg[:, :], ACT.Exp).then_inc(s_e, 1)
            barrier(act, 0)
            def group_std(i):
                act.wait_ge(s_gp, 2 * i + 2)
                act.activation(gn[:, 5:6], WB[0][0:C, 1:2], ACT.Sqrt, bias=eps[0:C, :]).then_inc(s_gs, 1)

            with act.Fori(0, B) as b:
                group_std(b * 2)
                with act.Fori(0, NR // 2) as r2:
                    for q in range(2):
                        i = b * NR + r2 * 2 + q
                        act.wait_ge(s_ust[q], 32 * (b * (NR // 2) + r2) + 1)
                        for j, rows in ((0, 128), (1, 64)):
                            act.wait_ge(s_cm, 2 * i + j + 1)
                            act.activation(p_us[0:rows, q, j, :], bank[2 * q + j][0:rows, 0:R4], ACT.Silu,
                                           bias=vec[0:rows, 2 + j:3 + j]).then_inc(s_us, 1)
                barrier(act, b * NBAR + 1)

                def stage_a(m):
                    act.wait_ge(s_xm, m + 1)
                    act.wait_ge(s_cst, 16 * m + 1)
                    act.copy(xd[0:XC, :], WB[0][0:XC, :]).then_inc(s_xd, 1)

                def stage_b(m, q):
                    act.wait_ge(s_btp, m + 1)
                    act.copy(bt[:, q, :, :], WB[1][:, 0:TB * N].rearrange("p (b n) -> p b n", b=TB)).then_inc(s_bt, 1)
                    for k in range(KT):
                        i = m * KT + k
                        act.wait_ge(s_dl, i + 1)
                        act.wait_ge(s_dt, (i - 1 if k >= 2 else m * KT) + 1)
                        act.activation(ee[:, k % 2, :], WB[k % 2][:, :], ACT.Abs).then_inc(s_abs, 1)
                        act.wait_ge(s_abs, i + 1)
                        act.activation(ee[:, k % 2, :], ee[:, k % 2, :], ACT.Exp, scale=-1.0).then_inc(s_e, 1)
                        act.wait_ge(s_e, i + 2)
                        act.activation(ll[:, k % 2, :], ee[:, k % 2, :], ACT.Ln, bias=1.0).then_inc(s_ln, 1)

                def stage_c(m, q):
                    for k in range(KT):
                        act.wait_ge(s_ct, m * KT + k + 1 + 1)
                        act.copy(duT[:, q, :, k * 128:(k + 1) * 128], WB[k % 2][:, :].rearrange("p (b d) -> p b d", b=TB)) \
                            .then_inc(s_ev, 1)

                def states(c, q, first, last):
                    with act.Fori(first, last) as p:
                        for par in range(2):
                            n = p * 2 + par
                            g = (b * NCH + c) * N + n
                            act.wait_ge(s_d, (g + 1) * KT)
                            for t in range(TB):
                                last_z = act.activation(z[:, par, t, :], duT[:, q, t, :], ACT.Copy, scale=bt[:, q, t, bass.ds(n, 1)])
                            last_z.then_inc(s_z, 1)
                            for k in range(KT):
                                act.wait_ge(s_scan, g * KT + k + 1)
                                act.activation(dA[:, k, :], dt[:, q, k, :], ACT.Exp,
                                               scale=aneg[:, bass.ds(n * KT + k, 1)]).then_inc(s_exp, 1)

                def chunk(c, q, last):
                    m = b * NCH + c
                    act.wait_ge(s_ev, KT * (m + 1) + 1)
                    act.wait_ge(s_bt, m + 1)
                    act.wait_ge(s_dt, KT * (m + 1) + 1)
                    states(c, q, 0, 2)
                    if not last:
                        stage_a(m + 1)
                    states(c, q, 2, 4)
                    if not last:
                        stage_b(m + 1, 1 - q)
                    states(c, q, 4, 6)
                    if not last:
                        stage_c(m + 1, 1 - q)
                    states(c, q, 6, 8)

                stage_a(b * NCH)
                stage_b(b * NCH, 0)
                stage_c(b * NCH, 0)
                with act.Fori(0, (NCH - 2) // 2) as cp:
                    chunk(cp * 2, 0, False)
                    chunk(cp * 2 + 1, 1, False)
                chunk(NCH - 2, 0, False)
                chunk(NCH - 1, 1, True)
                barrier(act, b * NBAR + 2)

                with act.Fori(0, NCH) as c:
                    m = b * NCH + c
                    act.wait_ge(s_pz, m + 1)
                    act.wait_ge(s_pp, 2 * m + 1)
                    for j, rows in ((0, 128), (1, 64)):
                        act.activation(o_s[0:rows, j, :], DB[j][0:rows, :], ACT.Silu, bias=bzs[0:rows, j:j + 1]) \
                            .then_inc(s_pa, 1)
                    act.wait_ge(s_pc, 2 * (m + 1) + 1)
                    act.wait_ge(s_pv, m + 1)
                    for j, rows in ((0, 128), (1, 64)):
                        act.activation(o_sq[0:rows, j, :], o_g[0:rows, j, :], ACT.Square).then_inc(s_pq, 1)
                    act.wait_ge(s_pv, m + 1 + 1)
                    act.wait_ge(s_pt, 2 * m + 1)
                    act.activation(o_rs, WB[1][:, :], ACT.Sqrt, bias=eps).then_inc(s_psd, 1)
                    act.wait_ge(s_pt, 2 * (m + 1) + 1)
                    for j, rows in ((0, 128), (1, 64)):
                        act.activation(o_n[0:rows, j, :], o_t[0:rows, j, :], ACT.Identity, bias=vec[0:rows, 6 + j:7 + j],
                                       scale=vec[0:rows, 4 + j:5 + j]).then_inc(s_pa, 1)
                barrier(act, b * NBAR + 3)

                group_std(b * 2 + 1)
                act.wait_ge(s_lb, b + 1)
                for o in range(NPASS):
                    ct = o % 2
                    act.wait_ge(s_lh, (b * NPASS + o) * PB + 1)
                    act.wait_ge(s_ly, (b * NPASS + o) * PB + 2)
                    alone(act)
                    with act.Fori(0, NR // 2) as r2:
                        for q in range(2):
                            r = r2 * 2 + q
                            i = (b * NPASS + o) * NR + r
                            at = bass.ds(r * R4, R4)
                            pb = bank[4 * q:4 * q + 4]
                            act.wait_ge(s_lp, 4 * i + 1)
                            act.activation(l_a[:, at], pb[0][:, 0:R4], ACT.Sigmoid, bias=nb1[:, ct:ct + 1], scale=-1.0)
                            act.wait_ge(s_lt, i + 1)
                            act.activation(l_sg[:, q, :], pb[0][:, 0:R4], ACT.Sigmoid, bias=b1s[:, ct:ct + 1]) \
                                .then_inc(s_ls, 1)
                            act.wait_ge(s_lp, 4 * i + 4)
                            act.activation(l_c[:, at], pb[3][:, 0:R4], ACT.Identity, bias=b1s[:, 6 + ct:7 + ct]) \
                                .then_inc(s_lc, 1)
                barrier(act, b * NBAR + 4)
                def gates(m):
                    for j in range(2):
                        act.wait_ge(s_mp, 8 + 4 * m + 2 * j + 1)
                        act.wait_ge(s_mr, 2 * m + j + 1)
                        act.activation(m_g[:, j, :], bank[2 * j][:, :], ACT.Sigmoid, bias=bmf[:, 2 + j:3 + j]) \
                            .then_inc(s_mg, 1)

                def store(m, c):
                    act.wait_ge(s_mx, m + 1 + 1)
                    act.dma_start(out[bass.ds(b, 1), :, bass.ds(c * T, T)].rearrange("o c l -> (o c) l"), m_o) \
                        .then_inc(s_mst, 16)

                gates(b * NCH)
                with act.Fori(1, NCH) as c:
                    gates(b * NCH + c)
                    store(b * NCH + c - 1, c - 1)
                store(b * NCH + NCH - 1, NCH - 1)
                act.wait_ge(s_mst, (b + 1) * NCH * 16 + 1)
                barrier(act, b * NBAR + 5)

        @block.vector
        def _(dve):
            for ahead in (s_du, s_dt, s_pt, s_lh, s_yev, s_pc, s_pr, s_mx):
                dve.sem_inc(ahead, 1)
            dve.sem_inc(s_scan, KT)
            dve.sem_inc(s_car, N)
            dve.sem_inc(s_px, 2)
            dve.sem_inc(s_lt, 2)
            dve.sem_inc(s_lv, 2)
            dve.sem_inc(s_mr, 2)
            dve.wait_ge(s_w, 16 * (NW + 1))
            dve.tensor_tensor(wx[:, 0, 0:4:2, :], wx[:, 0, 0:4:2, :], wx[:, 1, 0:4:2, :], ALU.add)
            dve.tensor_tensor(wx[0:64, 0, 1:4:2, :], wx[0:64, 0, 1:4:2, :], wx[0:64, 1, 1:4:2, :], ALU.add)
            for k in range(KT):
                s = K_SF if k == 2 else K_SB if k == 5 else K_ID
                dve.tensor_scalar(seld[:, k, :], cst[:, s:s + 128], dps[:, k:k + 1], None, ALU.mult)
            dve.wait_ge(s_e, 1)
            dve.tensor_scalar(aneg[:, :], aneg[:, :], -1.0, None, ALU.mult)
            for i in range(8):
                dve.wait_ge(s_ms, i + 1)
                dve.tensor_copy(s_mf[:, i, :], bank[i][:, :]).then_inc(s_mc, 1)
            dve.wait_ge(s_ms, 9)
            dve.tensor_tensor(bmf[:, :], bank[0][:, 0:4], bmt[:, :], ALU.add)
            barrier(dve, 0)

            def group_norm(i):
                for c in range(NCH):
                    dve.bn_stats(bnst[:, 6 * c:6 * c + 6], xr[:, c * T:(c + 1) * T])
                dve.drain()
                dve.bn_aggr(mv[:, :], bnst[:, :]).then_inc(s_st, 1)
                dve.wait_ge(s_gp, 2 * i + 1)
                dve.tensor_copy(gn[:, 0:1], WB[0][0:C, 0:1])
                dve.drain()
                dve.tensor_tensor(gn[:, 1:2], mv[:, 0:1], gn[:, 0:1], ALU.subtract)
                dve.drain()
                dve.scalar_tensor_tensor(gn[:, 2:3], gn[:, 1:2], gn[:, 1:2], mv[:, 1:2], ALU.mult, ALU.add) \
                    .then_inc(s_gq, 1)
                dve.wait_ge(s_gs, i + 1)
                dve.reciprocal(gn[:, 3:4], gn[:, 5:6])
                dve.drain()
                dve.scalar_tensor_tensor(gn[:, 4:5], gn[:, 0:1], -1.0, gn[:, 3:4], ALU.mult, ALU.mult)
                dve.drain()

            with dve.Fori(0, B) as b:
                dve.wait_ge(s_xin, 16 * (b + 1))
                group_norm(b * 2)
                dve.tensor_scalar(wzs[:, :], wz[:, :], gn[:, 3:4], None, ALU.mult).then_inc(s_zw, 1)
                dve.wait_ge(s_bzp, b + 1)
                dve.tensor_tensor(bzs[:, 0:1], WB[1][:, 0:1], vec[:, 0:1], ALU.add)
                dve.tensor_tensor(bzs[0:64, 1:2], WB[1][0:64, 1:2], vec[0:64, 1:2], ALU.add)
                dve.wait_ge(s_cw, 32 * (b + 1))
                dve.tensor_tensor(p_wa, p_wa, p_wi.unsqueeze(1).broadcast_to([C + 1, 9, D]), ALU.mult).then_inc(s_wa, 1)
                dve.wait_ge(s_zero, b + 1)
                dve.tensor_scalar(p_xp[0:C, 1:H + 1, 1:W + 1], xr.rearrange("c (h w) -> c h w", w=W), gn[:, 3:4],
                                  gn[:, 4:5], ALU.mult, ALU.add).then_inc(s_xp, 1)
                barrier(dve, b * NBAR + 1)

                dve.memset(carry[:, :, :], 0.0).then_inc(s_c0, 1)
                dve.wait_ge(s_c0, b + 1)

                def stage_b(m, q):
                    for k in range(KT):
                        i = m * KT + k
                        dve.wait_ge(s_e, i + 2)
                        dve.wait_ge(s_dt, i + 1)
                        dve.tensor_scalar(qq, ee[:, k % 2, :], 1.0, -1.0, ALU.add, ALU.add).then_inc(s_q1, 1)
                        dve.wait_ge(s_q1, i + 1)
                        dve.tensor_tensor(qq, ee[:, k % 2, :], qq, ALU.subtract).then_inc(s_q2, 1)
                        dve.wait_ge(s_ln, i + 1)
                        dve.scalar_tensor_tensor(ll[:, k % 2, :], WB[k % 2][:, :], 0.0, ll[:, k % 2, :], ALU.max, ALU.add) \
                            .then_inc(s_m, 1)
                        dve.wait_ge(s_q2, i + 1)
                        dve.wait_ge(s_m, i + 1)
                        dve.tensor_tensor(dt[:, q, k, :], ll[:, k % 2, :], qq, ALU.add).then_inc(s_dt, 1)
                        dve.wait_ge(s_dt, i + 1 + 1)
                        dve.wait_ge(s_ct, KT * m + 1)
                        u = uu[:, (0, 0, 1, 2, 2, 3)[k], :]
                        dve.tensor_tensor(du[:, k, :], dt[:, q, k, :], u if k < 3 else u[:, ::-1], ALU.mult).then_inc(s_du, 1)

                def scans(c, n, par):
                    g = (b * NCH + c) * N + n
                    dve.wait_ge(s_car, g + 1)
                    for k in range(KT):
                        if k % 3 == 0:
                            dve.wait_ge(s_hc, 2 * g + k // 3 + 2)
                        dve.wait_ge(s_exp, g * KT + k + 1)
                        dve.wait_ge(s_d, (g + 2) * KT + k + 1)
                        dve.tensor_tensor_scan(h[:, par, k, :], dA[:, k, :], DB[k % 3][:, :],
                                               carry[:, bass.ds(n, 1), k], ALU.mult, ALU.add).then_inc(s_scan, 1)
                    dve.wait_ge(s_scan, (g + 2) * KT)
                    alone(dve)
                    dve.tensor_copy(carry[:, bass.ds(n, 1), :].rearrange("p o k -> p (o k)"),
                                    h[:, par, :, T - 1]).then_inc(s_car, 1)

                def copy_y(m):
                    dve.wait_ge(s_ns, 2 * N * (m + 1) + 2)
                    dve.wait_ge(s_yst, 64 * m + 1)
                    dve.tensor_copy(ys[:, 0, :], Y[0][:, :]).then_inc(s_yev, 1)
                    dve.tensor_copy(ys[:, 1, ::-1], Y[1][:, :]).then_inc(s_yev, 1)
                    dve.tensor_copy(ys[0:64, 2, :], Y[2][0:64, :]).then_inc(s_yev, 1)
                    dve.tensor_copy(ys[64:128, 2, ::-1], Y[2][64:128, :]).then_inc(s_yev, 1)

                def chunk(c, q, first, last):
                    m = b * NCH + c
                    scans(c, 0, 0)
                    if not first:
                        copy_y(m - 1)
                    scans(c, 1, 1)
                    with dve.Fori(1, 2) as p:
                        scans(c, p * 2, 0)
                        scans(c, p * 2 + 1, 1)
                    with dve.Fori(2, 4) as p:
                        scans(c, p * 2, 0)
                        scans(c, p * 2 + 1, 1)
                    if not last:
                        stage_b(m + 1, 1 - q)
                    with dve.Fori(4, 8) as p:
                        scans(c, p * 2, 0)
                        scans(c, p * 2 + 1, 1)

                stage_b(b * NCH, 0)
                chunk(0, 0, True, False)
                with dve.Fori(0, (NCH - 2) // 2) as cp:
                    chunk(cp * 2 + 1, 1, False, False)
                    chunk(cp * 2 + 2, 0, False, False)
                chunk(NCH - 1, 1, False, True)
                copy_y(b * NCH + NCH - 1)
                barrier(dve, b * NBAR + 2)

                with dve.Fori(0, NCH // 2) as c2:
                    for q in range(2):
                        c = c2 * 2 + q
                        m = b * NCH + c
                        dve.wait_ge(s_pl[q], 80 * (b * (NCH // 2) + c2 + 1))
                        dve.wait_ge(s_pq, 2 * m + 1)
                        for j, rows in ((0, 128), (1, 64)):
                            dve.tensor_tensor(o_g[0:rows, j, :], o_yf[0:rows, q, j, :], o_yb[0:rows, q, j, :], ALU.add) \
                                .then_inc(s_pg, 1)
                        dve.wait_ge(s_pm, m + 1)
                        for j, rows in ((0, 128), (1, 64)):
                            dve.tensor_tensor(o_g[0:rows, j, :], o_g[0:rows, j, :], WB[0][0:rows, :], ALU.subtract) \
                                .then_inc(s_pc, 1)
                        dve.wait_ge(s_psd, m + 1)
                        dve.reciprocal(o_rs, o_rs).then_inc(s_pr, 1)
                        dve.wait_ge(s_pr, m + 1 + 1)
                        dve.wait_ge(s_pc, 2 * (m + 1) + 1)
                        dve.wait_ge(s_pa, 4 * m + 1)
                        for j, rows in ((0, 128), (1, 64)):
                            dve.tensor_tensor(o_t[0:rows, j, :], o_g[0:rows, j, :], o_rs[0:rows, :], ALU.mult) \
                                .then_inc(s_pt, 1)
                        dve.wait_ge(s_po, m + 1 + 1)
                        dve.tensor_tensor(xr[:, bass.ds(c * T, T)], Y[0][0:C, :], o_x[:, q, :], ALU.add).then_inc(s_px, 1)
                barrier(dve, b * NBAR + 3)

                group_norm(b * 2 + 1)
                dve.wait_ge(s_lw, 16 * (b + 1))
                dve.tensor_scalar(l_ws, l_w, gn[:, 3:4], None, ALU.mult).then_inc(s_lws, 1)
                dve.wait_ge(s_lbp, b + 1)
                dve.tensor_tensor(b1s[:, :], WB[1][:, 0:8], b1t[:, :], ALU.add)
                dve.drain()
                dve.tensor_scalar(nb1[:, :], b1s[:, 0:2], -1.0, None, ALU.mult).then_inc(s_lb, 1)
                for o in range(NPASS):
                    ct = o % 2

                    def zero_state(base, n_, count):
                        dve.wait_ge(s_ly, base + 2)
                        dve.memset(l_h[:, 1, n_ - 1:n_], 0.0).then_inc(s_l0, 1)
                        dve.wait_ge(s_l0, count)
                        alone(dve)

                    def scan(i, q, n_, a_, v_):
                        dve.wait_ge(s_lh, i + 1)
                        dve.wait_ge(s_ly, i + 1)
                        dve.tensor_tensor_scan(l_h[:, q, 0:n_], a_, v_, l_h[:, 1 - q, n_ - 1:n_],
                                               ALU.mult, ALU.add).then_inc(s_lh, 1)

                    base = (b * NPASS + o) * PB
                    zero_state(base, R4, (b * NPASS + o) * 2 + 1)
                    with dve.Fori(0, NR // 2) as r2:
                        for q in range(2):
                            r = r2 * 2 + q
                            i = (b * NPASS + o) * NR + r
                            at = bass.ds(r * R4, R4)
                            pb = bank[4 * q:4 * q + 4]
                            dve.wait_ge(s_ls, i + 1)
                            dve.wait_ge(s_lp, 4 * i + 2)
                            dve.scalar_tensor_tensor(l_t[:, q, :], pb[1][:, 0:R4], b1s[:, 4 + ct:5 + ct],
                                                     l_sg[:, q, :], ALU.add, ALU.mult).then_inc(s_lt, 1)
                            dve.wait_ge(s_lt, i + 3)
                            dve.wait_ge(s_lp, 4 * i + 3)
                            dve.scalar_tensor_tensor(l_v[:, at], pb[2][:, 0:R4], b1s[:, 2 + ct:3 + ct],
                                                     l_t[:, q, :], ALU.add, ALU.mult).then_inc(s_lv, 1)
                            dve.wait_ge(s_lv, i + 3)
                            scan(base + r, q, R4, l_a[:, at], l_v[:, at])
                    zero_state(base + NR, RB, (b * NPASS + o) * 2 + 2)
                    for r in range(NB):
                        scan(base + NR + r, r % 2, RB, backward(l_a, r), backward(l_v, r))
                barrier(dve, b * NBAR + 4)
                def close(m, c):
                    dve.wait_ge(s_mo, m + 1)
                    dve.wait_ge(s_mst, 16 * m + 1)
                    dve.scalar_tensor_tensor(m_o, bank[4][0:C, :], obt[:, 0:1], xr[:, bass.ds(c * T, T)],
                                             ALU.add, ALU.add).then_inc(s_mx, 1)

                def products(m):
                    for j in range(2):
                        dve.wait_ge(s_mg, 2 * m + j + 3)
                        dve.wait_ge(s_mp, 8 + 4 * m + 2 * j + 2)
                        dve.scalar_tensor_tensor(m_p[:, j, :], bank[2 * j + 1][:, :], bmf[:, j:j + 1], m_g[:, j, :],
                                                 ALU.add, ALU.mult).then_inc(s_mr, 1)

                products(b * NCH)
                with dve.Fori(1, NCH) as c:
                    close(b * NCH + c - 1, c - 1)
                    products(b * NCH + c)
                close(b * NCH + NCH - 1, NCH - 1)
                barrier(dve, b * NBAR + 5)

        @block.tensor
        def _(pe):
            for ahead in (s_skip, s_po, s_pv, s_ct):
                pe.sem_inc(ahead, 1)
            pe.sem_inc(s_d, 2 * KT)
            pe.sem_inc(s_ns, 2)
            pe.sem_inc(s_mp, 8)
            pe.wait_ge(s_w, 16 * (NW + 1))
            for d in range(4):
                for ct in range(2):
                    for j in range(2):
                        mm = pe.matmul(bank[2 * d + ct][:, :], s_yw[:, j, ct * 128:ct * 128 + 128], s_wt[:, 2 * d + j, :],
                                       start=(j == 0), stop=(j == 1))
                    mm.then_inc(s_ms, 1)
            pe.wait_ge(s_mc, 8)
            for i in range(4):
                for k in range(8):
                    mm = pe.matmul(bank[0][:, i:i + 1], s_wt[:, k, i * 128:i * 128 + 128], ybt[:, k % 2:k % 2 + 1],
                                   start=(k == 0), stop=(k == 7))
            mm.then_inc(s_ms, 1)
            barrier(pe, 0)

            def group_norm(i):
                pe.wait_ge(s_st, i + 1)
                pe.matmul(WB[0][0:C, 0:1], gmask, mv[:, 0:1], start=True, stop=True).then_inc(s_gp, 1)
                pe.wait_ge(s_gq, i + 1)
                pe.matmul(WB[0][0:C, 1:2], gmask, gn[:, 2:3], start=True, stop=True).then_inc(s_gp, 1)

            with pe.Fori(0, B) as b:
                group_norm(b * 2)
                pe.wait_ge(s_zw, b + 1)
                pe.matmul(WB[1][:, 0:1], wz[:, 0:128], gn[:, 4:5], start=True, stop=True)
                pe.matmul(WB[1][0:64, 1:2], wz[:, 128:D], gn[:, 4:5], start=True, stop=True).then_inc(s_bzp, 1)
                pe.wait_ge(s_wa, b + 1)
                pe.wait_ge(s_edge, 16 * (b + 1))
                pe.wait_ge(s_xp, b + 1)
                alone(pe)
                with pe.Fori(0, NR // 2) as r2:
                    for q in range(2):
                        r = r2 * 2 + q
                        i = b * NR + r
                        pe.wait_ge(s_us, 2 * i + 2)
                        for j, d0, rows in ((0, 0, 128), (1, 128, 64)):
                            for tap in range(9):
                                mm = pe.matmul(bank[2 * q + j][0:rows, 0:R4], p_wa[:, tap, d0:d0 + rows], conv_rhs(r, tap),
                                               start=(tap == 0), stop=(tap == 8))
                            mm.then_inc(s_cm, 1)
                barrier(pe, b * NBAR + 1)

                def stage_a(m):
                    pe.wait_ge(s_u, 96 * (m + 1))
                    pe.wait_ge(s_ev, KT * m + 1)
                    o = WB[0][0:XC, :]
                    pe.matmul(o, wx[:, 0, 0, :], uu[:, 0, :], start=True, stop=False)
                    pe.matmul(o, wx[0:64, 0, 1, :], uu[0:64, 1, :], start=False, stop=False)
                    pe.matmul(o, wx[:, 0, 2, :], uu[:, 2, ::-1], start=False, stop=False)
                    pe.matmul(o, wx[0:64, 0, 3, :], uu[0:64, 3, ::-1], start=False, stop=False)
                    pe.matmul(o, e6[:, :], onesr[:, :], start=False, stop=True).then_inc(s_xm, 1)

                def stage_b(m):
                    pe.wait_ge(s_xd, m + 1)
                    alone(pe)
                    for t in range(TB):
                        mm = pe.transpose(WB[1][:, t * N:(t + 1) * N], xd[B0:B0 + N, t * 128:(t + 1) * 128],
                                          cst[B0:B0 + N, K_ID + B0:K_ID + B0 + N])
                    mm.then_inc(s_btp, 1)
                    for k in range(KT):
                        i = m * KT + k
                        if k == 1:
                            pe.wait_ge(s_bt, m + 1)
                        if k >= 2:
                            pe.wait_ge(s_m, i - 1)
                        pe.matmul(WB[k % 2][:, :], wdl[:, k * 128:(k + 1) * 128], xd[0:DTR + 1, :], start=True, stop=True) \
                            .then_inc(s_dl, 1)

                def stage_c(m):
                    pe.wait_ge(s_du, KT * (m + 1) + 1)
                    for k in range(KT):
                        if k >= 2:
                            pe.wait_ge(s_ev, m * KT + k - 1 + 1)
                        for t in range(TB):
                            mm = pe.transpose(WB[k % 2][:, t * 128:(t + 1) * 128], du[:, k, t * 128:(t + 1) * 128], ident)
                        mm.then_inc(s_ct, 1)

                def turn(g, par):
                    pe.wait_ge(s_z, g + 1)
                    for k in range(KT):
                        pe.wait_ge(s_scan, g * KT + k + 4)
                        for t in range(TB):
                            mm = pe.transpose(DB[k % 3][:, t * 128:(t + 1) * 128], z[:, par, t, k * 128:(k + 1) * 128], ident)
                        mm.then_inc(s_d, 1)

                def state_sum(g):
                    for s in range(2):
                        pe.wait_ge(s_hc, 2 * g + s + 6)
                        for k in range(3 * s, 3 * s + 3):
                            w = cst[:, K_SF:K_SF + 128] if k == 2 else cst[:, K_SB:K_SB + 128] if k == 5 else ident
                            mm = pe.matmul(Y[2 if k % 3 == 2 else k // 3][:, :], w, hc[:, k, :], start=False, stop=True,
                                           skip_group_check=True)
                        mm.then_inc(s_ns, 1)

                def skip(m):
                    pe.wait_ge(s_yev, 4 * m + 1)
                    for k in range(KT):
                        u = uu[:, (0, 0, 1, 2, 2, 3)[k], :]
                        mm = pe.matmul(Y[2 if k % 3 == 2 else k // 3][:, :], seld[:, k, :], u if k < 3 else u[:, ::-1],
                                       start=(k in (0, 2, 3)), stop=(k in (1, 4, 5)), skip_group_check=True)
                    mm.then_inc(s_skip, 1)

                def chunk(c, last):
                    m = b * NCH + c
                    g0 = m * N

                    def pair(j):
                        turn(g0 + j * 2, 0)
                        state_sum(g0 + j * 2 - 1)
                        turn(g0 + j * 2 + 1, 1)
                        state_sum(g0 + j * 2)

                    skip(m)
                    turn(g0 + 1, 1)
                    state_sum(g0)
                    with pe.Fori(1, 2) as j:
                        pair(j)
                    if not last:
                        stage_a(m + 1)
                    with pe.Fori(2, 4) as j:
                        pair(j)
                    if not last:
                        stage_b(m + 1)
                    with pe.Fori(4, 6) as j:
                        pair(j)
                    if not last:
                        stage_c(m + 1)
                    with pe.Fori(6, 8) as j:
                        pair(j)
                    if not last:
                        turn(g0 + N, 0)
                    state_sum(g0 + N - 1)

                stage_a(b * NCH)
                stage_b(b * NCH)
                stage_c(b * NCH)
                turn(b * NCH * N, 0)
                with pe.Fori(0, NCH - 1) as c:
                    chunk(c, False)
                chunk(NCH - 1, True)
                barrier(pe, b * NBAR + 2)

                with pe.Fori(0, NCH // 2) as c2:
                    for q in range(2):
                        m = b * NCH + c2 * 2 + q
                        pe.wait_ge(s_pl[q], 80 * (b * (NCH // 2) + c2 + 1))
                        pe.wait_ge(s_pa, 4 * m + 1)
                        pe.matmul(DB[0][:, :], wzs[:, 0:128], o_x[:, q, :], start=True, stop=True)
                        pe.matmul(DB[1][0:64, :], wzs[:, 128:D], o_x[:, q, :], start=True, stop=True).then_inc(s_pz, 1)
                        pe.wait_ge(s_pg, 2 * (m + 1))
                        pe.wait_ge(s_pc, 2 * m + 1)
                        pe.matmul(WB[0][:, :], mean192, o_g[:, 0, :], start=True, stop=False)
                        pe.matmul(WB[0][:, :], mean192[0:64, :], o_g[0:64, 1, :], start=False, stop=True).then_inc(s_pm, 1)
                        pe.wait_ge(s_pq, 2 * (m + 1) + 1)
                        pe.wait_ge(s_pr, m + 1)
                        pe.matmul(WB[1][:, :], mean192, o_sq[:, 0, :], start=True, stop=False)
                        pe.matmul(WB[1][:, :], mean192[0:64, :], o_sq[0:64, 1, :], start=False, stop=True).then_inc(s_pv, 1)
                        pe.wait_ge(s_pp, 2 * (m + 1) + 1)
                        pe.wait_ge(s_px, m + 2)
                        pe.matmul(Y[0][0:C, :], wo[:, 0, :], o_p[:, 0, :], start=True, stop=False)
                        pe.matmul(Y[0][0:C, :], wo[0:64, 1, :], o_p[0:64, 1, :], start=False, stop=True).then_inc(s_po, 1)
                barrier(pe, b * NBAR + 3)

                group_norm(b * 2 + 1)
                pe.wait_ge(s_lws, b + 1)
                for j in range(8):
                    mm = pe.matmul(WB[1][:, j:j + 1], l_w[:, j * 128:(j + 1) * 128], gn[:, 4:5], start=True, stop=True)
                mm.then_inc(s_lbp, 1)
                pe.wait_ge(s_lb, b + 1)
                alone(pe)
                for o in range(NPASS):
                    order, ct = o // 2, o % 2
                    xv = xr.rearrange("c (h w) -> c h w", w=W)
                    if order:
                        xv = xv.rearrange("c h w -> c w h")
                    with pe.Fori(0, NR // 2) as r2:
                        for q in range(2):
                            r = r2 * 2 + q
                            i = (b * NPASS + o) * NR + r
                            pe.wait_ge(s_lc, i + 1)
                            pe.wait_ge(s_lv, i + 1)
                            for j in range(4):
                                w = 2 * (0, 2, 1, 3)[j] + ct
                                pe.matmul(bank[4 * q + j][:, 0:R4], l_ws[:, w * 128:(w + 1) * 128],
                                          xv[:, bass.ds(r * 4, 4), :], start=True, stop=True).then_inc(s_lp, 1)
                barrier(pe, b * NBAR + 4)

                def mix(m, turns, q, j):
                    pe.wait_ge(s_ml[q], 16 * turns)
                    pe.wait_ge(s_mr if j % 2 else s_mg, 2 * m + j // 2 + 1)
                    col = (LAT if j % 2 == 0 else 0) + (j // 2) * 128
                    for k in range(8):
                        mm = pe.matmul(bank[j][:, :], m_f[:, k, col:col + 128], m_y[:, q, k, :], start=(k == 0), stop=(k == 7))
                    mm.then_inc(s_mp, 1)

                def project(m):
                    pe.wait_ge(s_mr, 2 * m + 4)
                    pe.wait_ge(s_mx, m + 1)
                    for j in range(2):
                        mm = pe.matmul(bank[4][0:C, :], owt[:, j, :], m_p[:, j, :], start=(j == 0), stop=(j == 1))
                    mm.then_inc(s_mo, 1)

                def merge_chunk(m, turns, q, first):
                    mix(m, turns, q, 0)
                    if not first:
                        project(m - 1)
                    for j in range(1, 4):
                        mix(m, turns, q, j)

                pe.wait_ge(s_mfi, 16 * (b + 1))
                turns = b * (NCH // 2) + 1
                merge_chunk(b * NCH, turns, 0, True)
                with pe.Fori(0, (NCH - 2) // 2) as c2:
                    merge_chunk(b * NCH + c2 * 2 + 1, turns + c2, 1, False)
                    merge_chunk(b * NCH + c2 * 2 + 2, turns + c2 + 1, 0, False)
                merge_chunk(b * NCH + NCH - 1, turns + NCH // 2 - 1, 1, False)
                project(b * NCH + NCH - 1)
                barrier(pe, b * NBAR + 5)


def kernel(**inputs):
    import numpy as np
    import concourse.bacc as bacc
    from concourse import mybir as _mybir
    from concourse.bass_utils import run_bass_kernel_spmd

    v = {k: np.asarray(a) for k, a in inputs.items()}
    f = np.float32

    def tiles(a, n):
        out = np.zeros((n * 128,), f)
        out[:a.shape[0]] = a
        return out.reshape(n, 128).T

    order = []
    for way in range(2):
        for g in range(2):
            order += [(2 * way + g) * D + c for c in range(128)]
        for g in range(2):
            order += [(2 * way + g) * D + 128 + c for c in range(64)]
    order = np.array(order)
    wx = v["L0_conv_W_x"]
    wxp = np.zeros((4 * D, XC), f)
    wxp[:, 0:DTR] = wx[:, 0:DTR]
    wxp[:, B0:B0 + N] = wx[:, DTR:DTR + N]
    wxp[:, C0:C0 + N] = wx[:, DTR + N:]
    const = np.zeros((128, K_END), f)
    p = np.arange(128)
    const[p, K_ID + p] = 1
    const[p, K_SF + p % 64] = 1
    const[p, K_SB + 64 + p % 64] = 1
    c = np.arange(C)
    const[:C, K_GM:K_GM + C] = (c[:, None] // 3 == c[None, :] // 3) / f(3)
    const[:, K_MEAN:K_MEAN + 128] = 1 / D
    const[:, K_EPS] = EPS
    edge = np.zeros((3, PW * PW), f)
    edge[0] = 1
    edge[1, DTR] = 1
    inner = np.zeros((PW, PW), f)
    inner[1:-1, 1:-1] = 1
    edge[2] = inner.reshape(-1)
    bz = v["L0_conv_b_in"][D:]
    arrays = {
        "x": v["x"].reshape(B, C, L),
        "win": np.concatenate([v["L0_conv_W_in"], v["L0_conv_b_in"][None]], 0),
        "wdw": v["L0_conv_w_dw"].reshape(D, 9).T,
        "v192": np.concatenate([tiles(a, 2) for a in (bz, v["L0_conv_b_dw"], v["L0_conv_ln_g"], v["L0_conv_ln_b"])], 1),
        "wxp": wxp,
        "alog": v["L0_conv_A_log"][order].reshape(KT, 128, N).transpose(1, 2, 0).reshape(128, N * KT),
        "dp": v["L0_conv_Dp"][order].reshape(KT, 128).T,
        "wdel": np.concatenate([v["L0_conv_W_delta"], v["L0_conv_b_delta"][None]], 0)[:, order],
        "wout": v["L0_conv_W_out"],
        "w1": np.concatenate([v["L1_conv_dw"], v["L1_conv_xw"], v["L1_conv_bcw"]], 0).T,
        "b1": tiles(np.concatenate([v["L1_conv_db"], v["L1_conv_xb"], v["L1_conv_bcb"]]), 8),
        "yw": v["L1_conv_yw"],
        "yb": tiles(v["L1_conv_yb"], 2),
        "wt": np.concatenate([v["L1_conv_mw"], v["L1_conv_gw"]], 0).T,
        "bm": tiles(np.concatenate([v["L1_conv_mb"], v["L1_conv_gb"]]), 4),
        "ow": v["L1_conv_ow"].T,
        "ob": v["L1_conv_ob"].reshape(C, 1),
        "const": const,
        "edge": edge,
    }
    nc = bacc.Bacc("TRN2", target_bir_lowering=False, num_devices=1)
    feeds, args = {}, []
    for name, a in arrays.items():
        a = np.ascontiguousarray(a)
        feeds[f"in_{name}"] = a
        args.append(nc.dram_tensor(f"in_{name}", a.shape, _mybir.dt.from_np(a.dtype), kind="ExternalInput").ap())
    y = nc.dram_tensor("out_0", (B, C, L), F32, kind="ExternalOutput").ap()
    vmamba_then_s6(nc, *args, y)
    r = run_bass_kernel_spmd(nc, [feeds], core_ids=[0])
    return r.results[0]["out_0"].reshape(B, C, H, W)
```

```python
from contextlib import ExitStack

import concourse.bass as bass
from concourse import mybir

F32 = mybir.dt.float32
ALU = mybir.AluOpType
ACT = mybir.ActivationFunctionType

B, C, H, W = 2, 96, 96, 96
L = H * W
D = 192
N = 16
KT = 4 * D // 128
T = 512
NCH = L // T
TB = T // 128
KP = 4
R4 = 4 * W
NR = L // R4
PW = W + 2
XC = 80
DTR, B0, C0 = 6, 32, 64
LAT = 256
RB = 2 * R4
NB = L // RB
PB = NR + NB
S_XA, S_XD = 2, 4
S_DL, S_SP = 4, 6
S_CT, S_EV = 11, 13
NPASS = 4
EPS = 1e-5
K_ID, K_SEL, K_GM, K_MEAN = 0, 128, 192, 288
K_EPS = 416
K_END = 417


def vmamba_then_s6(nc, x, win, wdw, v192, wxp, alog, dp, wdel, wout, w1, b1, yw, yb, wt, bm, ow, ob, const, inner, out):
    ctx = ExitStack()
    with ctx:
        def sb(name, shape):
            return ctx.enter_context(nc.sbuf_tensor(name, shape, F32))

        def sem(name):
            return ctx.enter_context(nc.semaphore(name))

        u_d = nc.dram_tensor("u_d", [D, L], F32).ap()
        bc_d = nc.dram_tensor("bc_d", [2, N, 2, T], F32).ap()
        yf_d = nc.dram_tensor("yf_d", [D, L], F32).ap()
        yb_d = nc.dram_tensor("yb_d", [D, L], F32).ap()
        yc_d = nc.dram_tensor("yc_d", [4, LAT, L], F32).ap()
        mf_d = nc.dram_tensor("mf_d", [128, 8 * 2 * LAT], F32).ap()

        cst = sb("cst", [128, K_END])
        ident = cst[:, K_ID:K_ID + 128]
        gmask = cst[0:C, K_GM:K_GM + C]
        eps = cst[:, K_EPS:K_EPS + 1]
        mean192 = cst[:, K_MEAN:K_MEAN + 128]
        sel = cst[:, K_SEL:K_SEL + 64]
        wx = sb("wx", [128, 2, 4, XC])
        wdl = sb("wdl", [97, KT * 128])
        aneg = sb("aneg", [128, N * KT])
        dps = sb("dps", [128, 2, 4])
        dsum = sb("dsum", [128, 2])
        vec = sb("vec", [128, 8])
        wz = sb("wz", [C, D])
        wzs = sb("wzs", [C, D])
        bzs = sb("bzs", [128, 2])
        wo = sb("wo", [128, 2, C])
        b1t = sb("b1t", [128, 8])
        b1s = sb("b1s", [128, 8])
        nb1 = sb("nb1", [128, 2])
        bmt = sb("bmt", [128, 4])
        bmf = sb("bmf", [128, 4])
        owt = sb("owt", [128, 2, C])
        obt = sb("obt", [C, 1])
        ybt = sb("ybt", [128, 2])
        bnst = sb("bnst", [C, NCH * 6])
        mv = sb("mv", [C, 2])
        gn = sb("gn", [C, 8])
        carry = sb("carry", [128, N, KT])

        AR = 44000
        arena = sb("arena", [128, AR])

        def lay(at, sizes):
            out_ = []
            for n in sizes:
                out_.append(arena[:, at:at + n])
                at += n
            assert at <= AR, at
            return out_

        (xr,) = lay(0, [L])
        xr = xr[0:C, :]
        s_wt, s_yw, s_mf = lay(0, [8 * 512, 2 * LAT, 8 * 512])
        s_wt = s_wt.rearrange("p (k m) -> p k m", k=8)
        s_yw = s_yw.rearrange("p (k m) -> p k m", k=2)
        s_mf = s_mf.rearrange("p (k m) -> p k m", k=8)
        p_xp, p_wa, p_wi, p_wb, p_us = lay(L, [PW * PW, 9 * D, D, 12 * 128, 6 * R4])
        p_wa = p_wa[0:C + 1, :].rearrange("p (t d) -> p t d", t=9)
        p_xp = p_xp[0:C + 1, :].rearrange("p (h w) -> p h w", w=PW)
        p_wi = p_wi[0:C + 1, :]
        p_wb = p_wb[0:C + 1, :].rearrange("p (t d) -> p t d", t=12)
        p_xe = p_xp.rearrange("p (h e) w -> p h e w", e=2)
        p_us = p_us.rearrange("p (q j t) -> p q j t", q=2, j=3)
        (dt, duT, z, dA, h, hs, cb, uu, xd, ee, ll, qq, du, dud, ys) = lay(0, [
            2 * KT * T, 2 * TB * KP * 128, 2 * TB * KP * 128, KT * T, 2 * KT * T, 8 * T, 8 * T, 4 * T, T, 2 * T, 2 * T,
            T, KP * T, 2 * (KT - KP) * T, 3 * T])
        dt = dt.rearrange("p (q k t) -> p q k t", q=2, k=KT)
        duT = duT.rearrange("p (q b d) -> p q b d", q=2, b=TB)
        z = z.rearrange("p (q b d) -> p q b d", q=2, b=TB)
        dA = dA.rearrange("p (k t) -> p k t", k=KT)
        h = h.rearrange("p (q k t) -> p q k t", q=2, k=KT)
        hs = hs.rearrange("p (q k t) -> p q k t", q=2, k=4)
        cb = cb.rearrange("p (q j i t) -> p q j i t", q=2, j=2, i=2)
        uu = uu.rearrange("p (j t) -> p j t", j=4)
        ee = ee.rearrange("p (q t) -> p q t", q=2)
        ll = ll.rearrange("p (q t) -> p q t", q=2)
        du = du.rearrange("p (k t) -> p k t", k=KP)
        dud = dud.rearrange("p (q k t) -> p q k t", q=2, k=KT - KP)
        ys = ys.rearrange("p (k t) -> p k t", k=3)
        bt = sb("bt", [128, 2, TB, N])
        (o_in, o_g, o_sq, o_rs, o_n, o_s) = lay(L, [12 * T, 4 * T, 4 * T, 2 * T, 4 * T, 4 * T])
        o_in = o_in.rearrange("p (q i j t) -> p q i j t", q=2, i=3, j=2)
        o_rs = o_rs.rearrange("p (q t) -> p q t", q=2)
        o_g, o_sq, o_n, o_s = (v.rearrange("p (q j t) -> p q j t", q=2, j=2) for v in (o_g, o_sq, o_n, o_s))
        l_a, l_v, l_c, l_sg, l_t, l_h, l_y, l_w, l_ws = lay(L, [L, L, L, 2 * R4, 2 * R4, 2 * RB, 2 * RB, 8 * 128, 8 * 128])
        l_sg, l_t, l_h, l_y = (v.rearrange("p (q t) -> p q t", q=2) for v in (l_sg, l_t, l_h, l_y))
        l_w, l_ws = l_w[0:C, :], l_ws[0:C, :]
        m_f, m_y, m_g, m_p, m_o = lay(L, [8 * 512, 2 * 8 * T, 2 * T, 2 * T, T])
        m_f = m_f.rearrange("p (k m) -> p k m", k=8)
        m_y = m_y.rearrange("p (q k t) -> p q k t", q=2, k=8)
        m_g, m_p = (v.rearrange("p (j t) -> p j t", j=2) for v in (m_g, m_p))
        m_o = m_o[0:C, :]

        bank = [ctx.enter_context(nc.psum_tensor(f"bank{i}", [128, T], F32)) for i in range(8)]
        Y, DB, WB = bank[0:3], bank[3:6], bank[6:8]

        s_w = sem("weights_in")
        s_bar = sem("barrier")
        s_alone = sem("wait_carrier")
        s_set = sem("setup_step")
        s_ms = sem("merge_weight_psum"); s_mc = sem("merge_weight_copied")
        s_xin = sem("image_in")
        s_st = sem("stats_mean"); s_gp = sem("group_psum"); s_gq = sem("group_spread"); s_gs = sem("group_std");
        s_cw = sem("conv_weights_in"); s_wa = sem("conv_weights_ready"); s_wb = sem("conv_row_pair_weights_ready"); s_xp = sem("padded_ready")
        s_cm = sem("conv_psum"); s_us = sem("silu_done"); s_ust = [sem(f"u_stored_{q}") for q in range(2)]
        s_zero = sem("pads_zeroed"); s_edge = sem("edge_in")
        s_u = sem("u_in"); s_ha = sem("h01_added"); s_hb = sem("h23_added"); s_db = sem("dBu_by_vector")
        s_xm = sem("xdbl_psum"); s_xd = sem("xdbl_copied"); s_cst = sem("c_stored")
        s_btp = sem("bT_psum"); s_bt = sem("bT_ready")
        s_dl = sem("delta_psum"); s_abs = sem("abs_done"); s_e = sem("exp_neg_done"); s_ln = sem("ln_done")
        s_q1 = sem("log_rest1"); s_q2 = sem("log_rest"); s_m = sem("softplus_main"); s_dt = sem("dt_ready")
        s_du = sem("du_ready"); s_ct = sem("duT_psum"); s_ev = sem("duT_ready")
        s_z = sem("z_ready"); s_exp = sem("dA_ready"); s_d = sem("dBu_ready")
        s_scan = sem("scanned"); s_hc = sem("hc_ready"); s_ns = sem("n_summed"); s_car = sem("carry_kept")
        s_c0 = sem("carry_zeroed")
        s_cb = [sem(f"c_spread_{q}") for q in range(2)]; s_yev = sem("y_copied"); s_yst = sem("y_stored")
        s_zw = sem("z_weights"); s_p1 = sem("post_skip"); s_pe = sem("post_ln"); s_bzp = sem("z_bias_psum")
        s_pl = [sem(f"post_in_{q}") for q in range(2)]; s_pg = sem("post_sum"); s_pm = sem("post_mean"); s_pz = sem("post_z")
        s_pc = sem("post_centred"); s_pq = sem("post_square"); s_pv = sem("post_var"); s_pr = sem("post_rstd")
        s_pt = sem("post_norm"); s_pa = sem("post_scaled"); s_psi = sem("post_silu"); s_pp = sem("post_gated"); s_po = sem("post_out")
        s_px = sem("x1_ready")
        s_lw = sem("l1_weights_in"); s_lws = sem("l1_weights_scaled"); s_lbp = sem("l1_bias_psum"); s_lb = sem("l1_bias")
        s_lp = sem("l1_psum"); s_ls = sem("l1_gate"); s_lc = sem("l1_c"); s_lt = sem("l1_bgate"); s_lv = sem("l1_v")
        s_lh = sem("l1_scanned"); s_ly = sem("l1_y"); s_lst = [sem(f"l1_stored_{q}") for q in range(2)]; s_l0 = sem("l1_state_zeroed")
        s_mfi = sem("merge_weights_in"); s_ml = [sem(f"merge_in_{q}") for q in range(2)]; s_mp = sem("merge_psum"); s_mg = sem("merge_gate")
        s_mr = sem("merge_prod"); s_mo = sem("merge_out_psum"); s_mx = sem("merge_out"); s_mst = sem("out_stored")

        NW = 22
        NBAR = 5
        OY = 3 * NCH

        def alone(eng):
            eng.sem_inc(s_alone, 1)

        def barrier(eng, index):
            alone(eng)
            eng.drain().then_inc(s_bar, 1)
            eng.wait_ge(s_bar, 5 * (index + 1))
            alone(eng)

        def conv_rhs(r, tap):
            return p_xp[:, bass.ds(r * 4 + tap // 3, 4), tap % 3:tap % 3 + W]

        def backward(v, r):
            return v[:, ::-1][:, r * RB:(r + 1) * RB]

        block = ctx.enter_context(nc.Block())

        @block.sync
        def _(sp):
            loads = [
                (cst[:, :], const), (dps[:, :, :], dp), (aneg[:, :], alog), (wdl[:, :], wdel), (vec[:, :], v192),
                (wz[:, :], win[0:C, D:2 * D]), (wo[0:128, 0, :], wout[0:128, :]), (wo[0:64, 1, :], wout[128:D, :]),
                (b1t[:, :], b1), (bmt[:, :], bm), (owt[:, :, :], ow.rearrange("(k p) c -> p k c", p=128)),
                (obt[:, :], ob), (ybt[:, :], yb),
                (s_wt, wt.rearrange("(k p) m -> p k m", p=128)), (s_yw, yw.rearrange("(k p) m -> p k m", p=128)),
            ]
            for g in range(2):
                for way in range(2):
                    base = (2 * way + g) * D
                    loads.append((wx[0:128, g, 2 * way, :], wxp[base:base + 128, :]))
                    loads.append((wx[0:64, g, 2 * way + 1, :], wxp[base + 128:base + D, :]))
            assert len(loads) == NW + 1
            for ahead in (s_cst, s_yst, *s_ust, *s_lst):
                sp.sem_inc(ahead, 1)
            for to, of in loads:
                sp.dma_start(to, of).then_inc(s_w, 16)
            sp.wait_ge(s_mc, 8)
            sp.dma_start(mf_d, s_mf.rearrange("p k m -> p (k m)")).then_inc(s_set, 16)
            sp.wait_ge(s_set, 16)
            barrier(sp, 0)
            with sp.Fori(0, B) as b:
                sp.dma_start(xr, x[bass.ds(b, 1), :, :].rearrange("o c l -> (o c) l")).then_inc(s_xin, 16)
                sp.dma_start(p_wa, wdw.unsqueeze(0).broadcast_to([C + 1, 9, D])).then_inc(s_cw, 16)
                sp.dma_start(p_wi, win[:, 0:D]).then_inc(s_cw, 16)
                sp.wait_ge(s_zero, b + 1)
                alone(sp)
                sp.dma_start(p_xp[C:C + 1, :, :], inner.rearrange("o (h w) -> o h w", w=PW)).then_inc(s_edge, 16)
                with sp.Fori(0, NR // 4) as r4:
                    for q in range(2):
                        r2 = r4 * 2 + q
                        sp.wait_ge(s_us, 3 * (b * (NR // 2) + r2) + 9)
                        alone(sp)
                        sp.dma_start(u_d[0:128, bass.ds(r2 * 2 * R4, 2 * R4)],
                                     p_us[:, q, 0:2, :].rearrange("p j t -> p (j t)")).then_inc(s_ust[q], 16)
                        rows = u_d[128:D, bass.ds(r2 * 2 * R4, 2 * R4)].rearrange("d (h e w) -> d h e w", e=2, w=W)
                        for odd in range(2):
                            sp.dma_start(rows[:, :, odd, :], p_us[64 * odd:64 * odd + 64, q, 2, :]
                                         .rearrange("p (h w) -> p h w", w=W)).then_inc(s_ust[q], 16)
                for q in range(2):
                    sp.wait_ge(s_ust[q], (b + 1) * (NR // 4) * 48 + 1)
                    alone(sp)
                barrier(sp, b * NBAR + 1)

                def load_u(c, m):
                    sp.wait_ge(s_du, KT * m + 1)
                    alone(sp)
                    fwd, bwd = bass.ds(c * T, T), bass.ds(L - T - c * T, T)
                    sp.dma_start(uu[:, 0, :], u_d[0:128, fwd]).then_inc(s_u, 16)
                    sp.dma_start(uu[0:64, 1, :], u_d[128:D, fwd]).then_inc(s_u, 16)
                    sp.dma_start(uu[64:128, 1, :], u_d[128:D, fwd]).then_inc(s_u, 16)
                    sp.dma_start(uu[:, 2, :], u_d[0:128, bwd]).then_inc(s_u, 16)
                    sp.dma_start(uu[0:64, 3, :], u_d[128:D, bwd]).then_inc(s_u, 16)
                    sp.dma_start(uu[64:128, 3, :], u_d[128:D, bwd]).then_inc(s_u, 16)

                def store_c(m, q):
                    sp.wait_ge(s_xd, m + 1)
                    alone(sp)
                    sp.dma_start(bc_d[q, :, 0, :], xd[B0:B0 + N, :]).then_inc(s_cst, 16)
                    sp.dma_start(bc_d[q, :, 1, :], xd[C0:C0 + N, :]).then_inc(s_cst, 16)

                def store_y(c, m):
                    fwd, bwd = bass.ds(c * T, T), bass.ds(L - T - c * T, T)
                    sp.wait_ge(s_yev, 4 * (m + 1) + 1)
                    alone(sp)
                    sp.dma_start(yf_d[0:128, fwd], ys[:, 0, :]).then_inc(s_yst, 16)
                    sp.dma_start(yb_d[0:128, bwd], ys[:, 1, :]).then_inc(s_yst, 16)
                    sp.dma_start(yf_d[128:D, fwd], ys[0:64, 2, :]).then_inc(s_yst, 16)
                    sp.dma_start(yb_d[128:D, bwd], ys[64:128, 2, :]).then_inc(s_yst, 16)

                def spread_c(m, q, first, last):
                    alone(sp)
                    with sp.Fori(first, last) as p2:
                        for par in range(2):
                            p = p2 * 2 + par
                            pair = m * (N // 2) + p
                            sp.wait_ge(s_hc, 6 * pair + 1)
                            alone(sp)
                            sp.wait_ge(s_db, 4 * pair + 1)
                            alone(sp)
                            sp.dma_start(cb[:, par, :, :, :], bc_d[q, bass.ds(p * 2, 2), :, :].unsqueeze(0)
                                         .broadcast_to([128, 2, 2, T])).then_inc(s_cb[par], 16)

                def chunk(c, q, first, last):
                    m = b * NCH + c
                    sp.wait_ge(s_cst, 32 * (m + 1) + 1)
                    alone(sp)
                    spread_c(m, q, 0, 1)
                    if not last:
                        load_u(c + 1, m + 1)
                    if not first:
                        store_y(c - 1, m - 1)
                    spread_c(m, q, 1, 2)
                    if not last:
                        store_c(m + 1, 1 - q)
                    spread_c(m, q, 2, 4)

                load_u(0, b * NCH)
                store_c(b * NCH, 0)
                chunk(0, 0, True, False)
                with sp.Fori(0, (NCH - 2) // 2) as cp:
                    chunk(cp * 2 + 1, 1, False, False)
                    chunk(cp * 2 + 2, 0, False, False)
                chunk(NCH - 1, 1, False, True)
                store_y(NCH - 1, b * NCH + NCH - 1)
                sp.wait_ge(s_yst, (b + 1) * NCH * 64 + 1)
                alone(sp)
                barrier(sp, b * NBAR + 2)

                sp.dma_start(xr, x[bass.ds(b, 1), :, :].rearrange("o c l -> (o c) l")).then_inc(s_xin, 16)
                with sp.Fori(0, NCH // 2) as c2:
                    for q in range(2):
                        at = bass.ds((c2 * 2 + q) * T, T)
                        sp.wait_ge(s_pg, 2 * (b * NCH + c2 * 2 + q) + 2)
                        alone(sp)
                        for i, of in enumerate((u_d, yf_d, yb_d)):
                            sp.dma_start(o_in[:, q, i, 0, :], of[0:128, at]).then_inc(s_pl[q], 16)
                            sp.dma_start(o_in[0:64, q, i, 1, :], of[128:D, at]).then_inc(s_pl[q], 16)
                barrier(sp, b * NBAR + 3)

                sp.dma_start(l_w, w1).then_inc(s_lw, 16)
                for o in range(NPASS):
                    order, ct = o // 2, o % 2
                    for back, n_, len_ in ((0, NR, R4), (1, NB, RB)):
                        with sp.Fori(0, n_ // 2) as r2:
                            for q in range(2):
                                r = r2 * 2 + q
                                i = (b * NPASS + o) * PB + back * NR + r
                                sp.wait_ge(s_ly, i + 3)
                                alone(sp)
                                sp.dma_start(yc_d[order + 2 * back, ct * 128:ct * 128 + 128, bass.ds(r * len_, len_)],
                                             l_y[:, q, 0:len_]).then_inc(s_lst[q], 16)
                for q in range(2):
                    sp.wait_ge(s_lst[q], (b + 1) * NPASS * PB * 8 + 1)
                    alone(sp)
                alone(sp)
                barrier(sp, b * NBAR + 4)

                sp.dma_start(m_f.rearrange("p k m -> p (k m)"), mf_d).then_inc(s_mfi, 16)
                with sp.Fori(0, NCH // 2) as c2:
                    for q in range(2):
                        c = c2 * 2 + q
                        m = b * NCH + c
                        sp.wait_ge(s_mp, 4 * (m + 1))
                        alone(sp)
                        sp.dma_start(m_y[:, q, :, :], yc_d.rearrange("d (k p) l -> p (d k) l", p=128)[:, :, bass.ds(c * T, T)]) \
                            .then_inc(s_ml[q], 16)
                barrier(sp, b * NBAR + 5)
            sp.wait_ge(s_mst, B * NCH * 16 + 1)
            alone(sp)

        @block.gpsimd
        def _(pool):
            pool.sem_inc(s_pp, 1)
            pool.sem_inc(s_hc, 7)
            pool.sem_inc(s_ly, 2)
            barrier(pool, 0)
            with pool.Fori(0, B) as b:
                pool.memset(p_xp, 0.0).then_inc(s_zero, 1)
                barrier(pool, b * NBAR + 1)

                def times_u(m, q, k):
                    u = (uu[:, 0, :], uu[:, 0, :], uu[:, 2, ::-1], uu[:, 2, ::-1], uu[:, 1, :], uu[:, 3, ::-1])[k]
                    pool.wait_ge(s_dt, m * KT + k + 2)
                    if k == 0:
                        pool.wait_ge(s_ct, KP * m + 1)
                    pool.tensor_tensor(du[:, k, :] if k < KP else dud[:, q, k - KP, :], dt[:, q, k, :], u,
                                       ALU.mult).then_inc(s_du, 1)

                def times_c(g, par, slot):
                    cc = cb[:, slot, par, 1, :]
                    pool.wait_ge(s_ha, g + 3)
                    pool.tensor_tensor(hs[:, par, 0, :], hs[:, par, 0, :], cc, ALU.mult).then_inc(s_hc, 1)
                    pool.wait_ge(s_scan, g * KT + 4 + KT)
                    pool.wait_ge(s_ns, g + 1)
                    pool.tensor_tensor(hs[:, par, 1, :], h[:, par, 2, :], h[:, par, 3, :], ALU.add).then_inc(s_hb, 1)
                    pool.wait_ge(s_hb, g + 1)
                    pool.tensor_tensor(hs[:, par, 1, :], hs[:, par, 1, :], cc, ALU.mult).then_inc(s_hc, 1)
                    pool.wait_ge(s_scan, g * KT + 6 + KT)
                    pool.tensor_tensor(hs[:, par, 2:4, :], h[:, par, 4:6, :], cc.unsqueeze(1).broadcast_to([128, 2, T]),
                                       ALU.mult).then_inc(s_hc, 1)

                def states(c, p4, next_q=None):
                    for r in range(4):
                        slot, j = r // 2, r % 2
                        m = b * NCH + c
                        if j == 0:
                            pool.wait_ge(s_cb[slot], (m * (N // 4) + p4 + 1) * 16)
                        times_c(m * N + p4 * 4 + r, j, slot)
                        if next_q is not None and 0 <= p4 * 4 + r - S_SP < KT:
                            times_u(m + 1, next_q, p4 * 4 + r - S_SP)

                def chunk(c, q):
                    with pool.Fori(0, 1) as p4:
                        states(c, p4)
                    states(c, 1, 1 - q)
                    states(c, 2, 1 - q)
                    with pool.Fori(3, 4) as p4:
                        states(c, p4)

                for k in range(KT):
                    times_u(b * NCH, 0, k)
                with pool.Fori(0, (NCH - 2) // 2) as cp:
                    chunk(cp * 2, 0)
                    chunk(cp * 2 + 1, 1)
                chunk(NCH - 2, 0)
                with pool.Fori(0, N // 4) as p4:
                    states(NCH - 1, p4)
                barrier(pool, b * NBAR + 2)
                with pool.Fori(0, NCH // 2) as c2:
                    for q in range(2):
                        m = (b * (NCH // 2) + c2) * 2 + q
                        pool.wait_ge(s_pa, 2 * (m + 1) + 1)
                        pool.tensor_tensor(o_n[:, q, 0, :], o_n[:, q, 0, :], o_s[:, q, 0, :], ALU.mult).then_inc(s_pp, 1)
                        pool.tensor_tensor(o_n[0:64, q, 1, :], o_n[0:64, q, 1, :], o_s[0:64, q, 1, :], ALU.mult) \
                            .then_inc(s_pp, 1)
                barrier(pool, b * NBAR + 3)
                for o in range(NPASS):
                    def output(i, turns, q, n_, c_):
                        pool.wait_ge(s_lst[q], 16 * turns + 1)
                        pool.wait_ge(s_lh, i + 1 + 1)
                        pool.tensor_tensor(l_y[:, q, 0:n_], l_h[:, q, 0:n_], c_, ALU.mult).then_inc(s_ly, 1)

                    with pool.Fori(0, NR // 2) as r2:
                        for q in range(2):
                            r = r2 * 2 + q
                            pool.wait_ge(s_lc, (b * NPASS + o) * NR + r + 3)
                            output((b * NPASS + o) * PB + r, (b * NPASS + o) * (PB // 2) + r2, q, R4, l_c[:, bass.ds(r * R4, R4)])
                    for r in range(NB):
                        output((b * NPASS + o) * PB + NR + r, (b * NPASS + o) * (PB // 2) + (NR + r) // 2, r % 2, RB, backward(l_c, r))
                barrier(pool, b * NBAR + 4)
                barrier(pool, b * NBAR + 5)

        @block.scalar
        def _(act):
            for ahead in (s_pq, s_pa, s_mst, s_ev, s_pe, s_psi, s_pr):
                act.sem_inc(ahead, 1)
            act.sem_inc(s_us, 6)
            act.sem_inc(s_lc, 2)
            act.sem_inc(s_mg, 2)
            act.wait_ge(s_w, 16 * (NW + 1))
            act.activation(aneg[:, :], aneg[:, :], ACT.Exp).then_inc(s_e, 1)
            barrier(act, 0)
            def group_std(i):
                act.wait_ge(s_gp, 2 * i + 2)
                act.activation(gn[:, 5:6], WB[0][0:C, 1:2], ACT.Sqrt, bias=eps[0:C, :]).then_inc(s_gs, 1)

            with act.Fori(0, B) as b:
                group_std(b * 2)
                with act.Fori(0, NR // 4) as r4:
                    for q in range(2):
                        i = b * (NR // 2) + r4 * 2 + q
                        act.wait_ge(s_ust[q], 48 * (b * (NR // 4) + r4) + 1)
                        for j in range(3):
                            act.wait_ge(s_cm, 3 * i + j + 1)
                            act.activation(p_us[:, q, j, :], bank[3 * q + j][:, 0:R4], ACT.Silu,
                                           bias=vec[:, 6 + j // 2:7 + j // 2]).then_inc(s_us, 1)
                barrier(act, b * NBAR + 1)

                def stage_a(m):
                    act.wait_ge(s_xm, m + 1)
                    act.wait_ge(s_cst, 32 * m + 1)
                    act.copy(xd[0:XC, :], WB[0][0:XC, :]).then_inc(s_xd, 1)

                def copy_bt(m, q):
                    act.wait_ge(s_btp, m + 1)
                    act.copy(bt[:, q, :, :], WB[1][:, 0:TB * N].rearrange("p (b n) -> p b n", b=TB)).then_inc(s_bt, 1)

                def softplus(m, k):
                    i = m * KT + k
                    act.wait_ge(s_dl, i + 1)
                    act.wait_ge(s_dt, (i - 1 if k >= 2 else m * KT) + 1)
                    act.activation(ee[:, k % 2, :], WB[k % 2][:, :], ACT.Abs).then_inc(s_abs, 1)
                    act.wait_ge(s_abs, i + 1)
                    act.activation(ee[:, k % 2, :], ee[:, k % 2, :], ACT.Exp, scale=-1.0).then_inc(s_e, 1)
                    act.wait_ge(s_e, i + 2)
                    act.activation(ll[:, k % 2, :], ee[:, k % 2, :], ACT.Ln, bias=1.0).then_inc(s_ln, 1)

                def stage_c(m, q, ks):
                    for k in ks:
                        act.wait_ge(s_ct, m * KP + k + 2)
                        act.copy(duT[:, q, :, k * 128:(k + 1) * 128], WB[k % 2][:, :].rearrange("p (b d) -> p b d", b=TB)) \
                            .then_inc(s_ev, 1)

                def state(c, q, n, par, piece=None):
                    g = (b * NCH + c) * N + n
                    act.wait_ge(s_d, (g + 1) * KP)
                    for t in range(TB):
                        last_z = act.activation(z[:, par, t, :], duT[:, q, t, :], ACT.Copy, scale=bt[:, q, t, bass.ds(n, 1)])
                    last_z.then_inc(s_z, 1)
                    for k in range(KT):
                        act.wait_ge(s_scan, g * KT + k + 1)
                        act.activation(dA[:, k, :], dt[:, q, k, :], ACT.Exp,
                                       scale=aneg[:, bass.ds(n * KT + k, 1)]).then_inc(s_exp, 1)
                        if k == 2 and piece:
                            softplus(*piece)

                def chunk(c, q, last):
                    m = b * NCH + c
                    act.wait_ge(s_ev, KP * (m + 1) + 1)
                    act.wait_ge(s_bt, m + 1)
                    act.wait_ge(s_dt, KT * (m + 1) + 1)
                    if last:
                        with act.Fori(0, N // 2) as p:
                            for par in range(2):
                                state(c, q, p * 2 + par, par)
                        return
                    with act.Fori(0, 2) as p:
                        for par in range(2):
                            state(c, q, p * 2 + par, par)
                    for n in range(4, N):
                        k = n - S_SP
                        state(c, q, n, n % 2, (m + 1, k) if 0 <= k < KT else None)
                        if n == S_XD:
                            stage_a(m + 1)
                        if n == S_SP - 1:
                            copy_bt(m + 1, 1 - q)
                        if n >= S_EV and 2 * (n - S_EV) < KP:
                            stage_c(m + 1, 1 - q, range(2 * (n - S_EV), 2 * (n - S_EV) + 2))

                act.preload_act_table_set("natural_log_exp_and_others")
                act.wait_ge(s_c0, b + 1)
                stage_a(b * NCH)
                copy_bt(b * NCH, 0)
                for k in range(KT):
                    softplus(b * NCH, k)
                stage_c(b * NCH, 0, range(KP))
                with act.Fori(0, (NCH - 2) // 2) as cp:
                    chunk(cp * 2, 0, False)
                    chunk(cp * 2 + 1, 1, False)
                chunk(NCH - 2, 0, False)
                chunk(NCH - 1, 1, True)
                barrier(act, b * NBAR + 2)

                with act.Fori(0, NCH // 2) as c2:
                    m0 = (b * (NCH // 2) + c2) * 2
                    act.preload_act_table(ACT.Silu)
                    for q in range(2):
                        act.wait_ge(s_pz, m0 + q + 1)
                        act.wait_ge(s_pp, 2 * m0 + 1)
                        for j, rows in ((0, 128), (1, 64)):
                            act.activation(o_s[0:rows, q, j, :], bank[2 * q + j][0:rows, :], ACT.Silu,
                                           bias=bzs[0:rows, j:j + 1]).then_inc(s_psi, 1)
                    act.preload_act_table_set("natural_log_exp_and_others")
                    for q in range(2):
                        act.wait_ge(s_pc, 2 * (m0 + q + 1) + 1)
                        for j, rows in ((0, 128), (1, 64)):
                            act.activation(o_sq[0:rows, q, j, :], o_g[0:rows, q, j, :], ACT.Square).then_inc(s_pq, 1)
                    for q in range(2):
                        act.wait_ge(s_pv, m0 + q + 2)
                        act.activation(o_rs[:, q, :], DB[1 + q][:, :], ACT.Ln, bias=eps).then_inc(s_pe, 1)
                    for q in range(2):
                        act.wait_ge(s_pe, m0 + q + 2)
                        act.activation(o_rs[:, q, :], o_rs[:, q, :], ACT.Exp, scale=-0.5).then_inc(s_pr, 1)
                    for q in range(2):
                        act.wait_ge(s_pt, 2 * (m0 + q + 1) + 1)
                        act.wait_ge(s_po, m0 + 1)
                        for j, rows in ((0, 128), (1, 64)):
                            act.activation(o_n[0:rows, q, j, :], o_g[0:rows, q, j, :], ACT.Identity,
                                           bias=vec[0:rows, 4 + j:5 + j], scale=vec[0:rows, 2 + j:3 + j]).then_inc(s_pa, 1)
                barrier(act, b * NBAR + 3)

                group_std(b * 2 + 1)
                act.wait_ge(s_lb, b + 1)
                for o in range(NPASS):
                    ct = o % 2
                    act.wait_ge(s_lh, (b * NPASS + o) * PB + 1)
                    act.wait_ge(s_ly, (b * NPASS + o) * PB + 2)
                    alone(act)
                    with act.Fori(0, NR // 2) as r2:
                        for q in range(2):
                            r = r2 * 2 + q
                            i = (b * NPASS + o) * NR + r
                            at = bass.ds(r * R4, R4)
                            pb = bank[4 * q:4 * q + 4]
                            act.wait_ge(s_lp, 4 * i + 1)
                            act.activation(l_a[:, at], pb[0][:, 0:R4], ACT.Sigmoid, bias=nb1[:, ct:ct + 1], scale=-1.0)
                            act.wait_ge(s_lt, i + 1)
                            act.activation(l_sg[:, q, :], pb[0][:, 0:R4], ACT.Sigmoid, bias=b1s[:, ct:ct + 1]) \
                                .then_inc(s_ls, 1)
                            act.wait_ge(s_lp, 4 * i + 4)
                            act.activation(l_c[:, at], pb[3][:, 0:R4], ACT.Identity, bias=b1s[:, 6 + ct:7 + ct]) \
                                .then_inc(s_lc, 1)
                barrier(act, b * NBAR + 4)
                def gates(m):
                    for j in range(2):
                        act.wait_ge(s_mp, 8 + 4 * m + 2 * j + 1)
                        act.wait_ge(s_mr, 2 * m + j + 1)
                        act.activation(m_g[:, j, :], bank[2 * j][:, :], ACT.Sigmoid, bias=bmf[:, 2 + j:3 + j]) \
                            .then_inc(s_mg, 1)

                def store(m, c):
                    act.wait_ge(s_mx, m + 1 + 1)
                    act.dma_start(out[bass.ds(b, 1), :, bass.ds(c * T, T)].rearrange("o c l -> (o c) l"), m_o) \
                        .then_inc(s_mst, 16)

                gates(b * NCH)
                with act.Fori(1, NCH) as c:
                    gates(b * NCH + c)
                    store(b * NCH + c - 1, c - 1)
                store(b * NCH + NCH - 1, NCH - 1)
                act.wait_ge(s_mst, (b + 1) * NCH * 16 + 1)
                barrier(act, b * NBAR + 5)

        @block.vector
        def _(dve):
            for ahead in (s_du, s_dt, s_pt, s_lh, s_yev, s_pc, s_mx, s_px):
                dve.sem_inc(ahead, 1)
            dve.sem_inc(s_scan, KT)
            dve.sem_inc(s_car, N)
            dve.sem_inc(s_pg, 4)
            dve.sem_inc(s_ha, 2)
            dve.sem_inc(s_db, 5)
            dve.sem_inc(s_lt, 2)
            dve.sem_inc(s_lv, 2)
            dve.sem_inc(s_mr, 2)
            dve.wait_ge(s_w, 16 * (NW + 1))
            dve.tensor_tensor(wx[:, 0, 0:4:2, :], wx[:, 0, 0:4:2, :], wx[:, 1, 0:4:2, :], ALU.add)
            dve.tensor_tensor(wx[0:64, 0, 1:4:2, :], wx[0:64, 0, 1:4:2, :], wx[0:64, 1, 1:4:2, :], ALU.add)
            dve.tensor_tensor(dps[:, :, 0:2], dps[:, :, 0:2], dps[:, :, 2:4], ALU.add)
            dve.drain()
            dve.tensor_tensor(dsum[:, :], dps[:, :, 0], dps[:, :, 1], ALU.add)
            dve.wait_ge(s_e, 1)
            dve.tensor_scalar(aneg[:, :], aneg[:, :], -1.0, None, ALU.mult)
            for i in range(8):
                dve.wait_ge(s_ms, i + 1)
                dve.tensor_copy(s_mf[:, i, :], bank[i][:, :]).then_inc(s_mc, 1)
            dve.wait_ge(s_ms, 9)
            dve.tensor_tensor(bmf[:, :], bank[0][:, 0:4], bmt[:, :], ALU.add)
            barrier(dve, 0)

            def group_norm(i):
                dve.drain()
                dve.bn_aggr(mv[:, :], bnst[:, :]).then_inc(s_st, 1)
                dve.wait_ge(s_gp, 2 * i + 1)
                dve.tensor_copy(gn[:, 0:1], WB[0][0:C, 0:1])
                dve.drain()
                dve.tensor_tensor(gn[:, 1:2], mv[:, 0:1], gn[:, 0:1], ALU.subtract)
                dve.drain()
                dve.scalar_tensor_tensor(gn[:, 2:3], gn[:, 1:2], gn[:, 1:2], mv[:, 1:2], ALU.mult, ALU.add) \
                    .then_inc(s_gq, 1)
                dve.wait_ge(s_gs, i + 1)
                dve.reciprocal(gn[:, 3:4], gn[:, 5:6])
                dve.drain()
                dve.scalar_tensor_tensor(gn[:, 4:5], gn[:, 0:1], -1.0, gn[:, 3:4], ALU.mult, ALU.mult)
                dve.drain()

            with dve.Fori(0, B) as b:
                dve.wait_ge(s_xin, 32 * b + 16)
                for c in range(NCH):
                    dve.bn_stats(bnst[:, 6 * c:6 * c + 6], xr[:, c * T:(c + 1) * T])
                group_norm(b * 2)
                dve.tensor_scalar(wzs[:, :], wz[:, :], gn[:, 3:4], None, ALU.mult).then_inc(s_zw, 1)
                dve.wait_ge(s_bzp, b + 1)
                dve.tensor_tensor(bzs[:, 0:1], WB[1][:, 0:1], vec[:, 0:1], ALU.add)
                dve.tensor_tensor(bzs[0:64, 1:2], WB[1][0:64, 1:2], vec[0:64, 1:2], ALU.add)
                dve.wait_ge(s_cw, 32 * (b + 1))
                dve.tensor_tensor(p_wa, p_wa, p_wi.unsqueeze(1).broadcast_to([C + 1, 9, D]), ALU.mult).then_inc(s_wa, 1)
                dve.memset(p_wb[:, 9:12, 0:64], 0.0).then_inc(s_wb, 1)
                dve.memset(p_wb[:, 0:3, 64:128], 0.0).then_inc(s_wb, 1)
                dve.wait_ge(s_wa, b + 1)
                dve.tensor_copy(p_wb[:, 0:9, 0:64], p_wa[:, :, 128:D]).then_inc(s_wb, 1)
                dve.tensor_copy(p_wb[:, 3:12, 64:128], p_wa[:, :, 128:D]).then_inc(s_wb, 1)
                dve.wait_ge(s_zero, b + 1)
                dve.tensor_scalar(p_xp[0:C, 1:H + 1, 1:W + 1], xr.rearrange("c (h w) -> c h w", w=W), gn[:, 3:4],
                                  gn[:, 4:5], ALU.mult, ALU.add).then_inc(s_xp, 1)
                barrier(dve, b * NBAR + 1)

                dve.memset(xd[64:96, :], 0.0)
                dve.memset(xd[96:97, :], 1.0)
                dve.memset(carry[:, :, :], 0.0).then_inc(s_c0, 1)
                dve.wait_ge(s_c0, b + 1)

                def softplus(m, q, k):
                    i = m * KT + k
                    dve.wait_ge(s_e, i + 2)
                    dve.wait_ge(s_dt, i + 1)
                    dve.tensor_scalar(qq, ee[:, k % 2, :], 1.0, -1.0, ALU.add, ALU.add).then_inc(s_q1, 1)
                    dve.wait_ge(s_q1, i + 1)
                    dve.tensor_tensor(qq, ee[:, k % 2, :], qq, ALU.subtract).then_inc(s_q2, 1)
                    dve.wait_ge(s_ln, i + 1)
                    dve.scalar_tensor_tensor(ll[:, k % 2, :], WB[k % 2][:, :], 0.0, ll[:, k % 2, :], ALU.max, ALU.add) \
                        .then_inc(s_m, 1)
                    dve.wait_ge(s_q2, i + 1)
                    dve.wait_ge(s_m, i + 1)
                    dve.tensor_tensor(dt[:, q, k, :], ll[:, k % 2, :], qq, ALU.add).then_inc(s_dt, 1)

                def scans(c, q, p4, r):
                    n, par, slot = p4 * 4 + r, r % 2, r // 2
                    g = (b * NCH + c) * N + n

                    def times_b(k):
                        i = k - KP
                        dve.wait_ge(s_scan, (g + 1) * KT + k - 2)
                        dve.tensor_tensor(DB[k % 3][:, :], dud[:, q, i, :], cb[:, slot, par, 0, :], ALU.mult) \
                            .then_inc(s_db, 1)

                    def scan(k):
                        if k == 0:
                            dve.wait_ge(s_ha, g + 1)
                        elif k % 2 == 0:
                            dve.wait_ge(s_hc, 3 * g + 2 + k // 2)
                        dve.wait_ge(s_exp, g * KT + k + 1)
                        if k < KP:
                            dve.wait_ge(s_d, (g + 2) * KP + k + 1)
                        else:
                            dve.wait_ge(s_db, g * (KT - KP) + k - KP + 6)
                        dve.tensor_tensor_scan(h[:, par, k, :], dA[:, k, :], DB[k % 3][:, :],
                                               carry[:, bass.ds(n, 1), k], ALU.mult, ALU.add).then_inc(s_scan, 1)

                    dve.wait_ge(s_car, g + 1)
                    scan(0)
                    scan(1)
                    scan(2)
                    if par == 0:
                        dve.wait_ge(s_cb[slot], ((b * NCH + c) * (N // 4) + p4 + 1) * 16)
                    times_b(4)
                    dve.wait_ge(s_ns, g + 1)
                    dve.wait_ge(s_scan, g * KT + 2 + KT)
                    dve.tensor_tensor(hs[:, par, 0, :], h[:, par, 0, :], h[:, par, 1, :], ALU.add).then_inc(s_ha, 1)
                    times_b(5)
                    scan(3)
                    scan(4)
                    scan(5)
                    dve.wait_ge(s_scan, (g + 2) * KT)
                    alone(dve)
                    dve.tensor_copy(carry[:, bass.ds(n, 1), :].rearrange("p o k -> p (o k)"),
                                    h[:, par, :, T - 1]).then_inc(s_car, 1)

                def copy_y(m):
                    dve.wait_ge(s_ns, N * (m + 1) + 2)
                    dve.wait_ge(s_yst, 64 * m + 1)
                    dve.tensor_copy(ys[:, 0, :], Y[0][:, :]).then_inc(s_yev, 1)
                    dve.tensor_copy(ys[:, 1, ::-1], Y[1][:, :]).then_inc(s_yev, 1)
                    dve.tensor_copy(ys[0:64, 2, :], Y[2][0:64, :]).then_inc(s_yev, 1)
                    dve.tensor_copy(ys[64:128, 2, ::-1], Y[2][64:128, :]).then_inc(s_yev, 1)

                def chunk(c, q, first, last):
                    m = b * NCH + c
                    dve.wait_ge(s_du, KT * (m + 1) + 1)
                    scans(c, q, 0, 0)
                    if not first:
                        copy_y(m - 1)
                    if last:
                        for r in range(1, 4):
                            scans(c, q, 0, r)
                        with dve.Fori(1, 4) as p4:
                            for r in range(4):
                                scans(c, q, p4, r)
                        return
                    for n in range(1, 12):
                        scans(c, q, n // 4, n % 4)
                        if 0 <= n - S_SP < KT:
                            softplus(m + 1, 1 - q, n - S_SP)
                    with dve.Fori(3, 4) as p4:
                        for r in range(4):
                            scans(c, q, p4, r)

                for k in range(KT):
                    softplus(b * NCH, 0, k)
                chunk(0, 0, True, False)
                with dve.Fori(0, (NCH - 2) // 2) as cp:
                    chunk(cp * 2 + 1, 1, False, False)
                    chunk(cp * 2 + 2, 0, False, False)
                chunk(NCH - 1, 1, False, True)
                copy_y(b * NCH + NCH - 1)
                barrier(dve, b * NBAR + 2)

                dve.wait_ge(s_xin, 32 * b + 32)
                alone(dve)
                with dve.Fori(0, NCH // 2) as c2:
                    m0 = b * NCH + c2 * 2
                    both = ((0, 128), (1, 64))
                    for q in range(2):
                        dve.wait_ge(s_pl[q], 96 * (b * (NCH // 2) + c2 + 1))
                        dve.wait_ge(s_pa, 2 * m0 + 1)
                        for j, n_ in both:
                            dve.scalar_tensor_tensor(o_g[0:n_, q, j, :], o_in[0:n_, q, 0, j, :], dsum[0:n_, j:j + 1],
                                                     o_in[0:n_, q, 1, j, :], ALU.mult, ALU.add).then_inc(s_p1, 1)
                    for q in range(2):
                        dve.wait_ge(s_p1, 2 * (m0 + q + 1))
                        for j, n_ in both:
                            dve.tensor_tensor(o_g[0:n_, q, j, :], o_g[0:n_, q, j, :], o_in[0:n_, q, 2, j, :], ALU.add) \
                                .then_inc(s_pg, 1)
                    for q in range(2):
                        dve.wait_ge(s_pm, m0 + q + 1)
                        dve.wait_ge(s_pg, 2 * (m0 + q + 1) + 4)
                        for j, n_ in both:
                            dve.tensor_tensor(o_g[0:n_, q, j, :], o_g[0:n_, q, j, :], DB[1 + q][0:n_, :], ALU.subtract) \
                                .then_inc(s_pc, 1)
                    for q in range(2):
                        dve.wait_ge(s_pr, m0 + q + 2)
                        for j, n_ in both:
                            dve.tensor_tensor(o_g[0:n_, q, j, :], o_g[0:n_, q, j, :], o_rs[0:n_, q, :], ALU.mult) \
                                .then_inc(s_pt, 1)
                    for q in range(2):
                        c = c2 * 2 + q
                        at = bass.ds(c * T, T)
                        dve.wait_ge(s_po, m0 + q + 2)
                        dve.tensor_tensor(xr[:, at], WB[q][0:C, :], xr[:, at], ALU.add).then_inc(s_px, 1)
                        dve.wait_ge(s_px, m0 + q + 2)
                        dve.bn_stats(bnst[:, bass.ds(c * 6, 6)], xr[:, at])
                barrier(dve, b * NBAR + 3)

                group_norm(b * 2 + 1)
                dve.wait_ge(s_lw, 16 * (b + 1))
                dve.tensor_scalar(l_ws, l_w, gn[:, 3:4], None, ALU.mult).then_inc(s_lws, 1)
                dve.wait_ge(s_lbp, b + 1)
                dve.tensor_tensor(b1s[:, :], WB[1][:, 0:8], b1t[:, :], ALU.add)
                dve.drain()
                dve.tensor_scalar(nb1[:, :], b1s[:, 0:2], -1.0, None, ALU.mult).then_inc(s_lb, 1)
                for o in range(NPASS):
                    ct = o % 2

                    def zero_state(base, n_, count):
                        dve.wait_ge(s_ly, base + 2)
                        dve.memset(l_h[:, 1, n_ - 1:n_], 0.0).then_inc(s_l0, 1)
                        dve.wait_ge(s_l0, count)
                        alone(dve)

                    def scan(i, q, n_, a_, v_):
                        dve.wait_ge(s_lh, i + 1)
                        dve.wait_ge(s_ly, i + 1)
                        dve.tensor_tensor_scan(l_h[:, q, 0:n_], a_, v_, l_h[:, 1 - q, n_ - 1:n_],
                                               ALU.mult, ALU.add).then_inc(s_lh, 1)

                    base = (b * NPASS + o) * PB
                    zero_state(base, R4, (b * NPASS + o) * 2 + 1)
                    with dve.Fori(0, NR // 2) as r2:
                        for q in range(2):
                            r = r2 * 2 + q
                            i = (b * NPASS + o) * NR + r
                            at = bass.ds(r * R4, R4)
                            pb = bank[4 * q:4 * q + 4]
                            dve.wait_ge(s_ls, i + 1)
                            dve.wait_ge(s_lp, 4 * i + 2)
                            dve.scalar_tensor_tensor(l_t[:, q, :], pb[1][:, 0:R4], b1s[:, 4 + ct:5 + ct],
                                                     l_sg[:, q, :], ALU.add, ALU.mult).then_inc(s_lt, 1)
                            dve.wait_ge(s_lt, i + 3)
                            dve.wait_ge(s_lp, 4 * i + 3)
                            dve.scalar_tensor_tensor(l_v[:, at], pb[2][:, 0:R4], b1s[:, 2 + ct:3 + ct],
                                                     l_t[:, q, :], ALU.add, ALU.mult).then_inc(s_lv, 1)
                            dve.wait_ge(s_lv, i + 3)
                            scan(base + r, q, R4, l_a[:, at], l_v[:, at])
                    zero_state(base + NR, RB, (b * NPASS + o) * 2 + 2)
                    for r in range(NB):
                        scan(base + NR + r, r % 2, RB, backward(l_a, r), backward(l_v, r))
                barrier(dve, b * NBAR + 4)
                def close(m, c):
                    dve.wait_ge(s_mo, m + 1)
                    dve.wait_ge(s_mst, 16 * m + 1)
                    dve.scalar_tensor_tensor(m_o, bank[4][0:C, :], obt[:, 0:1], xr[:, bass.ds(c * T, T)],
                                             ALU.add, ALU.add).then_inc(s_mx, 1)

                def products(m):
                    for j in range(2):
                        dve.wait_ge(s_mg, 2 * m + j + 3)
                        dve.wait_ge(s_mp, 8 + 4 * m + 2 * j + 2)
                        dve.scalar_tensor_tensor(m_p[:, j, :], bank[2 * j + 1][:, :], bmf[:, j:j + 1], m_g[:, j, :],
                                                 ALU.add, ALU.mult).then_inc(s_mr, 1)

                products(b * NCH)
                with dve.Fori(1, NCH) as c:
                    close(b * NCH + c - 1, c - 1)
                    products(b * NCH + c)
                close(b * NCH + NCH - 1, NCH - 1)
                barrier(dve, b * NBAR + 5)

        @block.tensor
        def _(pe):
            for ahead in (s_po, s_pv, s_ct):
                pe.sem_inc(ahead, 1)
            pe.sem_inc(s_d, 2 * KP)
            pe.sem_inc(s_ns, 2)
            pe.sem_inc(s_mp, 8)
            pe.wait_ge(s_w, 16 * (NW + 1))
            for d in range(4):
                for ct in range(2):
                    for j in range(2):
                        mm = pe.matmul(bank[2 * d + ct][:, :], s_yw[:, j, ct * 128:ct * 128 + 128], s_wt[:, 2 * d + j, :],
                                       start=(j == 0), stop=(j == 1))
                    mm.then_inc(s_ms, 1)
            pe.wait_ge(s_mc, 8)
            for i in range(4):
                for k in range(8):
                    mm = pe.matmul(bank[0][:, i:i + 1], s_wt[:, k, i * 128:i * 128 + 128], ybt[:, k % 2:k % 2 + 1],
                                   start=(k == 0), stop=(k == 7))
            mm.then_inc(s_ms, 1)
            barrier(pe, 0)

            def group_norm(i):
                pe.wait_ge(s_st, i + 1)
                pe.matmul(WB[0][0:C, 0:1], gmask, mv[:, 0:1], start=True, stop=True).then_inc(s_gp, 1)
                pe.wait_ge(s_gq, i + 1)
                pe.matmul(WB[0][0:C, 1:2], gmask, gn[:, 2:3], start=True, stop=True).then_inc(s_gp, 1)

            with pe.Fori(0, B) as b:
                group_norm(b * 2)
                pe.wait_ge(s_zw, b + 1)
                pe.matmul(WB[1][:, 0:1], wz[:, 0:128], gn[:, 4:5], start=True, stop=True)
                pe.matmul(WB[1][0:64, 1:2], wz[:, 128:D], gn[:, 4:5], start=True, stop=True).then_inc(s_bzp, 1)
                pe.wait_ge(s_wb, 4 * (b + 1))
                pe.wait_ge(s_edge, 16 * (b + 1))
                pe.wait_ge(s_xp, b + 1)
                alone(pe)
                with pe.Fori(0, NR // 4) as r4:
                    for q in range(2):
                        r2 = r4 * 2 + q
                        pe.wait_ge(s_us, 3 * (b * (NR // 2) + r2) + 3)
                        for j in range(2):
                            for tap in range(9):
                                mm = pe.matmul(bank[3 * q + j][:, 0:R4], p_wa[:, tap, 0:128], conv_rhs(r2 * 2 + j, tap),
                                               start=(tap == 0), stop=(tap == 8))
                            mm.then_inc(s_cm, 1)
                        for tap in range(12):
                            row, col = tap // 3, tap % 3
                            mm = pe.matmul(bank[3 * q + 2][:, 0:R4], p_wb[:, tap, :],
                                           p_xe[:, bass.ds(r2 * 4 + row // 2, 4), row % 2, col:col + W],
                                           start=(tap == 0), stop=(tap == 11))
                        mm.then_inc(s_cm, 1)
                barrier(pe, b * NBAR + 1)

                def stage_a(m):
                    pe.wait_ge(s_u, 96 * (m + 1))
                    pe.wait_ge(s_ev, KP * m + 1)
                    o = WB[0][0:XC, :]
                    pe.matmul(o, wx[:, 0, 0, :], uu[:, 0, :], start=True, stop=False)
                    pe.matmul(o, wx[0:64, 0, 1, :], uu[0:64, 1, :], start=False, stop=False)
                    pe.matmul(o, wx[:, 0, 2, :], uu[:, 2, ::-1], start=False, stop=False)
                    pe.matmul(o, wx[0:64, 0, 3, :], uu[0:64, 3, ::-1], start=False, stop=True).then_inc(s_xm, 1)

                def turn_b(m):
                    pe.wait_ge(s_xd, m + 1)
                    alone(pe)
                    for t in range(TB):
                        mm = pe.transpose(WB[1][:, t * N:(t + 1) * N], xd[B0:B0 + N, t * 128:(t + 1) * 128],
                                          cst[B0:B0 + N, K_ID + B0:K_ID + B0 + N])
                    mm.then_inc(s_btp, 1)

                def delta(m, k):
                    i = m * KT + k
                    if k == 1:
                        pe.wait_ge(s_bt, m + 1)
                    if k >= 2:
                        pe.wait_ge(s_m, i - 1)
                    pe.matmul(WB[k % 2][:, :], wdl[:, k * 128:(k + 1) * 128], xd[0:97, :], start=True, stop=True) \
                        .then_inc(s_dl, 1)

                def stage_c(m, ks):
                    pe.wait_ge(s_m, KT * (m + 1))
                    for k in ks:
                        pe.wait_ge(s_du, KT * m + k + 2)
                        if k >= 2:
                            pe.wait_ge(s_ev, m * KP + k)
                        for t in range(TB):
                            mm = pe.transpose(WB[k % 2][:, t * 128:(t + 1) * 128], du[:, k, t * 128:(t + 1) * 128], ident)
                        mm.then_inc(s_ct, 1)

                def turn(g, par):
                    pe.wait_ge(s_z, g + 1)
                    for k in range(KP):
                        pe.wait_ge(s_scan, g * KT + k + 4)
                        for t in range(TB):
                            mm = pe.transpose(DB[k % 3][:, t * 128:(t + 1) * 128], z[:, par, t, k * 128:(k + 1) * 128], ident)
                        mm.then_inc(s_d, 1)

                def state_sum(g, par, m_first=None):
                    first = m_first is not None
                    if first:
                        pe.wait_ge(s_yev, 4 * m_first + 1)
                    for k in range(4):
                        if k < 3:
                            pe.wait_ge(s_hc, 3 * g + k + 8)
                        to, w = (Y[k][:, :], ident) if k < 2 else (Y[2][64 * (k - 2):64 * (k - 1), :], sel)
                        mm = pe.matmul(to, w, hs[:, par, k, :], start=first, stop=True, skip_group_check=True)
                    mm.then_inc(s_ns, 1)

                def chunk(c, last):
                    m = b * NCH + c
                    g0 = m * N

                    def pair(j):
                        turn(g0 + j * 2, 0)
                        state_sum(g0 + j * 2 - 1, 1)
                        turn(g0 + j * 2 + 1, 1)
                        state_sum(g0 + j * 2, 0)

                    turn(g0 + 1, 1)
                    state_sum(g0, 0, m)
                    if last:
                        with pe.Fori(1, N // 2) as j:
                            pair(j)
                    for n in range(1, N - 1 if not last else 1):
                        turn(g0 + n + 1, (n + 1) % 2)
                        state_sum(g0 + n, n % 2)
                        if n == S_XA:
                            stage_a(m + 1)
                        if n == S_DL:
                            turn_b(m + 1)
                        if 0 <= n - S_DL < KT:
                            delta(m + 1, n - S_DL)
                        if n >= S_CT and 2 * (n - S_CT) < KP:
                            stage_c(m + 1, range(2 * (n - S_CT), 2 * (n - S_CT) + 2))
                    if not last:
                        turn(g0 + N, 0)
                    state_sum(g0 + N - 1, 1)

                stage_a(b * NCH)
                turn_b(b * NCH)
                for k in range(KT):
                    delta(b * NCH, k)
                stage_c(b * NCH, range(KP))
                turn(b * NCH * N, 0)
                with pe.Fori(0, NCH - 1) as c:
                    chunk(c, False)
                chunk(NCH - 1, True)
                barrier(pe, b * NBAR + 2)

                pe.wait_ge(s_xin, 32 * b + 32)
                alone(pe)
                with pe.Fori(0, NCH // 2) as c2:
                    m0 = b * NCH + c2 * 2

                    def both(to, w, v, last):
                        pe.matmul(to, w[0], v[:, 0, :], start=True, stop=False)
                        pe.matmul(to, w[1], v[0:64, 1, :], start=False, stop=True).then_inc(last, 1)

                    for q in range(2):
                        at = bass.ds((c2 * 2 + q) * T, T)
                        pe.wait_ge(s_psi, 2 * m0 + 1)
                        pe.matmul(bank[2 * q][:, :], wzs[:, 0:128], xr[:, at], start=True, stop=True)
                        pe.matmul(bank[2 * q + 1][0:64, :], wzs[:, 128:D], xr[:, at], start=True, stop=True) \
                            .then_inc(s_pz, 1)
                    for q in range(2):
                        pe.wait_ge(s_pg, 2 * (m0 + q + 1) + 4)
                        pe.wait_ge(s_pe, m0 + 1)
                        both(DB[1 + q][:, :], (mean192, mean192[0:64, :]), o_g[:, q, :, :], s_pm)
                    for q in range(2):
                        pe.wait_ge(s_pq, 2 * (m0 + q + 1) + 1)
                        both(DB[1 + q][:, :], (mean192, mean192[0:64, :]), o_sq[:, q, :, :], s_pv)
                    for q in range(2):
                        pe.wait_ge(s_pp, 2 * (m0 + q + 1) + 1)
                        pe.wait_ge(s_px, m0 + 1)
                        both(WB[q][0:C, :], (wo[:, 0, :], wo[0:64, 1, :]), o_n[:, q, :, :], s_po)
                barrier(pe, b * NBAR + 3)

                group_norm(b * 2 + 1)
                pe.wait_ge(s_lws, b + 1)
                for j in range(8):
                    mm = pe.matmul(WB[1][:, j:j + 1], l_w[:, j * 128:(j + 1) * 128], gn[:, 4:5], start=True, stop=True)
                mm.then_inc(s_lbp, 1)
                pe.wait_ge(s_lb, b + 1)
                alone(pe)
                for o in range(NPASS):
                    order, ct = o // 2, o % 2
                    xv = xr.rearrange("c (h w) -> c h w", w=W)
                    if order:
                        xv = xv.rearrange("c h w -> c w h")
                    with pe.Fori(0, NR // 2) as r2:
                        for q in range(2):
                            r = r2 * 2 + q
                            i = (b * NPASS + o) * NR + r
                            pe.wait_ge(s_lc, i + 1)
                            pe.wait_ge(s_lv, i + 1)
                            for j in range(4):
                                w = 2 * (0, 2, 1, 3)[j] + ct
                                pe.matmul(bank[4 * q + j][:, 0:R4], l_ws[:, w * 128:(w + 1) * 128],
                                          xv[:, bass.ds(r * 4, 4), :], start=True, stop=True).then_inc(s_lp, 1)
                barrier(pe, b * NBAR + 4)

                def mix(m, turns, q, j):
                    pe.wait_ge(s_ml[q], 16 * turns)
                    pe.wait_ge(s_mr if j % 2 else s_mg, 2 * m + j // 2 + 1)
                    col = (LAT if j % 2 == 0 else 0) + (j // 2) * 128
                    for k in range(8):
                        mm = pe.matmul(bank[j][:, :], m_f[:, k, col:col + 128], m_y[:, q, k, :], start=(k == 0), stop=(k == 7))
                    mm.then_inc(s_mp, 1)

                def project(m):
                    pe.wait_ge(s_mr, 2 * m + 4)
                    pe.wait_ge(s_mx, m + 1)
                    for j in range(2):
                        mm = pe.matmul(bank[4][0:C, :], owt[:, j, :], m_p[:, j, :], start=(j == 0), stop=(j == 1))
                    mm.then_inc(s_mo, 1)

                def merge_chunk(m, turns, q, first):
                    mix(m, turns, q, 0)
                    if not first:
                        project(m - 1)
                    for j in range(1, 4):
                        mix(m, turns, q, j)

                pe.wait_ge(s_mfi, 16 * (b + 1))
                turns = b * (NCH // 2) + 1
                merge_chunk(b * NCH, turns, 0, True)
                with pe.Fori(0, (NCH - 2) // 2) as c2:
                    merge_chunk(b * NCH + c2 * 2 + 1, turns + c2, 1, False)
                    merge_chunk(b * NCH + c2 * 2 + 2, turns + c2 + 1, 0, False)
                merge_chunk(b * NCH + NCH - 1, turns + NCH // 2 - 1, 1, False)
                project(b * NCH + NCH - 1)
                barrier(pe, b * NBAR + 5)


def kernel(**inputs):
    import numpy as np
    import concourse.bacc as bacc
    from concourse import mybir as _mybir
    from concourse.bass_utils import run_bass_kernel_spmd

    v = {k: np.asarray(a) for k, a in inputs.items()}
    f = np.float32

    def tiles(a, n):
        out = np.zeros((n * 128,), f)
        out[:a.shape[0]] = a
        return out.reshape(n, 128).T

    order = [g * D + c for g in range(4) for c in range(128)]
    order += [g * D + 128 + c for g in range(4) for c in range(64)]
    order = np.array(order)
    wx = v["L0_conv_W_x"]
    wxp = np.zeros((4 * D, XC), f)
    wxp[:, 0:DTR] = wx[:, 0:DTR]
    wxp[:, B0:B0 + N] = wx[:, DTR:DTR + N]
    wxp[:, C0:C0 + N] = wx[:, DTR + N:]
    const = np.zeros((128, K_END), f)
    p = np.arange(128)
    const[p, K_ID + p] = 1
    const[p, K_SEL + p % 64] = 1
    c = np.arange(C)
    const[:C, K_GM:K_GM + C] = (c[:, None] // 3 == c[None, :] // 3) / f(3)
    const[:, K_MEAN:K_MEAN + 128] = 1 / D
    const[:, K_EPS] = EPS
    inner = np.zeros((PW, PW), f)
    inner[1:-1, 1:-1] = 1
    wdel = np.zeros((97, KT * 128), f)
    wdel[0:DTR] = v["L0_conv_W_delta"][:, order]
    wdel[96] = v["L0_conv_b_delta"][order]
    bdw = tiles(v["L0_conv_b_dw"], 2)
    bdw[64:, 1] = bdw[:64, 1]
    bz = v["L0_conv_b_in"][D:]
    arrays = {
        "x": v["x"].reshape(B, C, L),
        "win": np.concatenate([v["L0_conv_W_in"], v["L0_conv_b_in"][None]], 0),
        "wdw": v["L0_conv_w_dw"].reshape(D, 9).T,
        "v192": np.concatenate([tiles(a, 2) for a in (bz, v["L0_conv_ln_g"], v["L0_conv_ln_b"])] + [bdw], 1),
        "wxp": wxp,
        "alog": v["L0_conv_A_log"][order].reshape(KT, 128, N).transpose(1, 2, 0).reshape(128, N * KT),
        "dp": np.stack([tiles(v["L0_conv_Dp"][g * D:(g + 1) * D], 2) for g in range(4)], 2),
        "wdel": wdel,
        "wout": v["L0_conv_W_out"],
        "w1": np.concatenate([v["L1_conv_dw"], v["L1_conv_xw"], v["L1_conv_bcw"]], 0).T,
        "b1": tiles(np.concatenate([v["L1_conv_db"], v["L1_conv_xb"], v["L1_conv_bcb"]]), 8),
        "yw": v["L1_conv_yw"],
        "yb": tiles(v["L1_conv_yb"], 2),
        "wt": np.concatenate([v["L1_conv_mw"], v["L1_conv_gw"]], 0).T,
        "bm": tiles(np.concatenate([v["L1_conv_mb"], v["L1_conv_gb"]]), 4),
        "ow": v["L1_conv_ow"].T,
        "ob": v["L1_conv_ob"].reshape(C, 1),
        "const": const,
        "inner": inner.reshape(1, PW * PW),
    }
    nc = bacc.Bacc("TRN2", target_bir_lowering=False, num_devices=1)
    feeds, args = {}, []
    for name, a in arrays.items():
        a = np.ascontiguousarray(a)
        feeds[f"in_{name}"] = a
        args.append(nc.dram_tensor(f"in_{name}", a.shape, _mybir.dt.from_np(a.dtype), kind="ExternalInput").ap())
    y = nc.dram_tensor("out_0", (B, C, L), F32, kind="ExternalOutput").ap()
    vmamba_then_s6(nc, *args, y)
    r = run_bass_kernel_spmd(nc, [feeds], core_ids=[0])
    return r.results[0]["out_0"].reshape(B, C, H, W)
```

```python
from contextlib import ExitStack

import concourse.bass as bass
from concourse import mybir

F32 = mybir.dt.float32
ALU = mybir.AluOpType
ACT = mybir.ActivationFunctionType

B, C, H, W = 2, 96, 96, 96
L = H * W
D = 192
N = 16
KT = 4 * D // 128
T = 512
NCH = L // T
TB = T // 128
KP = 4
R4 = 4 * W
NR = L // R4
HH = H // 2
XR = 5
XB = (HH + 2) // XR
PW = W + 2
XC = 80
DTR, B0, C0 = 6, 32, 64
LAT = 256
S_XA, S_XD = 1, 3
S_DL, S_SP = 4, 6
S_CT, S_EV = 11, 13
NPASS = 2
NDIR = 4
PB = NDIR * NR
HB = NR // 2
DIRS = (0, 2, 1, 3)
EPS = 1e-5
K_ID, K_SEL, K_GM, K_MEAN = 0, 128, 192, 288
K_EPS = 416
K_END = 417


def vmamba_then_s6(nc, x, win, wdw, wdv, v192, wxp, alog, dp, wdel, wout, w1, b1, yw, yb, wt, bm, ow, ob, const, inner, out):
    ctx = ExitStack()
    with ctx:
        def sb(name, shape):
            return ctx.enter_context(nc.sbuf_tensor(name, shape, F32))

        def sem(name):
            return ctx.enter_context(nc.semaphore(name))

        u_d = nc.dram_tensor("u_d", [D, L], F32).ap()
        bc_d = nc.dram_tensor("bc_d", [2, N, 2, T], F32).ap()
        yf_d = nc.dram_tensor("yf_d", [D, L], F32).ap()
        yb_d = nc.dram_tensor("yb_d", [D, L], F32).ap()
        yc_d = nc.dram_tensor("yc_d", [4, LAT, L], F32).ap()
        mf_d = nc.dram_tensor("mf_d", [128, 8 * 2 * LAT], F32).ap()

        cst = sb("cst", [128, K_END])
        ident = cst[:, K_ID:K_ID + 128]
        gmask = cst[0:C, K_GM:K_GM + C]
        eps = cst[:, K_EPS:K_EPS + 1]
        mean192 = cst[:, K_MEAN:K_MEAN + 128]
        sel = cst[:, K_SEL:K_SEL + 64]
        wx = sb("wx", [128, 2, 4, XC])
        wdl = sb("wdl", [97, KT * 128])
        aneg = sb("aneg", [128, N * KT])
        dps = sb("dps", [128, 2, 4])
        dsum = sb("dsum", [128, 2])
        vec = sb("vec", [128, 8])
        taps = sb("taps", [128, 2, 9])
        wz = sb("wz", [C, D])
        wzs = sb("wzs", [C, D])
        bzs = sb("bzs", [128, 2])
        wo = sb("wo", [128, 2, C])
        b1t = sb("b1t", [128, 8])
        b1s = sb("b1s", [128, 8])
        nb1 = sb("nb1", [128, 2])
        bmt = sb("bmt", [128, 4])
        bmf = sb("bmf", [128, 4])
        owt = sb("owt", [128, 2, C])
        obt = sb("obt", [C, 1])
        ybt = sb("ybt", [128, 2])
        bnst = sb("bnst", [C, NCH * 6])
        mv = sb("mv", [C, 2])
        gn = sb("gn", [C, 8])
        carry = sb("carry", [128, N, KT])

        AR = 44000
        arena = sb("arena", [128, AR])

        def lay(at, sizes):
            out_ = []
            for n in sizes:
                out_.append(arena[:, at:at + n])
                at += n
            assert at <= AR, at
            return out_

        (xr,) = lay(0, [L])
        xr = xr[0:C, :]
        s_wt, s_yw, s_mf = lay(0, [8 * 512, 2 * LAT, 8 * 512])
        s_wt = s_wt.rearrange("p (k m) -> p k m", k=8)
        s_yw = s_yw.rearrange("p (k m) -> p k m", k=2)
        s_mf = s_mf.rearrange("p (k m) -> p k m", k=8)
        p_xp, p_wa, p_wi, p_x2, p_ac, p_us = lay(L, [PW * PW, 9 * 128, D, 2 * (HH + 2) * PW, 2 * HH * W, 2 * R4])
        p_wa = p_wa[0:C + 1, :].rearrange("p (t d) -> p t d", t=9)
        p_xp = p_xp[0:C + 1, :].rearrange("p (h w) -> p h w", w=PW)
        p_wi = p_wi[0:C + 1, :]
        p_x2 = p_x2.rearrange("p (s h w) -> p s h w", s=2, w=PW)
        p_ac = p_ac.rearrange("p (s h w) -> p s h w", s=2, w=W)
        p_us = p_us.rearrange("p (q t) -> p q t", q=2)
        (dt, duT, z, dA, h, hs, cb, uu, xd, ee, ll, qq, du, dud, ys) = lay(0, [
            2 * KT * T, 2 * TB * KP * 128, 2 * TB * KP * 128, KT * T, 2 * KT * T, 8 * T, 8 * T, 4 * T, T, 2 * T, 2 * T,
            T, KP * T, 2 * (KT - KP) * T, 3 * T])
        dt = dt.rearrange("p (q k t) -> p q k t", q=2, k=KT)
        duT = duT.rearrange("p (q b d) -> p q b d", q=2, b=TB)
        z = z.rearrange("p (q b d) -> p q b d", q=2, b=TB)
        dA = dA.rearrange("p (k t) -> p k t", k=KT)
        h = h.rearrange("p (q k t) -> p q k t", q=2, k=KT)
        hs = hs.rearrange("p (q k t) -> p q k t", q=2, k=4)
        cb = cb.rearrange("p (q j i t) -> p q j i t", q=2, j=2, i=2)
        uu = uu.rearrange("p (j t) -> p j t", j=4)
        ee = ee.rearrange("p (q t) -> p q t", q=2)
        ll = ll.rearrange("p (q t) -> p q t", q=2)
        du = du.rearrange("p (k t) -> p k t", k=KP)
        dud = dud.rearrange("p (q k t) -> p q k t", q=2, k=KT - KP)
        ys = ys.rearrange("p (k t) -> p k t", k=3)
        bt = sb("bt", [128, 2, TB, N])
        (o_in, o_g, o_sq, o_rs, o_n, o_s) = lay(L, [12 * T, 4 * T, 4 * T, 2 * T, 4 * T, 2 * L])
        o_in = o_in.rearrange("p (q i j t) -> p q i j t", q=2, i=3, j=2)
        o_rs = o_rs.rearrange("p (q t) -> p q t", q=2)
        o_g, o_sq, o_n = (v.rearrange("p (q j t) -> p q j t", q=2, j=2) for v in (o_g, o_sq, o_n))
        o_s = o_s.rearrange("p (j l) -> p j l", j=2)

        l_av, l_c, l_sg, l_t, l_h, l_y, l_cp, l_w = lay(L, [2 * L, L, 2 * R4, 2 * R4, 2 * R4, 4 * R4, 4 * R4, 8 * 128])
        l_av = l_av.rearrange("p (i l) -> p i l", i=2)
        l_a, l_v = l_av[:, 0, :], l_av[:, 1, :]
        l_sg, l_t, l_h = (v.rearrange("p (q t) -> p q t", q=2) for v in (l_sg, l_t, l_h))
        l_y = l_y.rearrange("p (y t) -> p y t", y=4)
        l_cp = l_cp.rearrange("p (q i t) -> p q i t", q=2, i=2)
        l_w = l_w[0:C, :]
        m_f, m_y, m_g, m_p, m_o = lay(L, [8 * 512, 2 * 8 * T, 2 * T, 2 * T, T])
        m_f = m_f.rearrange("p (k m) -> p k m", k=8)
        m_y = m_y.rearrange("p (q k t) -> p q k t", q=2, k=8)
        m_g, m_p = (v.rearrange("p (j t) -> p j t", j=2) for v in (m_g, m_p))
        m_o = m_o[0:C, :]

        bank = [ctx.enter_context(nc.psum_tensor(f"bank{i}", [128, T], F32)) for i in range(8)]
        Y, DB, WB = bank[0:3], bank[3:6], bank[6:8]

        s_w = sem("weights_in")
        s_bar = sem("barrier")
        s_alone = sem("wait_carrier")
        s_set = sem("setup_step")
        s_ms = sem("merge_weight_psum"); s_mc = sem("merge_weight_copied")
        s_xin = sem("image_in")
        s_st = sem("stats_mean"); s_gp = sem("group_psum"); s_gq = sem("group_spread"); s_gs = sem("group_std");
        s_cw = sem("conv_weights_in"); s_wa = sem("conv_weights_ready"); s_xx = sem("projection_psum")
        s_xc = sem("projection_copied"); s_tap = sem("tap_added"); s_u2 = sem("sets_silu"); s_us2 = sem("sets_stored")
        s_xp = sem("padded_ready")
        s_cm = sem("conv_psum"); s_us = sem("silu_done"); s_ust = [sem(f"u_stored_{q}") for q in range(2)]
        s_zero = sem("pads_zeroed"); s_edge = sem("edge_in")
        s_u = sem("u_in"); s_ha = sem("h01_added"); s_hb = sem("h23_added"); s_db = sem("dBu_by_vector")
        s_xm = sem("xdbl_psum"); s_xd = sem("xdbl_copied"); s_cst = sem("bc_stored")
        s_btp = sem("bT_psum"); s_bt = sem("bT_ready")
        s_dl = sem("delta_psum"); s_abs = sem("abs_done"); s_e = sem("exp_neg_done"); s_ln = sem("ln_done")
        s_q1 = sem("log_rest1"); s_q2 = sem("log_rest"); s_m = sem("softplus_main"); s_dt = sem("dt_ready")
        s_du = sem("du_ready"); s_ct = sem("duT_psum"); s_ev = sem("duT_ready")
        s_z = sem("z_ready"); s_exp = sem("dA_ready"); s_d = sem("dBu_ready")
        s_scan = sem("scanned"); s_hc = sem("h_times_c"); s_ns = sem("n_summed"); s_car = sem("carry_kept")
        s_c0 = sem("carry_zeroed")
        s_cb = [sem(f"bc_spread_{q}") for q in range(2)]; s_yev = sem("y_copied"); s_yst = sem("y_stored")
        s_zw = sem("z_weights"); s_p1 = sem("post_forward_sum"); s_pe = sem("post_ln"); s_bzp = sem("z_bias_psum")
        s_pl = [sem(f"post_in_{q}") for q in range(2)]; s_pg = sem("post_sum"); s_pm = sem("post_mean")
        s_pz = sem("post_z")
        s_pc = sem("post_centred"); s_pq = sem("post_square"); s_pv = sem("post_var"); s_pr = sem("post_rstd")
        s_pt = sem("post_norm"); s_pa = sem("post_scaled"); s_psi = sem("post_silu"); s_pp = sem("post_gated")
        s_po = sem("post_out")
        s_px = sem("x1_ready")
        s_lw = sem("l1_weights_in"); s_lws = sem("l1_weights_scaled"); s_lbp = sem("l1_bias_psum")
        s_lb = sem("l1_bias")
        s_lp = sem("l1_psum"); s_ls = sem("l1_gate"); s_lc = sem("l1_c"); s_lt = sem("l1_bgate"); s_lv = sem("l1_v")
        s_lh = sem("l1_scanned"); s_ly = [sem(f"l1_y_{q}") for q in range(2)]; s_lyv = sem("l1_y_by_vector")
        s_lcp = sem("l1_columns_copied"); s_lst = [sem(f"l1_stored_{y}") for y in range(4)]
        s_l0 = sem("l1_state_zeroed")
        s_mfi = sem("merge_weights_in"); s_ml = [sem(f"merge_in_{q}") for q in range(2)]; s_mp = sem("merge_psum")
        s_mg = sem("merge_gate")
        s_mr = sem("merge_prod"); s_mo = sem("merge_out_psum"); s_mx = sem("merge_out"); s_mst = sem("out_stored")

        NW = 24
        NBAR = 5

        def alone(eng):
            eng.sem_inc(s_alone, 1)

        def barrier(eng, index):
            alone(eng)
            eng.drain().then_inc(s_bar, 1)
            eng.wait_ge(s_bar, 5 * (index + 1))
            alone(eng)

        def conv_rhs(r, tap):
            return p_xp[:, bass.ds(r * 4 + tap // 3, 4), tap % 3:tap % 3 + W]

        def backward(v, r):
            return v[:, ::-1][:, r * R4:(r + 1) * R4]

        def columns(v, r, back):
            at = bass.ds(W - 4 - r * 4 if back else r * 4, 4)
            if len(v.shape) == 3:
                return v.rearrange("p i (h w) -> p i w h", w=W)[:, :, at, :]
            return v.rearrange("p (h w) -> p w h", w=W)[:, at, :]

        def output_of(d, r4, y):
            r, out_, state = r4 * 4 + y, l_y[:, y, :], l_h[:, y % 2, :]
            if d < 2:
                return out_, state, backward(l_c, r) if d else l_c[:, bass.ds(r * R4, R4)]
            out_, state = (v.rearrange("p (w h) -> p w h", h=H) for v in (out_, state))
            if d == 3:
                out_, state = out_[:, ::-1, ::-1], state[:, ::-1, ::-1]
            return out_, state, columns(l_c, r, d == 3)

        def skewed(eng, turn_, lag=2):
            def flags(i):
                return i < NCH, 1 <= i <= NCH, lag <= i < NCH + lag

            peel = lag + lag % 2
            for i in range(peel):
                turn_(i, i % 2, *flags(i))
            with eng.Fori(peel // 2, NCH // 2) as p:
                for q in range(2):
                    turn_(p * 2 + q, q, True, True, True)
            for i in range(NCH, NCH + lag):
                turn_(i, i % 2, *flags(i))

        block = ctx.enter_context(nc.Block())

        @block.sync
        def _(sp):
            loads = [
                (cst[:, :], const), (dps[:, :, :], dp), (aneg[:, :], alog), (wdl[:, :], wdel), (vec[:, :], v192),
                (wz[:, :], win[0:C, D:2 * D]), (wo[0:128, 0, :], wout[0:128, :]), (wo[0:64, 1, :], wout[128:D, :]),
                (b1t[:, :], b1), (bmt[:, :], bm), (owt[:, :, :], ow.rearrange("(k p) c -> p k c", p=128)),
                (obt[:, :], ob), (ybt[:, :], yb), (taps[:, :, :], wdv),
                (s_wt, wt.rearrange("(k p) m -> p k m", p=128)), (s_yw, yw.rearrange("(k p) m -> p k m", p=128)),
            ]
            for g in range(2):
                for way in range(2):
                    base = (2 * way + g) * D
                    loads.append((wx[0:128, g, 2 * way, :], wxp[base:base + 128, :]))
                    loads.append((wx[0:64, g, 2 * way + 1, :], wxp[base + 128:base + D, :]))
            assert len(loads) == NW
            for ahead in (s_cst, s_yst, *s_ust, *s_lst):
                sp.sem_inc(ahead, 1)
            for to, of in loads:
                sp.dma_start(to, of).then_inc(s_w, 16)
            sp.wait_ge(s_mc, 8)
            sp.dma_start(mf_d, s_mf.rearrange("p k m -> p (k m)")).then_inc(s_set, 16)
            sp.wait_ge(s_set, 16)
            barrier(sp, 0)
            with sp.Fori(0, B) as b:
                sp.dma_start(xr, x[bass.ds(b, 1), :, :].rearrange("o c l -> (o c) l")).then_inc(s_xin, 16)
                sp.dma_start(p_wa, wdw[:, 0:128].unsqueeze(0).broadcast_to([C + 1, 9, 128])).then_inc(s_cw, 16)
                sp.dma_start(p_wi, win[:, 0:D]).then_inc(s_cw, 16)
                sp.wait_ge(s_zero, b + 1)
                alone(sp)
                sp.dma_start(p_xp[C:C + 1, :, :], inner.rearrange("o (h w) -> o h w", w=PW)).then_inc(s_edge, 16)
                with sp.Fori(0, NR // 4) as r2:
                    for q in range(2):
                        r = r2 * 2 + q
                        sp.wait_ge(s_us, b * (NR // 2) + r + 3)
                        alone(sp)
                        sp.dma_start(u_d[0:128, bass.ds(r * R4, R4)], p_us[:, q, :]).then_inc(s_ust[q], 16)
                for set_ in range(2):
                    sp.wait_ge(s_u2, b * 4 + set_ * 2 + 2)
                    alone(sp)
                    if set_ == 0:
                        for half in range(2):
                            sp.dma_start(u_d[128:D, half * HH * W:(half + 1) * HH * W],
                                         p_ac[64 * half:64 * half + 64, 0, :, :].rearrange("p h w -> p (h w)")).then_inc(s_us2, 16)
                    else:
                        sp.dma_start(u_d[0:128, HH * W:], p_ac[:, 1, :, :].rearrange("p h w -> p (h w)")).then_inc(s_us2, 16)
                sp.wait_ge(s_us2, 48 * (b + 1))
                alone(sp)
                for q in range(2):
                    sp.wait_ge(s_ust[q], (b + 1) * NR * 4 + 1)
                    alone(sp)
                barrier(sp, b * NBAR + 1)

                def load_u(c, m):
                    sp.wait_ge(s_du, KT * m + 1)
                    alone(sp)
                    fwd, bwd = bass.ds(c * T, T), bass.ds(L - T - c * T, T)
                    sp.dma_start(uu[:, 0, :], u_d[0:128, fwd]).then_inc(s_u, 16)
                    sp.dma_start(uu[0:64, 1, :], u_d[128:D, fwd]).then_inc(s_u, 16)
                    sp.dma_start(uu[64:128, 1, :], u_d[128:D, fwd]).then_inc(s_u, 16)
                    sp.dma_start(uu[:, 2, :], u_d[0:128, bwd]).then_inc(s_u, 16)
                    sp.dma_start(uu[0:64, 3, :], u_d[128:D, bwd]).then_inc(s_u, 16)
                    sp.dma_start(uu[64:128, 3, :], u_d[128:D, bwd]).then_inc(s_u, 16)

                def store_bc(m, q):
                    sp.wait_ge(s_xd, m + 1)
                    alone(sp)
                    sp.dma_start(bc_d[q, :, 0, :], xd[B0:B0 + N, :]).then_inc(s_cst, 16)
                    sp.dma_start(bc_d[q, :, 1, :], xd[C0:C0 + N, :]).then_inc(s_cst, 16)

                def store_y(c, m):
                    fwd, bwd = bass.ds(c * T, T), bass.ds(L - T - c * T, T)
                    sp.wait_ge(s_yev, 4 * (m + 1) + 1)
                    alone(sp)
                    sp.dma_start(yf_d[0:128, fwd], ys[:, 0, :]).then_inc(s_yst, 16)
                    sp.dma_start(yb_d[0:128, bwd], ys[:, 1, :]).then_inc(s_yst, 16)
                    sp.dma_start(yf_d[128:D, fwd], ys[0:64, 2, :]).then_inc(s_yst, 16)
                    sp.dma_start(yb_d[128:D, bwd], ys[64:128, 2, :]).then_inc(s_yst, 16)

                def spread_bc(m, q, first, last):
                    alone(sp)
                    with sp.Fori(first, last) as p2:
                        for par in range(2):
                            p = p2 * 2 + par
                            pair = m * (N // 2) + p
                            sp.wait_ge(s_hc, 6 * pair + 1)
                            alone(sp)
                            sp.wait_ge(s_db, 4 * pair + 1)
                            alone(sp)
                            sp.dma_start(cb[:, par, :, :, :], bc_d[q, bass.ds(p * 2, 2), :, :].unsqueeze(0)
                                         .broadcast_to([128, 2, 2, T])).then_inc(s_cb[par], 16)

                def chunk(c, q, first, last):
                    m = b * NCH + c
                    sp.wait_ge(s_cst, 32 * (m + 1) + 1)
                    alone(sp)
                    spread_bc(m, q, 0, 1)
                    if not last:
                        load_u(c + 1, m + 1)
                    if not first:
                        store_y(c - 1, m - 1)
                    spread_bc(m, q, 1, 2)
                    if not last:
                        store_bc(m + 1, 1 - q)
                    spread_bc(m, q, 2, 4)

                load_u(0, b * NCH)
                store_bc(b * NCH, 0)
                chunk(0, 0, True, False)
                with sp.Fori(0, (NCH - 2) // 2) as cp:
                    chunk(cp * 2 + 1, 1, False, False)
                    chunk(cp * 2 + 2, 0, False, False)
                chunk(NCH - 1, 1, False, True)
                store_y(NCH - 1, b * NCH + NCH - 1)
                sp.wait_ge(s_yst, (b + 1) * NCH * 64 + 1)
                alone(sp)
                barrier(sp, b * NBAR + 2)

                sp.dma_start(xr, x[bass.ds(b, 1), :, :].rearrange("o c l -> (o c) l")).then_inc(s_xin, 16)
                with sp.Fori(0, NCH // 2) as c2:
                    for q in range(2):
                        at = bass.ds((c2 * 2 + q) * T, T)
                        sp.wait_ge(s_pg, 2 * (b * NCH + c2 * 2 + q) + 2)
                        alone(sp)
                        for i, of in enumerate((u_d, yf_d, yb_d)):
                            sp.dma_start(o_in[:, q, i, 0, :], of[0:128, at]).then_inc(s_pl[q], 16)
                            sp.dma_start(o_in[0:64, q, i, 1, :], of[128:D, at]).then_inc(s_pl[q], 16)
                barrier(sp, b * NBAR + 3)

                sp.dma_start(l_w, w1).then_inc(s_lw, 16)
                for ct in range(NPASS):
                    for d in range(NDIR):
                        with sp.Fori(0, NR // 4) as r4:
                            for y in range(4):
                                ps, turn_ = b * NPASS + ct, r4 * 2 + y // 2
                                if y % 2 == 0:
                                    sp.wait_ge(s_ly[0], ps * NDIR * HB + d * HB + turn_ + 2)
                                elif d == 0:
                                    sp.wait_ge(s_ly[1], ps * HB + turn_ + 2)
                                else:
                                    sp.wait_ge(s_lyv, (ps * (NDIR - 1) + d - 1) * HB + turn_ + 2)
                                alone(sp)
                                sp.dma_start(yc_d[DIRS[d], ct * 128:ct * 128 + 128, bass.ds((r4 * 4 + y) * R4, R4)],
                                             l_y[:, y, :]).then_inc(s_lst[y], 16)
                for y in range(4):
                    sp.wait_ge(s_lst[y], (b + 1) * NPASS * (PB // 4) * 16 + 1)
                    alone(sp)
                alone(sp)
                barrier(sp, b * NBAR + 4)

                sp.dma_start(m_f.rearrange("p k m -> p (k m)"), mf_d).then_inc(s_mfi, 16)
                with sp.Fori(0, NCH // 2) as c2:
                    for q in range(2):
                        c = c2 * 2 + q
                        m = b * NCH + c
                        sp.wait_ge(s_mp, 4 * (m + 1))
                        alone(sp)
                        sp.dma_start(m_y[:, q, :, :], yc_d.rearrange("d (k p) l -> p (d k) l", p=128)[:, :, bass.ds(c * T, T)]) \
                            .then_inc(s_ml[q], 16)
                barrier(sp, b * NBAR + 5)
            sp.wait_ge(s_mst, B * NCH * 16 + 1)
            alone(sp)

        @block.gpsimd
        def _(pool):
            pool.sem_inc(s_pp, 1)
            pool.sem_inc(s_hc, 7)
            for ahead in s_ly:
                pool.sem_inc(ahead, 1)
            barrier(pool, 0)
            with pool.Fori(0, B) as b:
                pool.memset(p_xp, 0.0).then_inc(s_zero, 1)
                barrier(pool, b * NBAR + 1)

                def times_u(m, q, k):
                    u = (uu[:, 0, :], uu[:, 0, :], uu[:, 2, ::-1], uu[:, 2, ::-1], uu[:, 1, :], uu[:, 3, ::-1])[k]
                    pool.wait_ge(s_dt, m * KT + k + 2)
                    if k == 0:
                        pool.wait_ge(s_ct, KP * m + 1)
                    pool.tensor_tensor(du[:, k, :] if k < KP else dud[:, q, k - KP, :], dt[:, q, k, :], u,
                                       ALU.mult).then_inc(s_du, 1)

                def times_c(g, par, slot):
                    cc = cb[:, slot, par, 1, :]
                    pool.wait_ge(s_ha, g + 3)
                    pool.tensor_tensor(hs[:, par, 0, :], hs[:, par, 0, :], cc, ALU.mult).then_inc(s_hc, 1)
                    pool.wait_ge(s_scan, g * KT + 4 + KT)
                    pool.wait_ge(s_ns, g + 1)
                    pool.tensor_tensor(hs[:, par, 1, :], h[:, par, 2, :], h[:, par, 3, :], ALU.add).then_inc(s_hb, 1)
                    pool.wait_ge(s_hb, g + 1)
                    pool.tensor_tensor(hs[:, par, 1, :], hs[:, par, 1, :], cc, ALU.mult).then_inc(s_hc, 1)
                    pool.wait_ge(s_scan, g * KT + 6 + KT)
                    pool.tensor_tensor(hs[:, par, 2:4, :], h[:, par, 4:6, :], cc.unsqueeze(1).broadcast_to([128, 2, T]),
                                       ALU.mult).then_inc(s_hc, 1)

                def states(c, p4, next_q=None):
                    for r in range(4):
                        slot, j = r // 2, r % 2
                        m = b * NCH + c
                        if j == 0:
                            pool.wait_ge(s_cb[slot], (m * (N // 4) + p4 + 1) * 16)
                        times_c(m * N + p4 * 4 + r, j, slot)
                        if next_q is not None and 0 <= p4 * 4 + r - S_SP < KT:
                            times_u(m + 1, next_q, p4 * 4 + r - S_SP)

                def chunk(c, q):
                    with pool.Fori(0, 1) as p4:
                        states(c, p4)
                    states(c, 1, 1 - q)
                    states(c, 2, 1 - q)
                    with pool.Fori(3, 4) as p4:
                        states(c, p4)

                for k in range(KT):
                    times_u(b * NCH, 0, k)
                with pool.Fori(0, (NCH - 2) // 2) as cp:
                    chunk(cp * 2, 0)
                    chunk(cp * 2 + 1, 1)
                chunk(NCH - 2, 0)
                with pool.Fori(0, N // 4) as p4:
                    states(NCH - 1, p4)
                barrier(pool, b * NBAR + 2)
                pool.wait_ge(s_psi, 2 * NCH * (b + 1) + 3)
                alone(pool)

                def turn_(i, q, front, middle, tail):
                    if not middle:
                        return
                    m, q, at = b * NCH + i - 1, 1 - q, bass.ds((i - 1) * T, T)
                    pool.wait_ge(s_pa, 2 * (m + 1) + 3)
                    for j, n_ in ((0, 128), (1, 64)):
                        pool.tensor_tensor(o_n[0:n_, q, j, :], o_n[0:n_, q, j, :], o_s[0:n_, j, at], ALU.mult).then_inc(s_pp, 1)

                skewed(pool, turn_)
                barrier(pool, b * NBAR + 3)
                for ct in range(NPASS):
                    ps = b * NPASS + ct
                    pool.wait_ge(s_lyv, ps * (NDIR - 1) * HB + 1)
                    alone(pool)

                    def output(d, r4, y):
                        pool.wait_ge(s_lst[y], 16 * (ps * (PB // 4) + d * (NR // 4) + r4) + 1)
                        pool.wait_ge(s_lh, ps * PB + d * NR + r4 * 4 + y + 2)
                        pool.tensor_tensor(*output_of(d, r4, y), ALU.mult).then_inc(s_ly[y % 2], 1)

                    with pool.Fori(0, NR // 4) as r4:
                        for y in range(4):
                            pool.wait_ge(s_lc, ps * NR + r4 * 4 + y + 3)
                            output(0, r4, y)
                    for r4 in range(NR // 4):
                        for y in (0, 2):
                            output(1, r4, y)
                    for d in (2, 3):
                        with pool.Fori(0, NR // 4) as r4:
                            for y in (0, 2):
                                output(d, r4, y)
                barrier(pool, b * NBAR + 4)
                barrier(pool, b * NBAR + 5)

        @block.scalar
        def _(act):
            for ahead in (s_pq, s_mst, s_ev, s_pr):
                act.sem_inc(ahead, 1)
            act.sem_inc(s_us, 2)
            act.sem_inc(s_pa, 3)
            act.sem_inc(s_pe, 2)
            act.sem_inc(s_psi, 3)
            act.sem_inc(s_lc, 2)
            act.sem_inc(s_lcp, 1)
            act.sem_inc(s_mg, 2)
            act.wait_ge(s_w, 16 * NW)
            act.activation(aneg[:, :], aneg[:, :], ACT.Exp).then_inc(s_e, 1)
            barrier(act, 0)
            def group_std(i):
                act.wait_ge(s_gp, 2 * i + 2)
                act.activation(gn[:, 5:6], WB[0][0:C, 1:2], ACT.Sqrt, bias=eps[0:C, :]).then_inc(s_gs, 1)

            with act.Fori(0, B) as b:
                group_std(b * 2)
                for i in range(2 * XB):
                    act.wait_ge(s_xx, b * 2 * XB + i + 1)
                    act.copy(p_x2[:, i // XB, i % XB * XR:(i % XB + 1) * XR, :],
                             bank[2 + i % 4][:, 0:XR * PW].rearrange("p (h w) -> p h w", w=PW)).then_inc(s_xc, 1)
                with act.Fori(0, NR // 4) as r2:
                    for q in range(2):
                        act.wait_ge(s_ust[q], 16 * (b * (NR // 4) + r2) + 1)
                        act.wait_ge(s_cm, b * (NR // 2) + r2 * 2 + q + 1)
                        act.activation(p_us[:, q, :], bank[q][:, 0:R4], ACT.Silu, bias=vec[:, 6:7]).then_inc(s_us, 1)
                for set_ in range(2):
                    for half in range(2):
                        act.wait_ge(s_tap, b * 36 + set_ * 18 + 17 + half)
                        rows = p_ac[:, set_, half * HH // 2:(half + 1) * HH // 2, :]
                        act.activation(rows, rows, ACT.Silu, bias=vec[:, 7 - set_:8 - set_]).then_inc(s_u2, 1)
                barrier(act, b * NBAR + 1)

                def stage_a(m):
                    act.wait_ge(s_xm, m + 1)
                    act.wait_ge(s_cst, 32 * m + 1)
                    act.copy(xd[0:XC, :], WB[0][0:XC, :]).then_inc(s_xd, 1)

                def copy_bt(m, q):
                    act.wait_ge(s_btp, m + 1)
                    act.copy(bt[:, q, :, :], WB[1][:, 0:TB * N].rearrange("p (b n) -> p b n", b=TB)).then_inc(s_bt, 1)

                def softplus(m, k):
                    i = m * KT + k
                    act.wait_ge(s_dl, i + 1)
                    act.wait_ge(s_dt, (i - 1 if k >= 2 else m * KT) + 1)
                    act.activation(ee[:, k % 2, :], WB[k % 2][:, :], ACT.Abs).then_inc(s_abs, 1)
                    act.wait_ge(s_abs, i + 1)
                    act.activation(ee[:, k % 2, :], ee[:, k % 2, :], ACT.Exp, scale=-1.0).then_inc(s_e, 1)
                    act.wait_ge(s_e, i + 2)
                    act.activation(ll[:, k % 2, :], ee[:, k % 2, :], ACT.Ln, bias=1.0).then_inc(s_ln, 1)

                def stage_c(m, q, ks):
                    for k in ks:
                        act.wait_ge(s_ct, m * KP + k + 2)
                        act.copy(duT[:, q, :, k * 128:(k + 1) * 128], WB[k % 2][:, :].rearrange("p (b d) -> p b d", b=TB)) \
                            .then_inc(s_ev, 1)

                def state(c, q, n, par, piece=None):
                    g = (b * NCH + c) * N + n
                    act.wait_ge(s_d, (g + 1) * KP)
                    for t in range(TB):
                        last_z = act.activation(z[:, par, t, :], duT[:, q, t, :], ACT.Copy, scale=bt[:, q, t, bass.ds(n, 1)])
                    last_z.then_inc(s_z, 1)
                    for k in range(KT):
                        act.wait_ge(s_scan, g * KT + k + 1)
                        act.activation(dA[:, k, :], dt[:, q, k, :], ACT.Exp,
                                       scale=aneg[:, bass.ds(n * KT + k, 1)]).then_inc(s_exp, 1)
                        if k == 2 and piece:
                            softplus(*piece)

                def chunk(c, q, last):
                    m = b * NCH + c
                    act.wait_ge(s_ev, KP * (m + 1) + 1)
                    act.wait_ge(s_bt, m + 1)
                    act.wait_ge(s_dt, KT * (m + 1) + 1)
                    if last:
                        with act.Fori(0, N // 2) as p:
                            for par in range(2):
                                state(c, q, p * 2 + par, par)
                        return
                    with act.Fori(0, 1) as p:
                        for par in range(2):
                            state(c, q, p * 2 + par, par)
                    for n in range(2, N):
                        k = n - S_SP
                        state(c, q, n, n % 2, (m + 1, k) if 0 <= k < KT else None)
                        if n == S_XD:
                            stage_a(m + 1)
                        if n == S_SP - 1:
                            copy_bt(m + 1, 1 - q)
                        if n >= S_EV and 2 * (n - S_EV) < KP:
                            stage_c(m + 1, 1 - q, range(2 * (n - S_EV), 2 * (n - S_EV) + 2))

                act.preload_act_table_set("natural_log_exp_and_others")
                act.wait_ge(s_c0, b + 1)
                stage_a(b * NCH)
                copy_bt(b * NCH, 0)
                for k in range(KT):
                    softplus(b * NCH, k)
                stage_c(b * NCH, 0, range(KP))
                with act.Fori(0, (NCH - 2) // 2) as cp:
                    chunk(cp * 2, 0, False)
                    chunk(cp * 2 + 1, 1, False)
                chunk(NCH - 2, 0, False)
                chunk(NCH - 1, 1, True)
                barrier(act, b * NBAR + 2)

                both = ((0, 128), (1, 64))
                act.preload_act_table(ACT.Silu)
                with act.Fori(0, NCH // 2) as c2:
                    for q in range(2):
                        c = c2 * 2 + q
                        act.wait_ge(s_pz, b * NCH + c + 1)
                        for j, n_ in both:
                            act.activation(o_s[0:n_, j, bass.ds(c * T, T)], bank[4 + 2 * q + j][0:n_, :], ACT.Silu,
                                           bias=bzs[0:n_, j:j + 1]).then_inc(s_psi, 1)
                act.preload_act_table_set("natural_log_exp_and_others")

                def turn_(i, q, front, middle, tail):
                    if middle:
                        m, s = b * NCH + i - 1, 1 - q
                        act.wait_ge(s_pv, m + 3)
                        act.wait_ge(s_pt, 2 * m + 1)
                        act.activation(o_rs[:, s, :], bank[2 + s][:, :], ACT.Ln, bias=eps).then_inc(s_pe, 1)
                        act.wait_ge(s_pe, m + 3)
                        act.activation(o_rs[:, s, :], o_rs[:, s, :], ACT.Exp, scale=-0.5).then_inc(s_pr, 1)
                        act.wait_ge(s_pt, 2 * m + 5)
                        act.wait_ge(s_po, m + 1)
                        for j, n_ in both:
                            act.activation(o_n[0:n_, s, j, :], o_g[0:n_, s, j, :], ACT.Identity,
                                           bias=vec[0:n_, 4 + j:5 + j], scale=vec[0:n_, 2 + j:3 + j]).then_inc(s_pa, 1)
                    if front:
                        m = b * NCH + i
                        act.wait_ge(s_pc, 2 * m + 5)
                        act.wait_ge(s_pv, m + 1)
                        for j, n_ in both:
                            act.activation(o_sq[0:n_, q, j, :], o_g[0:n_, q, j, :], ACT.Square).then_inc(s_pq, 1)

                skewed(act, turn_)
                barrier(act, b * NBAR + 3)

                group_std(b * 2 + 1)
                act.wait_ge(s_lb, b + 1)
                for ct in range(NPASS):
                    ps = b * NPASS + ct
                    act.wait_ge(s_lh, ps * PB + 1)
                    act.wait_ge(s_ly[0], ps * NDIR * HB + 1)
                    act.wait_ge(s_ly[1], ps * HB + 1)
                    act.wait_ge(s_lyv, ps * (NDIR - 1) * HB + 1)
                    act.wait_ge(s_lcp, ps * 2 * NR + 1)
                    alone(act)
                    with act.Fori(0, NR // 2) as r2:
                        for q in range(2):
                            r = r2 * 2 + q
                            i = ps * NR + r
                            at = bass.ds(r * R4, R4)
                            pb = bank[4 * q:4 * q + 4]
                            act.wait_ge(s_lp, 4 * i + 1)
                            act.activation(l_a[:, at], pb[0][:, 0:R4], ACT.Sigmoid, bias=nb1[:, ct:ct + 1], scale=-1.0)
                            act.wait_ge(s_lt, i + 1)
                            act.activation(l_sg[:, q, :], pb[0][:, 0:R4], ACT.Sigmoid, bias=b1s[:, ct:ct + 1]) \
                                .then_inc(s_ls, 1)
                            act.wait_ge(s_lp, 4 * i + 4)
                            act.activation(l_c[:, at], pb[3][:, 0:R4], ACT.Identity, bias=b1s[:, 6 + ct:7 + ct]) \
                                .then_inc(s_lc, 1)
                    act.wait_ge(s_ls, (ps + 1) * NR)
                    act.wait_ge(s_lv, (ps + 1) * NR + 2)
                    alone(act)
                    for d in (2, 3):
                        with act.Fori(0, NR // 2) as r2:
                            for q in range(2):
                                act.wait_ge(s_lh, ps * PB + d * NR + r2 * 2 + q)
                                act.copy(l_cp[:, q, :, :].rearrange("p i (w h) -> p i w h", h=H),
                                         columns(l_av, r2 * 2 + q, d == 3)).then_inc(s_lcp, 1)
                barrier(act, b * NBAR + 4)
                def gates(m):
                    for j in range(2):
                        act.wait_ge(s_mp, 8 + 4 * m + 2 * j + 1)
                        act.wait_ge(s_mr, 2 * m + j + 1)
                        act.activation(m_g[:, j, :], bank[2 * j][:, :], ACT.Sigmoid, bias=bmf[:, 2 + j:3 + j]) \
                            .then_inc(s_mg, 1)

                def store(m, c):
                    act.wait_ge(s_mx, m + 1 + 1)
                    act.dma_start(out[bass.ds(b, 1), :, bass.ds(c * T, T)].rearrange("o c l -> (o c) l"), m_o) \
                        .then_inc(s_mst, 16)

                gates(b * NCH)
                with act.Fori(1, NCH) as c:
                    gates(b * NCH + c)
                    store(b * NCH + c - 1, c - 1)
                store(b * NCH + NCH - 1, NCH - 1)
                act.wait_ge(s_mst, (b + 1) * NCH * 16 + 1)
                barrier(act, b * NBAR + 5)

        @block.vector
        def _(dve):
            for ahead in (s_du, s_dt, s_lh, s_yev, s_mx):
                dve.sem_inc(ahead, 1)
            dve.sem_inc(s_scan, KT)
            dve.sem_inc(s_car, N)
            dve.sem_inc(s_pg, 4)
            dve.sem_inc(s_pt, 3)
            dve.sem_inc(s_pc, 3)
            dve.sem_inc(s_px, 2)
            dve.sem_inc(s_ha, 2)
            dve.sem_inc(s_db, 5)
            dve.sem_inc(s_lt, 2)
            dve.sem_inc(s_lyv, 1)
            dve.sem_inc(s_lv, 2)
            dve.sem_inc(s_mr, 2)
            dve.wait_ge(s_w, 16 * NW)
            dve.tensor_tensor(wx[:, 0, 0:4:2, :], wx[:, 0, 0:4:2, :], wx[:, 1, 0:4:2, :], ALU.add)
            dve.tensor_tensor(wx[0:64, 0, 1:4:2, :], wx[0:64, 0, 1:4:2, :], wx[0:64, 1, 1:4:2, :], ALU.add)
            dve.tensor_tensor(dps[:, :, 0:2], dps[:, :, 0:2], dps[:, :, 2:4], ALU.add)
            dve.drain()
            dve.tensor_tensor(dsum[:, :], dps[:, :, 0], dps[:, :, 1], ALU.add)
            dve.wait_ge(s_e, 1)
            dve.tensor_scalar(aneg[:, :], aneg[:, :], -1.0, None, ALU.mult)
            for i in range(8):
                dve.wait_ge(s_ms, i + 1)
                dve.tensor_copy(s_mf[:, i, :], bank[i][:, :]).then_inc(s_mc, 1)
            dve.wait_ge(s_ms, 9)
            dve.tensor_tensor(bmf[:, :], bank[0][:, 0:4], bmt[:, :], ALU.add)
            barrier(dve, 0)

            def group_norm(i):
                dve.drain()
                dve.bn_aggr(mv[:, :], bnst[:, :]).then_inc(s_st, 1)
                dve.wait_ge(s_gp, 2 * i + 1)
                dve.tensor_copy(gn[:, 0:1], WB[0][0:C, 0:1])
                dve.drain()
                dve.tensor_tensor(gn[:, 1:2], mv[:, 0:1], gn[:, 0:1], ALU.subtract)
                dve.drain()
                dve.scalar_tensor_tensor(gn[:, 2:3], gn[:, 1:2], gn[:, 1:2], mv[:, 1:2], ALU.mult, ALU.add) \
                    .then_inc(s_gq, 1)
                dve.wait_ge(s_gs, i + 1)
                dve.reciprocal(gn[:, 3:4], gn[:, 5:6])
                dve.drain()
                dve.scalar_tensor_tensor(gn[:, 4:5], gn[:, 0:1], -1.0, gn[:, 3:4], ALU.mult, ALU.mult)
                dve.drain()

            with dve.Fori(0, B) as b:
                dve.wait_ge(s_xin, 32 * b + 16)
                for c in range(NCH):
                    dve.bn_stats(bnst[:, 6 * c:6 * c + 6], xr[:, c * T:(c + 1) * T])
                group_norm(b * 2)
                dve.tensor_scalar(wzs[:, :], wz[:, :], gn[:, 3:4], None, ALU.mult).then_inc(s_zw, 1)
                dve.wait_ge(s_bzp, b + 1)
                dve.tensor_tensor(bzs[:, 0:1], WB[1][:, 0:1], vec[:, 0:1], ALU.add)
                dve.tensor_tensor(bzs[0:64, 1:2], WB[1][0:64, 1:2], vec[0:64, 1:2], ALU.add)
                dve.wait_ge(s_cw, 32 * (b + 1))
                dve.tensor_tensor(p_wa, p_wa, p_wi[:, 0:128].unsqueeze(1).broadcast_to([C + 1, 9, 128]), ALU.mult) \
                    .then_inc(s_wa, 1)
                dve.wait_ge(s_zero, b + 1)
                dve.tensor_scalar(p_xp[0:C, 1:H + 1, 1:W + 1], xr.rearrange("c (h w) -> c h w", w=W), gn[:, 3:4],
                                  gn[:, 4:5], ALU.mult, ALU.add).then_inc(s_xp, 1)
                for set_ in range(2):
                    dve.wait_ge(s_xc, XB * (b * 2 + set_ + 1))
                    for tap in range(9):
                        for half in range(2):
                            r0, n_ = half * HH // 2, HH // 2
                            rows = p_ac[:, set_, r0:r0 + n_, :]
                            moved = p_x2[:, set_, r0 + tap // 3:r0 + tap // 3 + n_, tap % 3:tap % 3 + W]
                            if tap == 0:
                                dve.tensor_scalar(rows, moved, taps[:, set_, 0:1], None, ALU.mult).then_inc(s_tap, 1)
                            else:
                                dve.wait_ge(s_tap, b * 36 + set_ * 18 + (tap - 1) * 2 + half + 1)
                                dve.scalar_tensor_tensor(rows, moved, taps[:, set_, tap:tap + 1], rows, ALU.mult, ALU.add) \
                                    .then_inc(s_tap, 1)
                barrier(dve, b * NBAR + 1)

                dve.memset(xd[64:96, :], 0.0)
                dve.memset(xd[96:97, :], 1.0)
                dve.memset(carry[:, :, :], 0.0).then_inc(s_c0, 1)
                dve.wait_ge(s_c0, b + 1)

                def softplus(m, q, k):
                    i = m * KT + k
                    dve.wait_ge(s_e, i + 2)
                    dve.wait_ge(s_dt, i + 1)
                    dve.tensor_scalar(qq, ee[:, k % 2, :], 1.0, -1.0, ALU.add, ALU.add).then_inc(s_q1, 1)
                    dve.wait_ge(s_q1, i + 1)
                    dve.tensor_tensor(qq, ee[:, k % 2, :], qq, ALU.subtract).then_inc(s_q2, 1)
                    dve.wait_ge(s_ln, i + 1)
                    dve.scalar_tensor_tensor(ll[:, k % 2, :], WB[k % 2][:, :], 0.0, ll[:, k % 2, :], ALU.max, ALU.add) \
                        .then_inc(s_m, 1)
                    dve.wait_ge(s_q2, i + 1)
                    dve.wait_ge(s_m, i + 1)
                    dve.tensor_tensor(dt[:, q, k, :], ll[:, k % 2, :], qq, ALU.add).then_inc(s_dt, 1)

                def keep_carry(g, n, par):
                    dve.wait_ge(s_scan, (g + 2) * KT)
                    alone(dve)
                    dve.tensor_copy(carry[:, bass.ds(n, 1), :].rearrange("p o k -> p (o k)"),
                                    h[:, par, :, T - 1]).then_inc(s_car, 1)

                def scans(c, q, p4, r, first=False, before=False):
                    n, par, slot = p4 * 4 + r, r % 2, r // 2
                    g = (b * NCH + c) * N + n

                    def times_b(k):
                        i = k - KP
                        dve.wait_ge(s_scan, (g + 1) * KT + k - 2)
                        dve.tensor_tensor(DB[k % 3][:, :], dud[:, q, i, :], cb[:, slot, par, 0, :], ALU.mult) \
                            .then_inc(s_db, 1)

                    def scan(k):
                        if k == 0:
                            dve.wait_ge(s_ha, g + 1)
                        elif k % 2 == 0:
                            dve.wait_ge(s_hc, 3 * g + 2 + k // 2)
                        dve.wait_ge(s_exp, g * KT + k + 1)
                        if k < KP:
                            dve.wait_ge(s_d, (g + 2) * KP + k + 1)
                        else:
                            dve.wait_ge(s_db, g * (KT - KP) + k - KP + 6)
                        dve.tensor_tensor_scan(h[:, par, k, :], dA[:, k, :], DB[k % 3][:, :],
                                               carry[:, bass.ds(n, 1), k], ALU.mult, ALU.add).then_inc(s_scan, 1)

                    dve.wait_ge(s_car, g + N - 1)
                    scan(0)
                    scan(1)
                    scan(2)
                    if not first:
                        keep_carry(g - 1, N - 1 if before else n - 1, 1 - par)
                    if par == 0:
                        dve.wait_ge(s_cb[slot], ((b * NCH + c) * (N // 4) + p4 + 1) * 16)
                    times_b(4)
                    dve.wait_ge(s_ns, g + 1)
                    dve.wait_ge(s_scan, g * KT + 2 + KT)
                    dve.tensor_tensor(hs[:, par, 0, :], h[:, par, 0, :], h[:, par, 1, :], ALU.add).then_inc(s_ha, 1)
                    times_b(5)
                    scan(3)
                    scan(4)
                    scan(5)

                def copy_y(m):
                    dve.wait_ge(s_ns, N * (m + 1) + 2)
                    dve.wait_ge(s_yst, 64 * m + 1)
                    dve.tensor_copy(ys[:, 0, :], Y[0][:, :]).then_inc(s_yev, 1)
                    dve.tensor_copy(ys[:, 1, ::-1], Y[1][:, :]).then_inc(s_yev, 1)
                    dve.tensor_copy(ys[0:64, 2, :], Y[2][0:64, :]).then_inc(s_yev, 1)
                    dve.tensor_copy(ys[64:128, 2, ::-1], Y[2][64:128, :]).then_inc(s_yev, 1)

                def chunk(c, q, first, last):
                    m = b * NCH + c
                    dve.wait_ge(s_du, KT * (m + 1) + 1)
                    scans(c, q, 0, 0, first, True)
                    if not first:
                        copy_y(m - 1)
                    if last:
                        for r in range(1, 4):
                            scans(c, q, 0, r)
                        with dve.Fori(1, 4) as p4:
                            for r in range(4):
                                scans(c, q, p4, r)
                        return
                    for n in range(1, 12):
                        scans(c, q, n // 4, n % 4)
                        if 0 <= n - S_SP < KT:
                            softplus(m + 1, 1 - q, n - S_SP)
                    with dve.Fori(3, 4) as p4:
                        for r in range(4):
                            scans(c, q, p4, r)

                for k in range(KT):
                    softplus(b * NCH, 0, k)
                chunk(0, 0, True, False)
                with dve.Fori(0, (NCH - 2) // 2) as cp:
                    chunk(cp * 2 + 1, 1, False, False)
                    chunk(cp * 2 + 2, 0, False, False)
                chunk(NCH - 1, 1, False, True)
                keep_carry((b + 1) * NCH * N - 1, N - 1, 1)
                copy_y(b * NCH + NCH - 1)
                barrier(dve, b * NBAR + 2)

                dve.wait_ge(s_xin, 32 * b + 32)
                alone(dve)
                both = ((0, 128), (1, 64))

                def turn_(i, q, front, middle, tail):
                    m = b * NCH + i
                    if front:
                        dve.wait_ge(s_pl[q], 48 * (m - q) + 96)
                        dve.wait_ge(s_pa, 2 * m + 1)
                        for j, n_ in both:
                            dve.scalar_tensor_tensor(o_g[0:n_, q, j, :], o_in[0:n_, q, 0, j, :], dsum[0:n_, j:j + 1],
                                                     o_in[0:n_, q, 1, j, :], ALU.mult, ALU.add).then_inc(s_p1, 1)
                        for j, n_ in both:
                            dve.wait_ge(s_p1, 2 * m + j + 1)
                            dve.tensor_tensor(o_g[0:n_, q, j, :], o_g[0:n_, q, j, :], o_in[0:n_, q, 2, j, :], ALU.add) \
                                .then_inc(s_pg, 1)
                    if tail:
                        c = i - 3
                        at = bass.ds(c * T, T)
                        dve.wait_ge(s_po, m)
                        dve.tensor_tensor(xr[:, at], bank[5 - q][0:C, :], xr[:, at], ALU.add).then_inc(s_px, 1)
                        dve.wait_ge(s_px, m)
                        dve.bn_stats(bnst[:, bass.ds(c * 6, 6)], xr[:, at])
                    if middle:
                        s = 1 - q
                        dve.wait_ge(s_pr, m + 1)
                        dve.wait_ge(s_pc, 2 * m + 3)
                        for j, n_ in both:
                            dve.tensor_tensor(o_g[0:n_, s, j, :], o_g[0:n_, s, j, :], o_rs[0:n_, s, :], ALU.mult) \
                                .then_inc(s_pt, 1)
                    if front:
                        dve.wait_ge(s_pm, m + 1)
                        dve.wait_ge(s_pg, 2 * m + 6)
                        for j, n_ in both:
                            dve.tensor_tensor(o_g[0:n_, q, j, :], o_g[0:n_, q, j, :], bank[q][0:n_, :], ALU.subtract) \
                                .then_inc(s_pc, 1)
                skewed(dve, turn_, 3)
                barrier(dve, b * NBAR + 3)

                group_norm(b * 2 + 1)
                dve.wait_ge(s_lw, 16 * (b + 1))
                dve.tensor_scalar(l_w, l_w, gn[:, 3:4], None, ALU.mult).then_inc(s_lws, 1)
                dve.wait_ge(s_lbp, b + 1)
                dve.tensor_tensor(b1s[:, :], b1t[:, :], WB[1][:, 0:8], ALU.subtract)
                dve.drain()
                dve.tensor_scalar(nb1[:, :], b1s[:, 0:2], -1.0, None, ALU.mult).then_inc(s_lb, 1)
                for ct in range(NPASS):
                    ps = b * NPASS + ct

                    def zero_state(d):
                        dve.wait_ge(s_lh, ps * PB + d * NR + 1)
                        if d == 1:
                            dve.wait_ge(s_ly[1], (ps + 1) * HB + 1)
                        else:
                            dve.wait_ge(s_lyv, (ps * (NDIR - 1) + max(d - 1, 0)) * HB + 1)
                        dve.memset(l_h[:, 1, R4 - 1:R4], 0.0).then_inc(s_l0, 1)
                        dve.wait_ge(s_l0, ps * NDIR + d + 1)
                        alone(dve)

                    def scan(d, r, turn_, q, a_, v_):
                        dve.wait_ge(s_lh, ps * PB + d * NR + r + 1)
                        if q == 0:
                            dve.wait_ge(s_ly[0], (ps * NDIR + d) * HB + turn_ + 1)
                        elif d == 0:
                            dve.wait_ge(s_ly[1], ps * HB + turn_ + 1)
                        else:
                            dve.wait_ge(s_lyv, (ps * (NDIR - 1) + d - 1) * HB + turn_ + 1)
                        dve.tensor_tensor_scan(l_h[:, q, :], a_, v_, l_h[:, 1 - q, R4 - 1:R4], ALU.mult, ALU.add) \
                            .then_inc(s_lh, 1)

                    dve.wait_ge(s_lcp, ps * 2 * NR + 1)
                    zero_state(0)
                    with dve.Fori(0, NR // 2) as r2:
                        for q in range(2):
                            r = r2 * 2 + q
                            i = ps * NR + r
                            at = bass.ds(r * R4, R4)
                            pb = bank[4 * q:4 * q + 4]
                            dve.wait_ge(s_ls, i + 1)
                            dve.wait_ge(s_lp, 4 * i + 2)
                            dve.scalar_tensor_tensor(l_t[:, q, :], pb[1][:, 0:R4], b1s[:, 4 + ct:5 + ct],
                                                     l_sg[:, q, :], ALU.add, ALU.mult).then_inc(s_lt, 1)
                            dve.wait_ge(s_lt, i + 3)
                            dve.wait_ge(s_lp, 4 * i + 3)
                            dve.scalar_tensor_tensor(l_v[:, at], pb[2][:, 0:R4], b1s[:, 2 + ct:3 + ct],
                                                     l_t[:, q, :], ALU.add, ALU.mult).then_inc(s_lv, 1)
                            dve.wait_ge(s_lv, i + 3)
                            scan(0, r, r2, q, l_a[:, at], l_v[:, at])
                    def output(d, r4, y):
                        dve.wait_ge(s_lst[y], 16 * (ps * (PB // 4) + d * (NR // 4) + r4) + 1)
                        dve.wait_ge(s_lh, ps * PB + d * NR + r4 * 4 + y + 2)
                        dve.tensor_tensor(*output_of(d, r4, y), ALU.mult).then_inc(s_lyv, 1)

                    zero_state(1)
                    for r in range(NR):
                        scan(1, r, r // 2, r % 2, backward(l_a, r), backward(l_v, r))
                        if r % 2:
                            output(1, r // 4, r % 4)
                    for d in (2, 3):
                        zero_state(d)
                        with dve.Fori(0, NR // 4) as r4:
                            for y in range(4):
                                r, q = r4 * 4 + y, y % 2
                                dve.wait_ge(s_lcp, ps * 2 * NR + (d - 2) * NR + r + 2)
                                a_, v_ = l_cp[:, q, 0, :], l_cp[:, q, 1, :]
                                scan(d, r, r4 * 2 + y // 2, q, *((a_[:, ::-1], v_[:, ::-1]) if d == 3 else (a_, v_)))
                                if q:
                                    output(d, r4, y)
                barrier(dve, b * NBAR + 4)
                def close(m, c):
                    dve.wait_ge(s_mo, m + 1)
                    dve.wait_ge(s_mst, 16 * m + 1)
                    dve.scalar_tensor_tensor(m_o, bank[4][0:C, :], obt[:, 0:1], xr[:, bass.ds(c * T, T)],
                                             ALU.add, ALU.add).then_inc(s_mx, 1)

                def products(m):
                    for j in range(2):
                        dve.wait_ge(s_mg, 2 * m + j + 3)
                        dve.wait_ge(s_mp, 8 + 4 * m + 2 * j + 2)
                        dve.scalar_tensor_tensor(m_p[:, j, :], bank[2 * j + 1][:, :], bmf[:, j:j + 1], m_g[:, j, :],
                                                 ALU.add, ALU.mult).then_inc(s_mr, 1)

                products(b * NCH)
                with dve.Fori(1, NCH) as c:
                    close(b * NCH + c - 1, c - 1)
                    products(b * NCH + c)
                close(b * NCH + NCH - 1, NCH - 1)
                barrier(dve, b * NBAR + 5)

        @block.tensor
        def _(pe):
            pe.sem_inc(s_ct, 1)
            for ahead in (s_po, s_pv):
                pe.sem_inc(ahead, 2)
            pe.sem_inc(s_d, 2 * KP)
            pe.sem_inc(s_ns, 2)
            pe.sem_inc(s_mp, 8)
            pe.wait_ge(s_w, 16 * NW)
            for d in range(4):
                for ct in range(2):
                    for j in range(2):
                        mm = pe.matmul(bank[2 * d + ct][:, :], s_yw[:, j, ct * 128:ct * 128 + 128], s_wt[:, 2 * d + j, :],
                                       start=(j == 0), stop=(j == 1))
                    mm.then_inc(s_ms, 1)
            pe.wait_ge(s_mc, 8)
            for i in range(4):
                for k in range(8):
                    mm = pe.matmul(bank[0][:, i:i + 1], s_wt[:, k, i * 128:i * 128 + 128], ybt[:, k % 2:k % 2 + 1],
                                   start=(k == 0), stop=(k == 7))
            mm.then_inc(s_ms, 1)
            barrier(pe, 0)

            def group_norm(i):
                pe.wait_ge(s_st, i + 1)
                pe.matmul(WB[0][0:C, 0:1], gmask, mv[:, 0:1], start=True, stop=True).then_inc(s_gp, 1)
                pe.wait_ge(s_gq, i + 1)
                pe.matmul(WB[0][0:C, 1:2], gmask, gn[:, 2:3], start=True, stop=True).then_inc(s_gp, 1)

            with pe.Fori(0, B) as b:
                group_norm(b * 2)
                pe.wait_ge(s_zw, b + 1)
                pe.matmul(WB[1][:, 0:1], wz[:, 0:128], gn[:, 4:5], start=True, stop=True)
                pe.matmul(WB[1][0:64, 1:2], wz[:, 128:D], gn[:, 4:5], start=True, stop=True).then_inc(s_bzp, 1)
                pe.wait_ge(s_wa, b + 1)
                pe.wait_ge(s_edge, 16 * (b + 1))
                pe.wait_ge(s_xp, b + 1)
                alone(pe)
                for i in range(2 * XB):
                    if i >= 4:
                        pe.wait_ge(s_xc, b * 2 * XB + i - 3)
                    row = i % XB * XR
                    if i < XB:
                        for half in range(2):
                            at = half * HH + row
                            mm = pe.matmul(bank[2 + i % 4][64 * half:64 * half + 64, 0:XR * PW], p_wi[:, 128:D],
                                           p_xp[:, at:at + XR, :].rearrange("p h w -> p (h w)"), start=True, stop=True)
                    else:
                        mm = pe.matmul(bank[2 + i % 4][:, 0:XR * PW], p_wi[:, 0:128],
                                       p_xp[:, HH + row:HH + row + XR, :].rearrange("p h w -> p (h w)"), start=True, stop=True)
                    mm.then_inc(s_xx, 1)
                with pe.Fori(0, NR // 4) as r2:
                    for q in range(2):
                        r = r2 * 2 + q
                        pe.wait_ge(s_us, b * (NR // 2) + r + 1)
                        for tap in range(9):
                            mm = pe.matmul(bank[q][:, 0:R4], p_wa[:, tap, :], conv_rhs(r, tap), start=(tap == 0), stop=(tap == 8))
                        mm.then_inc(s_cm, 1)
                barrier(pe, b * NBAR + 1)

                def stage_a(m, half=None):
                    o = WB[0][0:XC, :]
                    if half == 1:
                        pe.matmul(o, wx[:, 0, 2, :], uu[:, 2, ::-1], start=False, stop=False)
                        pe.matmul(o, wx[0:64, 0, 3, :], uu[0:64, 3, ::-1], start=False, stop=True).then_inc(s_xm, 1)
                        return
                    pe.wait_ge(s_u, 96 * (m + 1))
                    pe.wait_ge(s_ev, KP * m + 1)
                    pe.matmul(o, wx[:, 0, 0, :], uu[:, 0, :], start=True, stop=False)
                    pe.matmul(o, wx[0:64, 0, 1, :], uu[0:64, 1, :], start=False, stop=False)
                    if half is None:
                        stage_a(m, 1)

                def turn_b(m):
                    pe.wait_ge(s_xd, m + 1)
                    alone(pe)
                    for t in range(TB):
                        mm = pe.transpose(WB[1][:, t * N:(t + 1) * N], xd[B0:B0 + N, t * 128:(t + 1) * 128],
                                          cst[B0:B0 + N, K_ID + B0:K_ID + B0 + N])
                    mm.then_inc(s_btp, 1)

                def delta(m, k):
                    i = m * KT + k
                    if k == 1:
                        pe.wait_ge(s_bt, m + 1)
                    if k >= 2:
                        pe.wait_ge(s_m, i - 1)
                    pe.matmul(WB[k % 2][:, :], wdl[:, k * 128:(k + 1) * 128], xd[0:97, :], start=True, stop=True) \
                        .then_inc(s_dl, 1)

                def stage_c(m, ks):
                    pe.wait_ge(s_m, KT * (m + 1))
                    for k in ks:
                        pe.wait_ge(s_du, KT * m + k + 2)
                        if k >= 2:
                            pe.wait_ge(s_ev, m * KP + k)
                        for t in range(TB):
                            mm = pe.transpose(WB[k % 2][:, t * 128:(t + 1) * 128], du[:, k, t * 128:(t + 1) * 128], ident)
                        mm.then_inc(s_ct, 1)

                def turn(g, par):
                    pe.wait_ge(s_z, g + 1)
                    for k in range(KP):
                        pe.wait_ge(s_scan, g * KT + k + 4)
                        for t in range(TB):
                            mm = pe.transpose(DB[k % 3][:, t * 128:(t + 1) * 128], z[:, par, t, k * 128:(k + 1) * 128], ident)
                        mm.then_inc(s_d, 1)

                def state_sum(g, par, m_first=None):
                    first = m_first is not None
                    if first:
                        pe.wait_ge(s_yev, 4 * m_first + 1)
                    for k in range(4):
                        if k < 3:
                            pe.wait_ge(s_hc, 3 * g + k + 8)
                        to, w = (Y[k][:, :], ident) if k < 2 else (Y[2][64 * (k - 2):64 * (k - 1), :], sel)
                        mm = pe.matmul(to, w, hs[:, par, k, :], start=first, stop=True, skip_group_check=True)
                    mm.then_inc(s_ns, 1)

                def chunk(c, last):
                    m = b * NCH + c
                    g0 = m * N

                    def pair(j):
                        turn(g0 + j * 2, 0)
                        state_sum(g0 + j * 2 - 1, 1)
                        turn(g0 + j * 2 + 1, 1)
                        state_sum(g0 + j * 2, 0)

                    turn(g0 + 1, 1)
                    state_sum(g0, 0, m)
                    if last:
                        with pe.Fori(1, N // 2) as j:
                            pair(j)
                    for n in range(1, N - 1 if not last else 1):
                        turn(g0 + n + 1, (n + 1) % 2)
                        state_sum(g0 + n, n % 2)
                        if S_XA <= n <= S_XA + 1:
                            stage_a(m + 1, n - S_XA)
                        if n == S_DL - 1:
                            turn_b(m + 1)
                        if 0 <= n - S_DL < KT:
                            delta(m + 1, n - S_DL)
                        if n >= S_CT and 2 * (n - S_CT) < KP:
                            stage_c(m + 1, range(2 * (n - S_CT), 2 * (n - S_CT) + 2))
                    if not last:
                        turn(g0 + N, 0)
                    state_sum(g0 + N - 1, 1)

                stage_a(b * NCH)
                turn_b(b * NCH)
                for k in range(KT):
                    delta(b * NCH, k)
                stage_c(b * NCH, range(KP))
                turn(b * NCH * N, 0)
                with pe.Fori(0, NCH - 1) as c:
                    chunk(c, False)
                chunk(NCH - 1, True)
                barrier(pe, b * NBAR + 2)

                pe.wait_ge(s_xin, 32 * b + 32)
                alone(pe)
                with pe.Fori(0, NCH // 2) as c2:
                    for q in range(2):
                        c = c2 * 2 + q
                        at = bass.ds(c * T, T)
                        pe.wait_ge(s_psi, 2 * (b * NCH + c) + 1)
                        pe.matmul(bank[4 + 2 * q][:, :], wzs[:, 0:128], xr[:, at], start=True, stop=True)
                        pe.matmul(bank[5 + 2 * q][0:64, :], wzs[:, 128:D], xr[:, at], start=True, stop=True).then_inc(s_pz, 1)

                def both(to, w, v, last):
                    pe.matmul(to, w[0], v[:, 0, :], start=True, stop=False)
                    pe.matmul(to, w[1], v[0:64, 1, :], start=False, stop=True).then_inc(last, 1)

                def turn_(i, q, front, middle, tail):
                    m, ones = b * NCH + i, (mean192, mean192[0:64, :])
                    if front:
                        pe.wait_ge(s_pg, 2 * m + 6)
                        pe.wait_ge(s_pc, 2 * m + 1)
                        both(bank[q][:, :], ones, o_g[:, q, :, :], s_pm)
                    if tail:
                        pe.wait_ge(s_pp, 2 * m - 1)
                        pe.wait_ge(s_px, m - 1)
                        both(bank[4 + q][0:C, :], (wo[:, 0, :], wo[0:64, 1, :]), o_n[:, q, :, :], s_po)
                    if front:
                        pe.wait_ge(s_pq, 2 * m + 3)
                        pe.wait_ge(s_pe, m + 1)
                        both(bank[2 + q][:, :], ones, o_sq[:, q, :, :], s_pv)

                pe.wait_ge(s_psi, 2 * NCH * (b + 1) + 3)
                alone(pe)
                skewed(pe, turn_)
                barrier(pe, b * NBAR + 3)

                group_norm(b * 2 + 1)
                pe.wait_ge(s_lws, b + 1)
                for j in range(8):
                    mm = pe.matmul(WB[1][:, j:j + 1], l_w[:, j * 128:(j + 1) * 128], gn[:, 0:1], start=True, stop=True)
                mm.then_inc(s_lbp, 1)
                pe.wait_ge(s_lb, b + 1)
                alone(pe)
                for ct in range(NPASS):
                    with pe.Fori(0, NR // 2) as r2:
                        for q in range(2):
                            r = r2 * 2 + q
                            i = (b * NPASS + ct) * NR + r
                            pe.wait_ge(s_lc, i + 1)
                            pe.wait_ge(s_lv, i + 1)
                            for j in range(4):
                                w = 2 * (0, 2, 1, 3)[j] + ct
                                pe.matmul(bank[4 * q + j][:, 0:R4], l_w[:, w * 128:(w + 1) * 128],
                                          xr[:, bass.ds(r * R4, R4)], start=True, stop=True).then_inc(s_lp, 1)
                barrier(pe, b * NBAR + 4)

                def mix(m, turns, q, j):
                    pe.wait_ge(s_ml[q], 16 * turns)
                    pe.wait_ge(s_mr if j % 2 else s_mg, 2 * m + j // 2 + 1)
                    col = (LAT if j % 2 == 0 else 0) + (j // 2) * 128
                    for k in range(8):
                        mm = pe.matmul(bank[j][:, :], m_f[:, k, col:col + 128], m_y[:, q, k, :], start=(k == 0), stop=(k == 7))
                    mm.then_inc(s_mp, 1)

                def project(m):
                    pe.wait_ge(s_mr, 2 * m + 4)
                    pe.wait_ge(s_mx, m + 1)
                    for j in range(2):
                        mm = pe.matmul(bank[4][0:C, :], owt[:, j, :], m_p[:, j, :], start=(j == 0), stop=(j == 1))
                    mm.then_inc(s_mo, 1)

                def merge_chunk(m, turns, q, first):
                    mix(m, turns, q, 0)
                    if not first:
                        project(m - 1)
                    for j in range(1, 4):
                        mix(m, turns, q, j)

                pe.wait_ge(s_mfi, 16 * (b + 1))
                turns = b * (NCH // 2) + 1
                merge_chunk(b * NCH, turns, 0, True)
                with pe.Fori(0, (NCH - 2) // 2) as c2:
                    merge_chunk(b * NCH + c2 * 2 + 1, turns + c2, 1, False)
                    merge_chunk(b * NCH + c2 * 2 + 2, turns + c2 + 1, 0, False)
                merge_chunk(b * NCH + NCH - 1, turns + NCH // 2 - 1, 1, False)
                project(b * NCH + NCH - 1)
                barrier(pe, b * NBAR + 5)


def kernel(**inputs):
    import numpy as np
    import concourse.bacc as bacc
    from concourse import mybir as _mybir
    from concourse.bass_utils import run_bass_kernel_spmd

    v = {k: np.asarray(a) for k, a in inputs.items()}
    f = np.float32

    def tiles(a, n):
        out = np.zeros((n * 128,), f)
        out[:a.shape[0]] = a
        return out.reshape(n, 128).T

    order = [g * D + c for g in range(4) for c in range(128)]
    order += [g * D + 128 + c for g in range(4) for c in range(64)]
    order = np.array(order)
    wx = v["L0_conv_W_x"]
    wxp = np.zeros((4 * D, XC), f)
    wxp[:, 0:DTR] = wx[:, 0:DTR]
    wxp[:, B0:B0 + N] = wx[:, DTR:DTR + N]
    wxp[:, C0:C0 + N] = wx[:, DTR + N:]
    const = np.zeros((128, K_END), f)
    p = np.arange(128)
    const[p, K_ID + p] = 1
    const[p, K_SEL + p % 64] = 1
    c = np.arange(C)
    const[:C, K_GM:K_GM + C] = (c[:, None] // 3 == c[None, :] // 3) / f(3)
    const[:, K_MEAN:K_MEAN + 128] = 1 / D
    const[:, K_EPS] = EPS
    inner = np.zeros((PW, PW), f)
    inner[1:-1, 1:-1] = 1
    wdel = np.zeros((97, KT * 128), f)
    wdel[0:DTR] = v["L0_conv_W_delta"][:, order]
    wdel[96] = v["L0_conv_b_delta"][order]
    bdw = tiles(v["L0_conv_b_dw"], 2)
    bdw[64:, 1] = bdw[:64, 1]
    bz = v["L0_conv_b_in"][D:]
    wdw = v["L0_conv_w_dw"].reshape(D, 9)
    arrays = {
        "x": v["x"].reshape(B, C, L),
        "win": np.concatenate([v["L0_conv_W_in"], v["L0_conv_b_in"][None]], 0),
        "wdw": wdw.T,
        "wdv": np.stack([np.concatenate([wdw[128:]] * 2, 0), wdw[:128]], 1),
        "v192": np.concatenate([tiles(a, 2) for a in (bz, v["L0_conv_ln_g"], v["L0_conv_ln_b"])] + [bdw], 1),
        "wxp": wxp,
        "alog": v["L0_conv_A_log"][order].reshape(KT, 128, N).transpose(1, 2, 0).reshape(128, N * KT),
        "dp": np.stack([tiles(v["L0_conv_Dp"][g * D:(g + 1) * D], 2) for g in range(4)], 2),
        "wdel": wdel,
        "wout": v["L0_conv_W_out"],
        "w1": np.concatenate([v["L1_conv_dw"], v["L1_conv_xw"], v["L1_conv_bcw"]], 0).T,
        "b1": tiles(np.concatenate([v["L1_conv_db"], v["L1_conv_xb"], v["L1_conv_bcb"]]), 8),
        "yw": v["L1_conv_yw"],
        "yb": tiles(v["L1_conv_yb"], 2),
        "wt": np.concatenate([v["L1_conv_mw"], v["L1_conv_gw"]], 0).T,
        "bm": tiles(np.concatenate([v["L1_conv_mb"], v["L1_conv_gb"]]), 4),
        "ow": v["L1_conv_ow"].T,
        "ob": v["L1_conv_ob"].reshape(C, 1),
        "const": const,
        "inner": inner.reshape(1, PW * PW),
    }
    nc = bacc.Bacc("TRN2", target_bir_lowering=False, num_devices=1)
    feeds, args = {}, []
    for name, a in arrays.items():
        a = np.ascontiguousarray(a)
        feeds[f"in_{name}"] = a
        args.append(nc.dram_tensor(f"in_{name}", a.shape, _mybir.dt.from_np(a.dtype), kind="ExternalInput").ap())
    y = nc.dram_tensor("out_0", (B, C, L), F32, kind="ExternalOutput").ap()
    vmamba_then_s6(nc, *args, y)
    r = run_bass_kernel_spmd(nc, [feeds], core_ids=[0])
    return r.results[0]["out_0"].reshape(B, C, H, W)
```
